# Optimizing a Trainium2 kernel written in Bass

```python
import numpy as np
import jax
import jax.numpy as jnp

def _softmax(x, axis=-1):
    return jax.nn.softmax(x, axis=axis)

def _gelu(x):
    return jax.nn.gelu(x, approximate=True)

def _silu(x):
    return jax.nn.silu(x)

def _sigmoid(x):
    return jax.nn.sigmoid(x)

def _layernorm(x, axis=-1, eps=1e-05):
    m = jnp.mean(x, axis=axis, keepdims=True)
    v = jnp.var(x, axis=axis, keepdims=True)
    return (x - m) / jnp.sqrt(v + eps)

def _scatter_add(tgt, idx, src, axis=0):
    return tgt.at[idx].add(src)

def _segment_sum(src, seg, n):
    return jax.ops.segment_sum(src, seg, n)
kernel_name = 'mk_gnn_ffn_d1_gnn_r8_648e0a'

def setup_inputs(seed: int=0):
    np.random.seed(seed)
    _w = jnp.asarray

    def _rec_inputs():
        import jax
        import jax.numpy as jnp
        _gk = jax.random.key(seed)
        x = -0.0003713 + 1 * jax.random.normal(jax.random.fold_in(_gk, 1), (6250, 256), jnp.float32)
        _s = jax.random.randint(jax.random.fold_in(_gk, 2), (50000,), 0, 6250, jnp.int32)
        _d = jax.random.randint(jax.random.fold_in(_gk, 3), (50000,), 0, 6250, jnp.int32)
        _loop = jnp.arange(6250, dtype=jnp.int32)
        src = jnp.concatenate([_s, _d, _loop])
        dst = jnp.concatenate([_d, _s, _loop])
        _o = jnp.argsort(dst, stable=True)
        src = src[_o]
        dst = dst[_o]
        return (x, src, dst)
    x, src, dst = _rec_inputs()

    def _L0_gnn_setup():
        import jax, jax.numpy as jnp
        import numpy as np
        N = 6250
        E = 100000
        D = 256
        SMALL = 25
        key = jax.random.key(seed)
        k1, k2, k3, k4, k5 = jax.random.split(key, 5)
        x = jax.random.normal(k1, (N, D), jnp.float32)
        src = jax.random.randint(k2, (E,), 0, N)
        dst = jax.random.randint(k3, (E,), 0, N)
        Wq = jax.random.normal(k4, (D, SMALL), jnp.float32) / np.float32(np.sqrt(D))
        bq = jnp.zeros((SMALL,), jnp.float32)
        Wk = jax.random.normal(k5, (D, SMALL), jnp.float32) / np.float32(np.sqrt(D))
        bk = jnp.zeros((SMALL,), jnp.float32)
        return {'x': x, 'src': src, 'dst': dst, 'Wq': Wq, 'bq': bq, 'Wk': Wk, 'bk': bk}
    _L0_gnn_all = _L0_gnn_setup()
    _L0_gnn_in = {k: v for k, v in _L0_gnn_all.items() if k in ('Wq', 'bq', 'Wk', 'bk')}
    del _L0_gnn_all

    def _L0_ffn_setup():
        import jax, jax.numpy as jnp
        import numpy as np
        E = 8
        K = 2
        D = 256
        H = 512
        DOUT = 256
        EPS = 1e-05
        key = jax.random.key(seed)
        ks = jax.random.split(key, 9)
        s = 0.02
        return {'x': jax.random.normal(ks[0], (4, 1024, D), jnp.float32), 'gamma': 1.0 + 0.05 * jax.random.normal(ks[1], (D,), jnp.float32), 'beta': 0.05 * jax.random.normal(ks[2], (D,), jnp.float32), 'Wr': 0.01 * jax.random.normal(ks[3], (D, E), jnp.float32), 'br': jnp.zeros((E,), jnp.float32), 'W1': s * jax.random.normal(ks[4], (E, D, H), jnp.float32), 'b1': s * jax.random.normal(ks[5], (E, H), jnp.float32), 'W2': s * jax.random.normal(ks[6], (E, H, DOUT), jnp.float32), 'b2': s * jax.random.normal(ks[7], (E, DOUT), jnp.float32)}
    _L0_ffn_all = _L0_ffn_setup()
    _L0_ffn_in = {k: v for k, v in _L0_ffn_all.items() if k in ('gamma', 'beta', 'Wr', 'br', 'W1', 'b1', 'W2', 'b2')}
    del _L0_ffn_all
    return {'x': x, 'src': src, 'dst': dst, 'L0_gnn_Wq': _L0_gnn_in['Wq'], 'L0_gnn_bq': _L0_gnn_in['bq'], 'L0_gnn_Wk': _L0_gnn_in['Wk'], 'L0_gnn_bk': _L0_gnn_in['bk'], 'L0_ffn_gamma': _L0_ffn_in['gamma'], 'L0_ffn_beta': _L0_ffn_in['beta'], 'L0_ffn_Wr': _L0_ffn_in['Wr'], 'L0_ffn_br': _L0_ffn_in['br'], 'L0_ffn_W1': _L0_ffn_in['W1'], 'L0_ffn_b1': _L0_ffn_in['b1'], 'L0_ffn_W2': _L0_ffn_in['W2'], 'L0_ffn_b2': _L0_ffn_in['b2']}

def reference(x, src, dst, L0_gnn_Wq, L0_gnn_bq, L0_gnn_Wk, L0_gnn_bk, L0_ffn_gamma, L0_ffn_beta, L0_ffn_Wr, L0_ffn_br, L0_ffn_W1, L0_ffn_b1, L0_ffn_W2, L0_ffn_b2):
    import jax
    import jax.numpy as jnp

    def _L0_gnn_ref(x, src, dst, Wq, bq, Wk, bk):
        import jax, jax.numpy as jnp
        import numpy as np
        N = 6250
        E = 100000
        D = 256
        SMALL = 25
        d_k = np.float32(np.sqrt(SMALL))
        q = jnp.tanh(x @ Wq + bq)
        k = x @ Wk + bk
        loop = jnp.arange(N, dtype=src.dtype)
        s = jnp.concatenate([src, loop])
        d = jnp.concatenate([dst, loop])
        w = jnp.sum(q[s] * k[d], axis=1) / d_k
        wmax = jax.ops.segment_max(w, d, num_segments=N)
        ew = jnp.exp(w - wmax[d])
        denom = jax.ops.segment_sum(ew, d, num_segments=N)
        alpha = ew / denom[d]
        out = jax.ops.segment_sum(alpha[:, None] * x[s], d, num_segments=N)
        return out

    def _L0_ffn_ref(x, gamma, beta, Wr, br, W1, b1, W2, b2):
        import jax, jax.numpy as jnp
        import numpy as np
        E = 8
        K = 2
        D = 256
        H = 512
        DOUT = 256
        EPS = 1e-05
        mu = jnp.mean(x, axis=-1, keepdims=True)
        var = jnp.mean(jnp.square(x - mu), axis=-1, keepdims=True)
        xn = (x - mu) * jax.lax.rsqrt(var + EPS) * gamma + beta
        logits = jnp.einsum('bsd,de->bse', xn, Wr) + br
        top_vals, top_idx = jax.lax.top_k(logits, K)
        w = jax.nn.softmax(top_vals, axis=-1)
        w_full = jnp.einsum('bsk,bske->bse', w, jax.nn.one_hot(top_idx, E, dtype=w.dtype))
        y = jnp.zeros(x.shape[:-1] + (DOUT,), x.dtype)
        for e in range(E):
            h = jax.nn.gelu(jnp.einsum('bsd,dh->bsh', xn, W1[e]) + b1[e], approximate=False)
            y_e = jnp.einsum('bsh,hd->bsd', h, W2[e]) + b2[e]
            y = y + y_e * w_full[..., e, None]
        return y
    x = x + _L0_gnn_ref(_layernorm(x, axis=-1), src, dst, L0_gnn_Wq, L0_gnn_bq, L0_gnn_Wk, L0_gnn_bk)
    x = x + _L0_ffn_ref(_layernorm(x, axis=-1)[None], L0_ffn_gamma, L0_ffn_beta, L0_ffn_Wr, L0_ffn_br, L0_ffn_W1, L0_ffn_b1, L0_ffn_W2, L0_ffn_b2)[0]
    return x

_drawn_inputs = setup_inputs


def setup_inputs(seed=0):
    import zlib

    import numpy as np

    out = dict(_drawn_inputs(seed))
    spreads = {'L0_gnn_bq': (0.0, 0.8), 'L0_gnn_bk': (0.0, 0.434), 'L0_ffn_br': (0.0, 0.1)}
    factors = {'L0_ffn_gamma': 6.732, 'L0_ffn_beta': 5.529, 'L0_ffn_b1': 8.0, 'L0_ffn_b2': 4.844}
    for name, (base, spread) in spreads.items():
        noise = np.random.default_rng([zlib.crc32(name.encode()), seed]).standard_normal(out[name].shape)
        drawn = base * np.exp(spread * noise) if base else spread * noise
        out[name] = jnp.asarray(drawn.astype(out[name].dtype))
    for name, factor in factors.items():
        out[name] = (out[name] * factor).astype(out[name].dtype)
    return out
```

```python
import numpy as np
import concourse.bass as bass
from concourse import mybir
from contextlib import ExitStack

F32 = mybir.dt.float32
BF16 = mybir.dt.bfloat16
I32 = mybir.dt.int32
I16 = mybir.dt.int16
U32 = mybir.dt.uint32
ALU = mybir.AluOpType
ACT = mybir.ActivationFunctionType
X_AXIS = mybir.AxisListType.X

P = 128
N = 6250
D = 256
S = 25
E_IN = 106250
NE = 8
H = 512
EPS = 1e-5

NT = -(-N // P)
LAST = N - (NT - 1) * P
CH = 7
NCH = NT // CH
CHROWS = CH * P
NULL_T = NT
NTX = NT + 1
PAD_DST = NT * P - 1

G = 4
GE = G * P
NG = -(-E_IN // GE)
GP = NG // 2
FULLP = E_IN // (2 * GE)
RESTE = E_IN - FULLP * 2 * GE
ROW = D + 1 + S
W1COLS = D + 1
XSLOTS = 4
ISLOTS = 8
AHEAD = 4

ICOLS = 80
ITEMS = P * ICOLS
TBITS = 64
BIG = 1e30
DK = 5.0

CAP = 6528
ST = 256
MROW = D + 4
XE_ROWS = NE * CAP
OUT_ROWS = N + ST


def build(nc, x, src, dst, Wq, bq, Wk, bk, gamma, beta, Wr, br, W1, b1, W2, b2, out):
    ctx = ExitStack()
    with ctx:
        def sb(name, shape, dt=F32):
            return ctx.enter_context(nc.sbuf_tensor(name, shape, dt))

        def sem(name):
            return ctx.enter_context(nc.semaphore(name))

        ctx.enter_context(nc.allow_non_contiguous_dma(reason="small columns of weights"))

        rows_dram = nc.dram_tensor("rows_dram", (NT * P, ROW), F32, kind="Internal").ap()
        grp_dram = nc.dram_tensor("grp_dram", (2, NG), F32, kind="Internal").ap()
        item_dram = nc.dram_tensor("item_dram", (ITEMS,), I16, kind="Internal").ap()
        xe_dram = nc.dram_tensor("xe_dram", (XE_ROWS, MROW), F32, kind="Internal").ap()

        acc = sb("acc", [P, NTX, W1COLS])
        m_all = sb("m_all", [P, NTX])
        item_row = sb("item_row", [1, ITEMS], I16)
        srccol = sb("srccol", [P, NG, G], I32)
        dstcol = sb("dstcol", [P, NG, G])
        ident = sb("ident", [P, P])
        pen = sb("pen", [P, P], BF16)
        tri = sb("tri", [P, P])
        ones = sb("ones", [P, P])
        iota8 = sb("iota8", [P, NE])
        ecap = sb("ecap", [P, NE])
        tok = sb("tok", [P, NT])
        itemidx = sb("itemidx", [P, ICOLS])
        vmask = sb("vmask", [P, 1])
        tail = sb("tail", [P, 2, MROW])
        wqk = sb("wqk", [P, 2, 2 * S])
        bqk = sb("bqk", [P, 2 * S])
        bkcol = sb("bkcol", [S, 1])
        wr = sb("wr", [P, 2, NE])
        brb = sb("brb", [P, NE])
        gcol = sb("gcol", [P, 2])
        bcol = sb("bcol", [P, 2])
        epsc = sb("epsc", [P, 1])

        arena_b = sb("arena_b", [P, 2 * NTX * P])
        kT = arena_b[:, 0:NTX * P]
        iota_n = arena_b[:, NTX * P:2 * NTX * P]
        w1s = arena_b[:, 0:2048].rearrange("p (e c h) -> p e c h", e=2, c=2)
        w2s = arena_b[:, 2048:4096].rearrange("p (e c d) -> p e c d", e=2, c=4)
        b2b = arena_b[:, 4096:6144].rearrange("p (e d) -> p e d", e=NE)
        b1c = arena_b[:, 6144:6144 + 4 * NE]
        xrows = arena_b[:, 6400:6400 + 2 * MROW].rearrange("p (k r) -> p k r", k=2)
        xT = arena_b[:, 7000:7512].rearrange("p (c n) -> p c n", c=2)
        hT = arena_b[:, 7600:8624].rearrange("p (m n) -> p m n", m=4)
        ybuf = arena_b[:, 8700:9212].rearrange("p (k d) -> p k d", k=2)
        ysum = arena_b[:, 9300:9812].rearrange("p (k d) -> p k d", k=2)

        arena_a = sb("arena_a", [P, 12750])
        xlr = arena_a[:, 0:2 * CH * W1COLS].rearrange("p (b u d) -> p b u d", b=2, u=CH)
        prod = arena_a[:, 3600:3600 + NT * S].rearrange("p (t s) -> p t s", t=NT)
        qk_all = arena_a[:, 4900:4900 + NT * 2 * S].rearrange("p (t s) -> p t s", t=NT)
        q_all = arena_a[:, 7400:7400 + NT * S].rearrange("p (t s) -> p t s", t=NT)
        rawf = arena_a[:, 8650:8650 + 2048].rearrange("p (k n) -> p k n", k=2)
        raw_i = arena_a[:, 10700:10700 + 2048].bitcast(I32).rearrange("p (k n) -> p k n", k=2)
        xg = arena_a[:, 0:XSLOTS * G * ROW].rearrange("p (n r) -> p n r", r=ROW)
        xr = arena_a[:, 0:2 * CH * D].rearrange("p (b u d) -> p b u d", b=2, u=CH)
        rows = arena_a[:, 3600:3600 + 2 * CH * MROW].rearrange("p (b u r) -> p b u r", b=2, u=CH)
        xnT = arena_a[:, 7300:7300 + 2 * D].rearrange("p (b c n) -> p b c n", b=2, c=2)

        xlT = sb("xlT", [P, 2, 2, P])
        st = sb("st", [P, CH, 6])
        mv = sb("mv", [P, 2, CH, 2])
        lnv = sb("lnv", [P, CH])
        rstd = sb("rstd", [P, 2, CH])
        gmax = sb("gmax", [P, 2])
        gmin = sb("gmin", [P, 2])
        ghl = sb("ghl", [P, 2, 2], I32)
        ghf = sb("ghf", [P, 2, 2])
        cntb = sb("cntb", [P, 2, NG])
        incl = sb("incl", [P, NG])
        basef = sb("basef", [P, NG])
        delta = sb("delta", [P, NG])
        stepw = sb("stepw", [P, NG])
        gsel = sb("gsel", [P, NG])
        icode = sb("icode", [P, ICOLS])
        ivalid = sb("ivalid", [P, ICOLS])
        ilist = sb("ilist", [P, ICOLS], I16)
        incl_i = sb("incl_i", [1, NG + 1], I32)
        idx = sb("idx", [P, ISLOTS, G], I32)
        kts = sb("kts", [S, P])
        qs = sb("qs", [P, G, S])
        qT = sb("qT", [S, GE])
        mask = sb("mask", [P, G, P], BF16)
        prob = sb("prob", [P, GE])
        probT = sb("probT", [P, GE])
        mx = sb("mx", [P, 1])
        mnew = sb("mnew", [P, 1])
        nbias = sb("nbias", [P, 1])
        mdiff = sb("mdiff", [P, 1])
        alpha = sb("alpha", [P, 1])
        rl = sb("rl", [P, CH])
        lg = sb("lg", [P, CH, NE])
        top = sb("top", [P, CH, NE])
        topi = sb("topi", [P, CH, NE], U32)
        idxf = sb("idxf", [P, CH, 2])
        oh = sb("oh", [P, 2, CH, NE])
        asg = sb("asg", [P, CH, NE])
        tdiff = sb("tdiff", [P, CH])
        ex = sb("ex", [P, CH])
        den2 = sb("den2", [P, CH])
        w0 = sb("w0", [P, CH])
        ebase = sb("ebase", [P, CH + 1, NE])
        slotv = sb("slotv", [P, CH, NE])
        slotp = sb("slotp", [P, 2, CH, NE])
        slotf = sb("slotf", [P, 2, CH])
        slots = sb("slots", [P, 2, 2, CH], I32)
        cnt_i = sb("cnt_i", [1, NE], I32)
        nst_i = sb("nst_i", [1, NE], I32)
        nst_f = sb("nst_f", [1, NE])
        zero8 = sb("zero8", [1, NE])
        eend_f = sb("eend_f", [1, NE])
        eend = sb("eend", [1, NE + 1], I32)
        metaA = sb("metaA", [P, 2, 4])
        wsel = sb("wsel", [P, 2])
        weq = sb("weq", [P, 2])
        wtok = sb("wtok", [P, 2])
        tokB = sb("tokB", [P, 2], I32)
        probe = sb("probe", [1, 8])

        pb = [ctx.enter_context(nc.psum_tensor(f"pb{i}", [P, 512], F32)) for i in range(8)]

        s_cst = sem("s_cst"); s_zero = sem("s_zero"); s_wl = sem("s_wl"); s_x = sem("s_x"); s_edge = sem("s_edge")
        s_id = sem("s_id"); s_rawf = sem("s_rawf"); s_et = sem("s_et"); s_ec = sem("s_ec"); s_eng0 = sem("s_eng0")
        s_v0 = sem("s_v0"); s_grp = sem("s_grp"); s_grpb = sem("s_grpb"); s_iw = sem("s_iw"); s_ir = sem("s_ir")
        s_st = sem("s_st"); s_mv = sem("s_mv"); s_ln = sem("s_ln"); s_rs = sem("s_rs"); s_xl = sem("s_xl")
        s_accw = sem("s_accw"); s_tp = sem("s_tp"); s_ev = sem("s_ev"); s_qk = sem("s_qk"); s_kt = sem("s_kt")
        s_qks = sem("s_qks"); s_q = sem("s_q"); s_m0 = sem("s_m0"); s_rw = sem("s_rw"); s_code = sem("s_code")
        s_idx = [sem(f"s_idx{i}") for i in range(ISLOTS)]
        s_g = [sem(f"s_g{i}") for i in range(XSLOTS)]
        xg_free = sem("xg_free"); xg_ready = sem("xg_ready")
        s_qs = sem("s_qs"); s_qt = sem("s_qt"); s_qTs = sem("s_qTs"); s_kts = sem("s_kts"); s_mask = sem("s_mask")
        s_sc = sem("s_sc"); s_mx = sem("s_mx"); s_mn = sem("s_mn"); s_nb = sem("s_nb"); s_md = sem("s_md")
        s_ms = sem("s_ms"); s_p = sem("s_p"); s_al = sem("s_al"); s_pt = sem("s_pt"); s_pts = sem("s_pts")
        s_pv = sem("s_pv"); s_acc = sem("s_acc")
        tk_v = sem("tk_v"); tk_a = sem("tk_a"); tk_p = sem("tk_p"); tk_g = sem("tk_g"); tk_s = sem("tk_s")
        a_x = [sem(f"a_x{i}") for i in range(2)]
        a_o = [sem(f"a_o{i}") for i in range(2)]
        a_v = sem("a_v"); a_x2 = sem("a_x2"); a_mv = sem("a_mv"); a_ln = sem("a_ln"); a_rs = sem("a_rs")
        a_xn = sem("a_xn"); a_tp = sem("a_tp"); a_ev = sem("a_ev"); a_lg = sem("a_lg"); a_df = sem("a_df")
        a_ex = sem("a_ex"); a_as = sem("a_as"); a_pos = sem("a_pos"); a_slot = sem("a_slot"); a_sc = sem("a_sc")
        a_free = sem("a_free"); a_cnt = sem("a_cnt"); a_tail = sem("a_tail")
        b_w = [sem(f"b_w{i}") for i in range(2)]
        b_c = sem("b_c"); b_v = sem("b_v"); b_rl = sem("b_rl"); b_xt = sem("b_xt"); b_xe = sem("b_xe")
        b_h = sem("b_h"); b_g = sem("b_g"); b_y = sem("b_y"); b_meta = sem("b_meta"); b_lat = sem("b_lat")
        b_ys = sem("b_ys"); b_yb = sem("b_yb"); b_sc = sem("b_sc"); b_t = sem("b_t")

        block = ctx.enter_context(nc.Block())

        def col(ap, i, n=1):
            return ap[:, bass.ds(i, n)]

        def load_code(eng, i):
            code = eng.value_load(item_row[0:1, bass.ds(i, 1)], min_val=0, max_val=NULL_T + TBITS * (NG - 1))
            return (eng.snap(code & (TBITS - 1)).with_bounds(min_val=0, max_val=NULL_T),
                    eng.snap(code >> 6).with_bounds(min_val=0, max_val=NG - 1))

        def item_count(eng):
            return eng.value_load(incl_i[0:1, NG - 1:NG], min_val=NG, max_val=NG * NT)

        def last_item(eng):
            return eng.value_load(incl_i[0:1, NG:NG + 1], min_val=NG - 1, max_val=NG * NT)

        def expert_ends(eng, e):
            lo = eng.value_load(eend[0:1, bass.ds(e, 1)], min_val=0, max_val=NE * 25)
            hi = eng.value_load(eend[0:1, bass.ds(e + 1, 1)], min_val=1, max_val=NE * 25)
            return lo, hi

        def x_tiles(ap, lo, n):
            return ap[bass.ds(lo, n * P), :].rearrange("(t p) d -> p t d", p=P)

        @block.sync
        def _(sp):
            for o, i in ((wqk[:, :, 0:S], Wq.rearrange("(c p) s -> p c s", p=P)),
                         (wqk[:, :, S:2 * S], Wk.rearrange("(c p) s -> p c s", p=P)),
                         (bqk[:, 0:S], bq.partition_broadcast(P)),
                         (bqk[:, S:2 * S], bk.partition_broadcast(P)),
                         (bkcol[:, :], bk.rearrange("(s o) -> s o", o=1)),
                         (wr[:, :, :], Wr.rearrange("(c p) e -> p c e", p=P)),
                         (brb[:, :], br.partition_broadcast(P)),
                         (gcol[:, :], gamma.rearrange("(c p) -> p c", p=P)),
                         (bcol[:, :], beta.rearrange("(c p) -> p c", p=P))):
                sp.dma_start(o, i).then_inc(s_wl, 16)
            sp.wait_ge(s_zero, 3)
            for k, e in enumerate((src, dst)):
                sp.dma_start(raw_i[0:FULLP, k, :],
                             e[0:FULLP * 2 * GE].rearrange("(p n) -> p n", p=FULLP)).then_inc(s_edge, 16)
                sp.dma_start(raw_i[FULLP:FULLP + 1, k, 0:RESTE],
                             e[FULLP * 2 * GE:E_IN].rearrange("(p n) -> p n", p=1)).then_inc(s_edge, 16)
            for c in range(NCH - 1):
                sp.dma_start(acc[:, c * CH:(c + 1) * CH, 0:D], x_tiles(x, c * CHROWS, CH)).then_inc(s_x, 16)
            sp.dma_start(acc[:, NT - CH:NT - 1, 0:D], x_tiles(x, (NT - CH) * P, CH - 1)).then_inc(s_x, 16)
            sp.dma_start(acc[0:LAST, NT - 1, 0:D], x[(NT - 1) * P:N, :]).then_inc(s_x, 16)
            sp.wait_ge(s_grp, 1)
            for k in range(2):
                sp.dma_start(grp_dram[k, :].rearrange("(p h) -> p h", h=2), ghf[0:GP, k, :]).then_inc(s_grpb, 16)
            sp.wait_ge(s_grpb, 32)
            for k in range(2):
                sp.dma_start(cntb[:, k, :], grp_dram[k, :].partition_broadcast(P)).then_inc(s_grpb, 16)
            sp.wait_ge(s_code, 1)
            sp.dma_start(item_dram.rearrange("(p c) -> p c", p=P), ilist[:, :]).then_inc(s_iw, 16)
            sp.wait_ge(s_iw, 16)
            sp.dma_start(item_row[:, :], item_dram.rearrange("(o n) -> o n", o=1)).then_inc(s_ir, 16)
            with sp.Fori(0, NCH - 1) as c:
                sp.wait_ge(s_accw, c + 3)
                sp.dma_start(rows_dram[bass.ds(c * CHROWS, CHROWS), 0:W1COLS].rearrange("(t p) d -> p t d", p=P),
                             acc[:, bass.ds(c * CH, CH), :]).then_inc(s_rw, 16)
            sp.wait_ge(s_accw, 2 + NCH)
            sp.dma_start(rows_dram[(NT - CH) * P:NT * P, 0:W1COLS].rearrange("(t p) d -> p t d", p=P),
                         acc[:, NT - CH:NT, :]).then_inc(s_rw, 16)
            sp.wait_ge(s_q, 1)
            sp.dma_start(rows_dram[:, W1COLS:ROW].rearrange("(t p) s -> p t s", p=P), q_all[:, :, :]).then_inc(s_rw, 16)

            sp.wait_ge(s_ec, 4)
            for v in range(AHEAD):
                sp.dma_start(idx[:, v, :], srccol[:, v, :]).then_inc(s_idx[v], 16)

            def give_back(g, v):
                done = sp.value_load(incl_i[0:1, bass.ds(g, 1)], min_val=1, max_val=NG * NT)
                sp.wait_ge(s_pv, done)
                sp.sem_inc(xg_free, 1)
                sp.dma_start(idx[:, (v + AHEAD) % ISLOTS, :], srccol[:, bass.ds(g + AHEAD, 1), :].rearrange("p o g -> p (o g)"))\
                    .then_inc(s_idx[(v + AHEAD) % ISLOTS], 16)

            sp.wait_ge(s_m0, 1)
            with sp.Fori(0, NG // ISLOTS - 1) as k:
                for v in range(ISLOTS):
                    give_back(k * ISLOTS + v, v)
            for v in range(ISLOTS - AHEAD):
                give_back(NG - ISLOTS + v, v)

            n_items = item_count(sp)
            sp.wait_ge(s_acc, n_items + 1)
            sp.sem_inc(tk_s, 1)
            sp.wait_ge(s_qs, n_items + 2)
            sp.sem_inc(tk_s, 1)

            def load_x(c, b, last=False):
                if not last:
                    sp.dma_start(xr[:, b, :, :], x_tiles(x, c * CHROWS, CH)).then_inc(a_x[b], 16)
                else:
                    sp.dma_start(xr[:, b, 0:CH - 1, :], x_tiles(x, c * CHROWS, CH - 1)).then_inc(a_x[b], 16)
                    sp.dma_start(xr[0:LAST, b, CH - 1, :], x[(NT - 1) * P:N, :]).then_inc(a_x[b], 16)

            def store_x2(c, b, k, last=False):
                sp.wait_ge(a_x2, CH * (c + 1))
                if not last:
                    sp.dma_start(x_tiles(out, c * CHROWS, CH), xr[:, b, :, :]).then_inc(a_o[b], 16)
                else:
                    sp.dma_start(x_tiles(out, c * CHROWS, CH - 1), xr[:, b, 0:CH - 1, :]).then_inc(a_o[b], 16)
                    sp.dma_start(out[(NT - 1) * P:N, :], xr[0:LAST, b, CH - 1, :]).then_inc(a_o[b], 16)

            for k in range(2):
                sp.dma_start(out[N + k * P:N + (k + 1) * P, :], tail[:, k, 0:D]).then_inc(a_tail, 16)
            sp.dma_start(b2b[:, :, :].rearrange("p e d -> p (e d)"),
                         b2.rearrange("e d -> (e d)").partition_broadcast(P)).then_inc(a_tail, 16)
            for e in range(NE):
                sp.dma_start(b1c[:, 4 * e:4 * e + 4], b1[e, :].rearrange("(m p) -> p m", p=P)).then_inc(a_tail, 16)
            load_x(0, 0)
            load_x(1, 1)
            with sp.Fori(0, 2) as k:
                for b in range(2):
                    store_x2(2 * k + b, b, k)
                    sp.wait_ge(a_o[b], 16 * (k + 1))
                    sp.wait_ge(a_xn, 2 * CH * (2 * k + b) + CH)
                    sp.sem_inc(tk_s, 1)
                    load_x(2 * k + b + 2, b)
            store_x2(4, 0, 2)
            sp.wait_ge(a_o[0], 16 * 3)
            sp.wait_ge(a_xn, 2 * CH * 4 + CH)
            load_x(6, 0, last=True)
            store_x2(5, 1, 2)
            store_x2(6, 0, 3, last=True)

            sp.wait_ge(a_cnt, 1)
            with sp.Fori(0, NE) as e:
                cnt = sp.value_load(cnt_i[0:1, bass.ds(e, 1)], min_val=0, max_val=N)
                for k in range(2):
                    sp.dma_start(xe_dram[bass.ds(e * CAP + cnt + k * P, P), :], tail[:, k, :]).then_inc(a_tail, 16)
            sp.wait_ge(a_tail, 16 * (3 + NE + 2 * NE))
            sp.wait_ge(a_free, 2 + NCH)
            sp.wait_ge(b_c, 1)
            with sp.Fori(0, NE) as e:
                lo, hi = expert_ends(sp, e)
                first = sp.snap(e * CAP - lo * ST)
                with sp.Fori(lo, hi) as i:
                    sp.wait_ge(b_xt, i + 1)
                    sp.wait_ge(b_meta, i + 1)
                    row = (first + i * ST).with_bounds(min_val=0, max_val=XE_ROWS - ST)
                    sp.dma_start(xrows[:, :, :], xe_dram[bass.ds(row, ST), :]
                                 .rearrange("(k p) r -> p k r", p=P)).then_inc(b_rl, 16)
            hi = sp.value_load(eend[0:1, NE:NE + 1], min_val=1, max_val=NE * 25)
            sp.wait_ge(b_xt, hi + 1)
            sp.wait_ge(b_meta, hi + 1)
            sp.sem_inc(tk_s, 1)
            sp.dma_start(xrows[:, :, :], xe_dram[0:ST, :].rearrange("(k p) r -> p k r", p=P)).then_inc(b_rl, 16)
            sp.wait_ge(b_rl, hi * 16 + 16)
            sp.sem_inc(tk_s, 1)
            sp.wait_ge(b_t, hi + 1)
            sp.sem_inc(tk_s, 1)

        @block.gpsimd
        def _(g):
            def cst(ins):
                ins.then_inc(s_cst, 1)

            cst(g.memset(ident[:, :], 0.0))
            cst(g.memset(pen[:, :], 0.0))
            cst(g.memset(ones[:, :], 1.0))
            cst(g.memset(tri[:, :], 1.0))
            cst(g.memset(vmask[:, :], 1.0))
            cst(g.memset(tail[:, :, :], 0.0))
            g.wait_ge(s_cst, 6)
            g.affine_select(out=ident[:, :], in_=ident[:, :], compare_op=ALU.not_equal, fill=1.0, base=0,
                            pattern=[[-1, P]], channel_multiplier=1).then_inc(s_id, 1)
            g.affine_select(out=pen[:, :], in_=pen[:, :], compare_op=ALU.not_equal, fill=-BIG, base=0,
                            pattern=[[-1, P]], channel_multiplier=1).then_inc(s_id, 1)
            g.affine_select(out=tri[:, :], in_=tri[:, :], compare_op=ALU.is_gt, fill=0.0, base=0,
                            pattern=[[1, P]], channel_multiplier=-1).then_inc(s_id, 1)
            g.affine_select(out=vmask[:, :], in_=vmask[:, :], compare_op=ALU.is_ge, fill=0.0, base=LAST - 1,
                            pattern=[[0, 1]], channel_multiplier=-1).then_inc(s_id, 1)
            g.iota(tail[:, :, D:D + 1], [[P, 2]], base=N, channel_multiplier=1,
                   allow_small_or_imprecise_dtypes=True).then_inc(s_id, 1)
            g.memset(tail[:, :, D + 3:D + 4], -1.0).then_inc(s_id, 1)
            g.iota(itemidx[:, :], [[1, ICOLS]], base=0, channel_multiplier=ICOLS,
                   allow_small_or_imprecise_dtypes=True).then_inc(s_id, 1)
            g.iota(iota8[:, :], [[1, NE]], base=0, channel_multiplier=0,
                   allow_small_or_imprecise_dtypes=True).then_inc(s_id, 1)
            g.iota(ecap[:, :], [[CAP, NE]], base=0, channel_multiplier=0,
                   allow_small_or_imprecise_dtypes=True).then_inc(s_id, 1)
            g.iota(tok[:, :], [[P, NT]], base=0, channel_multiplier=1,
                   allow_small_or_imprecise_dtypes=True).then_inc(s_id, 1)
            g.iota(iota_n, [[1, NTX * P]], base=0, channel_multiplier=0,
                   allow_small_or_imprecise_dtypes=True).then_inc(s_id, 1)
            g.memset(kT[:, NT * P:NTX * P], 0.0).then_inc(s_id, 1)
            g.memset(acc[:, NULL_T, :], 0.0).then_inc(s_id, 1)
            g.memset(m_all[:, NULL_T:NTX], 0.0).then_inc(s_id, 1)
            g.sem_inc(s_accw, 2)

            def keep(c, b):
                g.wait_ge(s_xl, CH * (c + 2))
                g.sem_inc(tk_g, 1)
                g.tensor_copy(acc[:, bass.ds(c * CH, CH), :], xlr[:, b, :, :]).then_inc(s_accw, 1)

            with g.Fori(0, NCH // 2) as k:
                for b in range(2):
                    keep(2 * k + b, b)
            keep(NCH - 1, 0)

            g.wait_ge(s_rw, 16 * (NCH + 1))
            g.wait_ge(s_m0, 1)
            g.sem_inc(xg_free, XSLOTS)

            def gather(k, v, first=False):
                gr = k * ISLOTS + v
                slot = v % XSLOTS
                g.wait_ge(s_idx[v], 16 * (k + 1))
                g.wait_ge(xg_free, gr + 1)
                g.sem_inc(tk_g, 1)
                for j in range(G):
                    g.indirect_dma_start(
                        out=xg[:, slot * G + j, :], out_offset=None, in_=rows_dram[:, :],
                        in_offset=bass.IndirectOffsetOnAxis(ap=idx[:, v, j:j + 1], axis=0)).then_inc(s_g[slot], 16)
                if not first:
                    landed = 2 * k + (v - 1) // XSLOTS + 1
                    g.wait_ge(s_g[(v - 1) % XSLOTS], 16 * G * landed)
                    g.sem_inc(xg_ready, 1)

            for v in range(ISLOTS):
                gather(0, v, first=v == 0)
            with g.Fori(1, NG // ISLOTS) as k:
                for v in range(ISLOTS):
                    gather(k, v)
            g.wait_ge(s_g[XSLOTS - 1], 16 * G * (NG // XSLOTS))
            g.sem_inc(xg_ready, 1)

            def load_w(e, b):
                g.dma_start(w1s[:, b, :, :], W1[bass.ds(e, 1), :, :].rearrange("o (c p) h -> p (o c) h", p=P)).then_inc(b_w[b], 16)
                g.dma_start(w2s[:, b, :, :], W2[bass.ds(e, 1), :, :].rearrange("o (c p) d -> p (o c) d", p=P)).then_inc(b_w[b], 16)

            n_items = item_count(g)
            g.wait_ge(s_acc, n_items + 1)
            g.sem_inc(tk_g, 1)
            load_w(0, 0)
            load_w(1, 1)

            def scatter(c, b, k, last=False):
                g.wait_ge(a_slot, c + 1)
                g.sem_inc(tk_g, 1)
                for u in range(CH):
                    n = LAST if last and u == CH - 1 else P
                    for r in range(2):
                        g.indirect_dma_start(
                            out=xe_dram[:, :], in_=rows[0:n, b, u, :], in_offset=None,
                            out_offset=bass.IndirectOffsetOnAxis(ap=slots[0:n, b, r, u:u + 1], axis=0))\
                            .then_inc(a_sc, 16)
                g.wait_ge(a_sc, 16 * 2 * CH * (c + 1))
                g.sem_inc(a_free, 1)

            with g.Fori(0, NCH // 2) as k:
                for b in range(2):
                    scatter(2 * k + b, b, k)
            scatter(NCH - 1, 0, NCH // 2, last=True)

            g.wait_ge(a_o[0], 16 * 5)
            g.wait_ge(a_o[1], 16 * 3)
            g.wait_ge(a_tail, 16 * (3 + NE + 2 * NE))
            g.wait_ge(b_c, 1)

            def add_rows(e):
                lo, hi = expert_ends(g, e)
                with g.Fori(lo, hi) as i:
                    g.wait_ge(b_yb, i + 1)
                    g.sem_inc(tk_g, 1)
                    for k in range(2):
                        g.indirect_dma_start(
                            out=out[:, :], in_=ybuf[:, k, :], in_offset=None,
                            out_offset=bass.IndirectOffsetOnAxis(ap=tokB[:, k:k + 1], axis=0),
                            compute_op=ALU.add).then_inc(b_sc, 16)
                        g.wait_ge(b_sc, i * 32 + 16 * (k + 1))
                        g.sem_inc(b_t if k else tk_g, 1)

            add_rows(0)
            with g.Fori(0, NE // 2 - 1) as k:
                for b in range(2):
                    load_w(2 * k + 2 + b, b)
                    add_rows(2 * k + 1 + b)
            add_rows(NE - 1)

        @block.vector
        def _(v):
            v.memset(acc[96:P, NT - 1, 0:D], 0.0).then_inc(s_zero, 1)
            v.memset(raw_i[96:P, 0, :], 0).then_inc(s_zero, 1)
            v.memset(raw_i[96:P, 1, :], PAD_DST).then_inc(s_zero, 1)
            v.memset(xlr[:, :, :, D:W1COLS], 1.0).then_inc(s_v0, 1)
            v.memset(epsc[:, :], EPS).then_inc(s_v0, 1)
            v.memset(zero8[:, :], 0.0).then_inc(s_v0, 1)
            v.memset(ebase[:, 0, :], 0.0).then_inc(s_v0, 1)
            v.memset(eend[:, :], 0).then_inc(s_v0, 1)
            v.sem_inc(s_qks, 2)
            v.sem_inc(s_acc, 1)
            v.memset(stepw[:, :], 0.0).then_inc(s_v0, 1)
            v.sem_inc(s_xl, CH)
            v.wait_ge(s_edge, 64)
            for k in range(2):
                v.tensor_copy(rawf[0:GP, k, :], raw_i[0:GP, k, :]).then_inc(s_rawf, 1)
            v.wait_ge(s_rawf, 2)
            dg = rawf[0:GP, 1, :].rearrange("p (h n) -> p h n", h=2)
            v.tensor_reduce(gmin[0:GP, :], dg, axis=X_AXIS, op=ALU.min).then_inc(s_eng0, 1)
            v.tensor_reduce(gmax[0:GP, :], dg, axis=X_AXIS, op=ALU.max).then_inc(s_eng0, 1)
            v.wait_ge(s_eng0, 2)
            v.tensor_copy(ghl[0:GP, 0, :], gmax[0:GP, :]).then_inc(s_eng0, 1)
            v.tensor_copy(ghl[0:GP, 1, :], gmin[0:GP, :]).then_inc(s_eng0, 1)
            v.wait_ge(s_eng0, 4)
            v.tensor_scalar(ghl[0:GP, :, :], ghl[0:GP, :, :], 7, None, ALU.arith_shift_right).then_inc(s_eng0, 1)
            v.wait_ge(s_eng0, 5)
            v.tensor_copy(ghf[0:GP, 1, :], ghl[0:GP, 1, :]).then_inc(s_eng0, 1)
            v.tensor_tensor(ghf[0:GP, 0, :], ghl[0:GP, 0, :], ghl[0:GP, 1, :], ALU.subtract).then_inc(s_eng0, 1)
            v.wait_ge(s_eng0, 7)
            v.tensor_scalar(ghf[0:GP, 0, :], ghf[0:GP, 0, :], 1.0, None, ALU.add).then_inc(s_grp, 1)
            for h in range(2):
                for k, o in ((0, srccol), (1, dstcol)):
                    v.wait_ge(s_et, 2 * h + k + 1)
                    v.tensor_copy(o[:, h:NG:2, :].rearrange("p q j -> p j q"),
                                  pb[6 + k][:, 0:G * GP].rearrange("p (j q) -> p j q", j=G)).then_inc(s_ec, 1)
            v.wait_ge(s_grpb, 64)
            v.wait_ge(s_v0, 6)
            v.wait_ge(s_id, 14)
            v.tensor_tensor_scan(incl[:, :], cntb[:, 0, :], stepw[:, :], 0.0, ALU.add, ALU.add).then_inc(s_eng0, 1)
            v.wait_ge(s_eng0, 8)
            v.tensor_tensor(basef[:, :], incl[:, :], cntb[:, 0, :], ALU.subtract).then_inc(s_eng0, 1)
            v.tensor_copy(incl_i[:, 0:NG], incl[0:1, :]).then_inc(s_eng0, 1)
            v.wait_ge(s_eng0, 10)
            v.tensor_tensor(delta[:, :], cntb[:, 1, :], basef[:, :], ALU.subtract).then_inc(s_eng0, 1)
            v.wait_ge(s_eng0, 11)
            v.tensor_scalar(stepw[:, 0:1], delta[:, 0:1], 1.0, float(TBITS), ALU.mult, ALU.add).then_inc(s_eng0, 1)
            v.tensor_tensor(stepw[:, 1:NG], delta[:, 1:NG], delta[:, 0:NG - 1], ALU.subtract).then_inc(s_eng0, 1)
            v.wait_ge(s_eng0, 13)
            v.tensor_scalar(stepw[:, 1:NG], stepw[:, 1:NG], float(TBITS), None, ALU.add).then_inc(s_eng0, 1)
            v.wait_ge(s_eng0, 14)
            with v.Fori(0, ICOLS) as c:
                v.wait_ge(s_eng0, c + 14)
                v.sem_inc(tk_v, 1)
                v.scalar_tensor_tensor(out=gsel[:, :], in0=basef[:, :], scalar=col(itemidx, c), in1=stepw[:, :],
                                       op0=ALU.is_le, op1=ALU.mult, accum_out=col(icode, c)).then_inc(s_eng0, 1)
            v.wait_ge(s_eng0, 14 + ICOLS)
            v.tensor_tensor(icode[:, :], icode[:, :], itemidx[:, :], ALU.add).then_inc(s_eng0, 1)
            v.tensor_scalar(incl_i[:, NG:NG + 1], incl[0:1, NG - 1:NG], -1.0, None, ALU.add).then_inc(s_v0, 1)
            v.tensor_scalar(ivalid[:, :], itemidx[:, :], incl[:, NG - 1:NG], None, ALU.is_lt).then_inc(s_eng0, 1)
            null = float(NULL_T + TBITS * (NG - 1))
            v.wait_ge(s_eng0, 16 + ICOLS)
            v.tensor_scalar(icode[:, :], icode[:, :], -float(TBITS) - null, None, ALU.add).then_inc(s_eng0, 1)
            v.wait_ge(s_eng0, 17 + ICOLS)
            v.tensor_tensor(icode[:, :], icode[:, :], ivalid[:, :], ALU.mult).then_inc(s_eng0, 1)
            v.wait_ge(s_eng0, 18 + ICOLS)
            v.tensor_scalar(ilist[:, :], icode[:, :], null, None, ALU.add).then_inc(s_code, 1)

            v.wait_ge(s_x, 16 * (NCH + 1))
            v.wait_ge(s_wl, 16 * 9)
            v.wait_ge(s_zero, 3)

            def norm_chunk(c, b):
                v.wait_ge(s_xl, CH * (c + 1))
                v.sem_inc(tk_v, 1)
                for u in range(CH):
                    v.bn_stats(st[:, u, :], acc[:, bass.ds(c * CH + u, 1), 0:D].rearrange("p o d -> p (o d)")).then_inc(s_st, 1)
                v.wait_ge(s_st, CH * (c + 1))
                v.sem_inc(tk_v, 1)
                for u in range(CH):
                    v.bn_aggr(mv[:, b, u, :], st[:, u, :]).then_inc(s_mv, 1)
                v.wait_ge(s_rs, c + 1)
                v.wait_ge(s_tp, CH * (c + 1))
                v.wait_ge(s_accw, c + 1)
                v.wait_ge(s_mv, CH * (c + 1))
                v.sem_inc(tk_v, 1)
                for u in range(CH):
                    v.tensor_scalar(xlr[:, b, u, 0:D], acc[:, bass.ds(c * CH + u, 1), 0:D].rearrange("p o d -> p (o d)"),
                                    mv[:, b, u, 0:1], rstd[:, b, u:u + 1],
                                    ALU.subtract, ALU.mult).then_inc(s_xl, 1)
                for u in range(CH):
                    t = c * CH + u
                    v.wait_ge(s_qk, t + 3)
                    v.sem_inc(tk_v, 1)
                    v.tensor_tensor(qk_all[:, bass.ds(t, 1), :].rearrange("p o s -> p (o s)"),
                                    pb[2 + (7 * b + u) % 2][:, 0:2 * S], bqk[:, :], ALU.add).then_inc(s_qks, 1)

            with v.Fori(0, NCH // 2) as k:
                for b in range(2):
                    norm_chunk(2 * k + b, b)
            norm_chunk(NCH - 1, 0)
            v.wait_ge(s_q, 1)
            v.wait_ge(s_qks, 2 + NT)
            v.tensor_tensor(prod[:, :, :], q_all[:, :, :], qk_all[:, :, S:2 * S], ALU.mult).then_inc(s_eng0, 1)
            v.wait_ge(s_eng0, 19 + ICOLS)
            v.wait_ge(s_accw, 2 + NCH)
            v.wait_ge(s_kt, 2 + NT)
            v.wait_ge(s_ir, 16)
            v.wait_ge(s_id, 14)
            v.tensor_reduce(m_all[:, 0:NT], prod[:, :, :], axis=X_AXIS, op=ALU.add).then_inc(s_m0, 1)
            v.wait_ge(s_m0, 1)

            def edge_mask(t, gr, want, first=False):
                if not first:
                    v.wait_ge(s_sc, want)
                v.tensor_tensor(mask[:, :, :],
                                iota_n[:, bass.ds(t * P, P)].unsqueeze(1).to_broadcast([P, G, P]),
                                dstcol[:, bass.ds(gr, 1), :].rearrange("p o j -> p (o j)").unsqueeze(2).to_broadcast([P, G, P]),
                                ALU.not_equal).then_inc(s_mask, 1)

            def add_sums(t, want):
                a = acc[:, bass.ds(t, 1), :].rearrange("p o d -> p (o d)")
                v.wait_ge(s_pv, want)
                v.wait_ge(s_al, want)
                v.wait_ge(s_acc, want)
                v.sem_inc(tk_v, 1)
                v.scalar_tensor_tensor(out=a, in0=a, scalar=alpha[:, :], in1=pb[3][:, 0:W1COLS],
                                       op0=ALU.mult, op1=ALU.add).then_inc(s_acc, 1)

            def maximum(t, want, first=False):
                m = m_all[:, bass.ds(t, 1)]
                v.wait_ge(s_sc, want)
                if not first:
                    v.wait_ge(s_mn, want - 1)
                    v.wait_ge(s_ms, want - 1)
                v.sem_inc(tk_v, 1)
                v.tensor_reduce(mx[:, :], pb[1][:, :], axis=X_AXIS, op=ALU.max).then_inc(s_mx, 1)
                v.wait_ge(s_mx, want)
                if not first:
                    v.wait_ge(s_md, want - 1)
                    v.wait_ge(s_nb, want - 1)
                v.sem_inc(tk_v, 1)
                v.tensor_tensor(mnew[:, :], m, mx[:, :], ALU.max).then_inc(s_mn, 1)
                v.wait_ge(s_mn, want)
                if not first:
                    v.wait_ge(s_p, want - 1)
                v.sem_inc(tk_v, 1)
                v.tensor_scalar(nbias[:, :], mnew[:, :], -1.0 / DK, None, ALU.mult).then_inc(s_nb, 1)
                if not first:
                    v.wait_ge(s_al, want - 1)
                    v.sem_inc(tk_v, 1)
                v.tensor_tensor(mdiff[:, :], m, mnew[:, :], ALU.subtract).then_inc(s_md, 1)
                v.wait_ge(s_md, want)
                v.sem_inc(tk_v, 1)
                v.tensor_copy(m, mnew[:, :]).then_inc(s_ms, 1)

            n_items = item_count(v)
            t0, g0 = load_code(v, 0)
            edge_mask(t0, g0, 0, first=True)
            maximum(t0, 1, first=True)
            t1, g1 = load_code(v, 1)
            edge_mask(t1, g1, 1)
            with v.Fori(1, n_items) as i:
                tp, _ = load_code(v, i - 1)
                t, _ = load_code(v, i)
                tn, gn = load_code(v, i + 1)
                maximum(t, i + 1)
                edge_mask(tn, gn, i + 1)
                add_sums(tp, i)
            tl, _ = load_code(v, last_item(v))
            add_sums(tl, n_items)

            v.wait_ge(s_acc, n_items + 1)
            v.sem_inc(tk_v, 1)
            steps = 40

            def chunk_a(c, b, k, last=False):
                n = [0]

                def step(ins):
                    ins.then_inc(a_v, 1)
                    n[0] += 1

                def after_steps():
                    v.wait_ge(a_v, steps * c + n[0])
                    v.sem_inc(tk_v, 1)

                t0 = c * CH
                step(v.reciprocal(rl[:, :], acc[:, bass.ds(t0, CH), D:W1COLS].rearrange("p u o -> p (u o)")))
                after_steps()
                v.wait_ge(a_x[b], 16 * (k + 1) + (16 if last else 0))
                v.sem_inc(tk_v, 1)
                for u in range(CH):
                    v.scalar_tensor_tensor(out=xr[:, b, u, :], in0=acc[:, bass.ds(t0 + u, 1), 0:D].rearrange("p o d -> p (o d)"),
                                           scalar=rl[:, u:u + 1], in1=xr[:, b, u, :],
                                           op0=ALU.mult, op1=ALU.add).then_inc(a_x2, 1)
                v.wait_ge(a_free, c + 1)
                v.wait_ge(a_x2, CH * (c + 1))
                v.sem_inc(tk_v, 1)
                for r in range(2):
                    ap = (lambda u: xr[:, b, u, :]) if r == 0 else (lambda u: rows[:, b, u, 0:D])
                    for u in range(CH):
                        step(v.bn_stats(st[:, u, :], ap(u)))
                    after_steps()
                    for u in range(CH):
                        v.bn_aggr(mv[:, b, u, :], st[:, u, :]).then_inc(a_mv, 1)
                    v.wait_ge(a_mv, 2 * CH * c + CH * (r + 1))
                    v.wait_ge(a_rs, 2 * c + r + 1)
                    v.sem_inc(tk_v, 1)
                    for u in range(CH):
                        v.tensor_scalar(rows[:, b, u, 0:D], ap(u), mv[:, b, u, 0:1], rstd[:, b, u:u + 1],
                                        ALU.subtract, ALU.mult).then_inc(a_xn, 1)
                    v.wait_ge(a_xn, 2 * CH * c + CH * (r + 1))
                    v.sem_inc(tk_v, 1)
                v.wait_ge(a_lg, CH * (c + 1))
                v.sem_inc(tk_v, 1)
                step(v.tensor_tensor(lg[:, :, :], pb[6][:, 0:CH * NE].rearrange("p (u e) -> p u e", u=CH),
                                     brb[:, :].unsqueeze(1).to_broadcast([P, CH, NE]), ALU.add))
                after_steps()
                for u in range(CH):
                    last_i = v.max(top[:, u, :], lg[:, u, :])
                step(last_i)
                after_steps()
                for u in range(CH):
                    last_i = v.max_index(topi[:, u, :], top[:, u, :], lg[:, u, :])
                step(last_i)
                v.tensor_tensor(tdiff[:, :], top[:, :, 1], top[:, :, 0], ALU.subtract).then_inc(a_df, 1)
                after_steps()
                step(v.tensor_copy(idxf[:, :, :], topi[:, :, 0:2]))
                after_steps()
                for r in range(2):
                    step(v.tensor_tensor(oh[:, r, :, :], iota8[:, :].unsqueeze(1).to_broadcast([P, CH, NE]),
                                         idxf[:, :, r:r + 1].to_broadcast([P, CH, NE]), ALU.is_equal))
                after_steps()
                last_i = v.tensor_tensor(asg[:, :, :], oh[:, 0, :, :], oh[:, 1, :, :], ALU.add)
                if last:
                    step(last_i)
                    after_steps()
                    last_i = v.tensor_scalar(asg[:, CH - 1, :], asg[:, CH - 1, :], vmask[:, :], None, ALU.mult)
                last_i.then_inc(a_as, 1)
                v.wait_ge(a_ex, c + 1)
                v.sem_inc(tk_v, 1)
                step(v.tensor_scalar(den2[:, :], ex[:, :], 1.0, None, ALU.add))
                after_steps()
                step(v.reciprocal(w0[:, :], den2[:, :]))
                after_steps()
                step(v.tensor_tensor(rows[:, b, :, D + 1], ex[:, :], w0[:, :], ALU.mult))
                step(v.tensor_copy(rows[:, b, :, D], tok[:, bass.ds(t0, CH)]))
                step(v.tensor_copy(rows[:, b, :, D + 3], idxf[:, :, 0]))
                after_steps()
                step(v.tensor_tensor(rows[:, b, :, D + 2], w0[:, :], rows[:, b, :, D + 1], ALU.subtract))
                v.wait_ge(a_pos, c + 1)
                v.sem_inc(tk_v, 1)
                for u in range(CH):
                    step(v.tensor_tensor(ebase[:, u + 1, :], ebase[:, u, :],
                                         pb[7][:, 64 + NE * u:64 + NE * (u + 1)], ALU.add))
                    after_steps()
                step(v.tensor_tensor(slotv[:, :, :], pb[7][:, 0:CH * NE].rearrange("p (u e) -> p u e", u=CH),
                                     ebase[:, 0:CH, :], ALU.add))
                after_steps()
                step(v.tensor_tensor(slotv[:, :, :], slotv[:, :, :],
                                     ecap[:, :].unsqueeze(1).to_broadcast([P, CH, NE]), ALU.add))
                step(v.tensor_copy(ebase[:, 0, :], ebase[:, CH, :]))
                after_steps()
                for r in range(2):
                    v.tensor_tensor(slotp[:, r, :, :], oh[:, r, :, :], slotv[:, :, :], ALU.mult)
                    last_i = None
                step(v.drain())
                after_steps()
                step(v.tensor_reduce(slotf[:, :, :], slotp[:, :, :, :], axis=X_AXIS, op=ALU.add))
                after_steps()
                while n[0] < steps:
                    v.sem_inc(a_v, 1)
                    n[0] += 1
                assert n[0] == steps, n[0]
                v.tensor_copy(slots[:, b, :, :], slotf[:, :, :]).then_inc(a_slot, 1)

            v.sem_inc(a_free, 2)
            with v.Fori(0, NCH // 2) as k:
                for b in range(2):
                    chunk_a(2 * k + b, b, k)
            chunk_a(NCH - 1, 0, NCH // 2, last=True)

            v.wait_ge(a_slot, NCH)
            v.tensor_copy(cnt_i[:, :], ebase[0:1, 0, :]).then_inc(a_cnt, 1)
            v.wait_ge(a_cnt, 1)
            v.tensor_scalar(nst_f[:, :], cnt_i[:, :], float(ST - 1), None, ALU.add).then_inc(b_v, 1)
            v.wait_ge(b_v, 1)
            v.tensor_copy(nst_i[:, :], nst_f[:, :]).then_inc(b_v, 1)
            v.wait_ge(b_v, 2)
            v.tensor_scalar(nst_i[:, :], nst_i[:, :], 8, None, ALU.arith_shift_right).then_inc(b_v, 1)
            v.wait_ge(b_v, 3)
            v.tensor_scalar(nst_f[:, :], nst_i[:, :], 1.0, None, ALU.max).then_inc(b_v, 1)
            v.wait_ge(b_v, 4)
            v.tensor_tensor_scan(eend_f[:, :], nst_f[:, :], zero8[:, :], 0.0, ALU.add, ALU.add).then_inc(b_v, 1)
            v.wait_ge(b_v, 5)
            v.tensor_copy(eend[:, 1:NE + 1], eend_f[:, :]).then_inc(b_c, 1)
            v.wait_ge(b_c, 1)

            def meta(want):
                v.wait_ge(b_rl, want * 16)
                v.wait_ge(b_lat, want)
                v.sem_inc(tk_v, 1)
                v.tensor_copy(metaA[:, :, :], xrows[:, :, D:MROW]).then_inc(b_meta, 1)

            def finish(e, i):
                v.wait_ge(b_t, i + 1)
                v.wait_ge(b_meta, i + 2)
                v.sem_inc(tk_v, 1)
                v.tensor_copy(tokB[:, :], metaA[:, :, 0])
                v.tensor_scalar(weq[:, :], metaA[:, :, 3], iota8[:, bass.ds(e, 1)], None, ALU.is_equal)
                v.drain().then_inc(b_v, 1)
                v.wait_ge(b_v, 5 + i * 2 + 1)
                v.sem_inc(tk_v, 1)
                v.tensor_tensor(weq[:, :], weq[:, :], metaA[:, :, 2], ALU.mult)
                v.drain().then_inc(b_v, 1)
                v.wait_ge(b_v, 5 + i * 2 + 2)
                v.sem_inc(tk_v, 1)
                v.tensor_tensor(wsel[:, :], weq[:, :], metaA[:, :, 1], ALU.add).then_inc(b_lat, 1)
                v.wait_ge(b_y, i + 1)
                v.wait_ge(b_lat, i + 2)
                v.sem_inc(tk_v, 1)
                for k in range(2):
                    v.tensor_tensor(ysum[:, k, :], pb[3 + k][:, 0:D], b2b[:, bass.ds(e, 1), :].rearrange("p o d -> p (o d)"),
                                    ALU.add).then_inc(b_ys, 1)
                v.wait_ge(b_ys, i * 2 + 4)
                v.sem_inc(tk_v, 1)
                v.tensor_scalar(ybuf[:, 0, :], ysum[:, 0, :], wsel[:, 0:1], None, ALU.mult)
                v.tensor_scalar(ybuf[:, 1, :], ysum[:, 1, :], wsel[:, 1:2], None, ALU.mult)
                v.drain().then_inc(b_yb, 1)

            v.wait_ge(a_tail, 16 * (3 + NE + 2 * NE))
            v.sem_inc(b_ys, 2)
            v.sem_inc(b_lat, 1)
            v.sem_inc(b_meta, 1)
            v.sem_inc(b_t, 1)
            with v.Fori(0, NE) as e:
                lo, hi = expert_ends(v, e)
                with v.Fori(lo, hi) as i:
                    meta(i + 1)
                    finish(e, i)
            hi = v.value_load(eend[0:1, NE:NE + 1], min_val=1, max_val=NE * 25)
            meta(hi + 1)

        @block.scalar
        def _(a):
            a.sem_inc(s_ev, 2)
            a.sem_inc(s_kt, 2)
            a.wait_ge(s_wl, 16 * 9)
            a.wait_ge(s_v0, 6)

            def inverse_std(b, ln_sem, ln_want, rs_sem):
                nc.scalar.activation(lnv[:, :], mv[:, b, :, 1], ACT.Ln, bias=epsc[:, :]).then_inc(ln_sem, 1)
                a.wait_ge(ln_sem, ln_want)
                a.sem_inc(tk_a, 1)
                nc.scalar.activation(rstd[:, b, :], lnv[:, :], ACT.Exp, scale=-0.5).then_inc(rs_sem, 1)

            def chunk_0(c, b):
                a.wait_ge(s_mv, CH * (c + 1))
                a.wait_ge(s_xl, CH * (c + 1))
                a.sem_inc(tk_a, 1)
                inverse_std(b, s_ln, c + 1, s_rs)
                for u in range(CH):
                    t = c * CH + u
                    w = (7 * b + u) % 2
                    a.wait_ge(s_tp, 2 * CH + t + 1)
                    a.wait_ge(s_qk, t + 1)
                    a.sem_inc(tk_a, 1)
                    nc.scalar.copy(xlT[:, w, :, :].rearrange("p c n -> p (c n)"), pb[w][:, 0:D]).then_inc(s_ev, 1)
                    a.wait_ge(s_qk, t + 3)
                    a.sem_inc(tk_a, 1)
                    nc.scalar.activation(kT[0:S, bass.ds(t * P, P)], pb[4 + w][0:S, 0:P], ACT.Identity,
                                         bias=bkcol[:, :]).then_inc(s_kt, 1)

            with a.Fori(0, NCH // 2) as k:
                for b in range(2):
                    chunk_0(2 * k + b, b)
            chunk_0(NCH - 1, 0)
            a.wait_ge(s_qks, 2 + NT)
            nc.scalar.activation(q_all[:, :, :], qk_all[:, :, 0:S], ACT.Tanh).then_inc(s_q, 1)

            a.wait_ge(s_m0, 1)
            a.wait_ge(s_kt, 2 + NT)

            def copy_k(t, want, first=False):
                if not first:
                    a.wait_ge(s_sc, want)
                    a.sem_inc(tk_a, 1)
                nc.scalar.copy(kts[:, :], kT[0:S, bass.ds(t * P, P)]).then_inc(s_kts, 1)

            def copy_q(gr, want, first=False):
                if not first:
                    a.wait_ge(s_qt, want)
                a.wait_ge(xg_ready, gr + 1)
                a.sem_inc(tk_a, 1)
                nc.scalar.copy(qs[:, :, :], xg[:, bass.ds((gr % XSLOTS) * G, G), W1COLS:ROW]).then_inc(s_qs, 1)

            def copy_qT(want):
                a.wait_ge(s_qt, want)
                a.sem_inc(tk_a, 1)
                nc.scalar.copy(qT[:, :], pb[0][0:S, :]).then_inc(s_qTs, 1)

            def exponentials(want, first=False):
                a.wait_ge(s_nb, want)
                if not first:
                    a.wait_ge(s_pt, want - 1)
                a.sem_inc(tk_a, 1)
                nc.scalar.activation(prob[:, :], pb[1][:, :], ACT.Exp, bias=nbias[:, :], scale=1.0 / DK).then_inc(s_p, 1)

            def scale_and_copy(want):
                a.wait_ge(s_md, want)
                a.wait_ge(s_acc, want)
                a.sem_inc(tk_a, 1)
                nc.scalar.activation(alpha[:, :], mdiff[:, :], ACT.Exp, scale=1.0 / DK).then_inc(s_al, 1)
                a.wait_ge(s_pt, want)
                a.sem_inc(tk_a, 1)
                nc.scalar.copy(probT[:, :], pb[2][:, :]).then_inc(s_pts, 1)

            n_items = item_count(a)
            t0, g0 = load_code(a, 0)
            copy_q(g0, 0, first=True)
            copy_k(t0, 0, first=True)
            copy_qT(1)
            t1, g1 = load_code(a, 1)
            copy_q(g1, 1)
            exponentials(1, first=True)
            copy_qT(2)
            copy_k(t1, 1)
            scale_and_copy(1)
            _, g2 = load_code(a, 2)
            copy_q(g2, 2)
            with a.Fori(1, n_items) as i:
                tn, _ = load_code(a, i + 1)
                _, gn = load_code(a, i + 2)
                exponentials(i + 1)
                copy_qT(i + 2)
                copy_k(tn, i + 1)
                scale_and_copy(i + 1)
                copy_q(gn, i + 2)

            a.wait_ge(s_acc, n_items + 1)
            a.sem_inc(a_ev, 4)

            def chunk_a(c, b):
                for r in range(2):
                    a.wait_ge(a_mv, 2 * CH * c + CH * (r + 1))
                    a.sem_inc(tk_a, 1)
                    inverse_std(b, a_ln, 2 * c + r + 1, a_rs)
                for u in range(CH):
                    t = c * CH + u
                    w = (7 * b + u) % 2
                    a.wait_ge(a_tp, 2 * (t + 1))
                    a.sem_inc(tk_a, 1)
                    for h in range(2):
                        ins = nc.scalar.activation(xnT[:, w, h, :], pb[4 + w][:, h * P:(h + 1) * P], ACT.Identity,
                                                   bias=bcol[:, h:h + 1], scale=gcol[:, h:h + 1])
                        ins.then_inc(a_ev, 1)
                a.wait_ge(a_df, c + 1)
                a.sem_inc(tk_a, 1)
                nc.scalar.activation(ex[:, :], tdiff[:, :], ACT.Exp).then_inc(a_ex, 1)

            with a.Fori(0, NCH // 2) as k:
                for b in range(2):
                    chunk_a(2 * k + b, b)
            chunk_a(NCH - 1, 0)

            a.wait_ge(b_c, 1)
            a.wait_ge(a_tail, 16 * (3 + NE + 2 * NE))
            a.sem_inc(b_g, 3)

            def xT_copy(want):
                a.wait_ge(b_xt, want + 1)
                a.sem_inc(tk_a, 1)
                for h in range(2):
                    nc.scalar.activation(xT[:, h, :], pb[0][:, h * ST:(h + 1) * ST], ACT.Identity,
                                         bias=bcol[:, h:h + 1], scale=gcol[:, h:h + 1]).then_inc(b_xe, 1)

            xT_copy(1)
            with a.Fori(0, NE) as e:
                lo, hi = expert_ends(a, e)
                with a.Fori(lo, hi) as i:
                    for m in range(4):
                        a.wait_ge(b_h, i * 4 + (m + 1))
                        a.sem_inc(tk_a, 1)
                        nc.scalar.activation(hT[:, m, :], pb[1 + m % 2][:, 0:ST], ACT.Gelu,
                                             bias=b1c[:, bass.ds(e * 4 + m, 1)]).then_inc(b_g, 1)
                    xT_copy(i + 2)

        @block.tensor
        def _(pe):
            mm = nc.tensor.matmul
            pe.wait_ge(s_id, 14)
            pe.wait_ge(s_rawf, 2)
            pe.sem_inc(s_tp, 2 * CH)
            pe.sem_inc(s_qk, 2)
            for h in range(2):
                if h:
                    pe.wait_ge(s_ec, 2)
                for k in range(2):
                    for j in range(G):
                        last = nc.tensor.transpose(pb[6 + k][:, j * GP:(j + 1) * GP],
                                                   rawf[0:GP, k, (h * G + j) * P:(h * G + j + 1) * P], ident[0:GP, 0:GP])
                    last.then_inc(s_et, 1)
            pe.wait_ge(s_wl, 16 * 9)

            def chunk_0(c, b):
                for u in range(CH):
                    t = c * CH + u
                    w = (7 * b + u) % 2
                    pe.wait_ge(s_xl, CH + t + 1)
                    pe.wait_ge(s_ev, t + 1)
                    pe.sem_inc(tk_p, 1)
                    for h in range(2):
                        last = nc.tensor.transpose(pb[w][:, h * P:(h + 1) * P], xlr[:, b, u, h * P:(h + 1) * P], ident[:, :])
                    last.then_inc(s_tp, 1)
                    pe.wait_ge(s_ev, t + 3)
                    pe.wait_ge(s_kt, t + 1)
                    pe.wait_ge(s_qks, t + 1)
                    pe.sem_inc(tk_p, 1)
                    for h in range(2):
                        mm(pb[2 + w][:, 0:2 * S], xlT[:, w, h, :], wqk[:, h, :], start=h == 0, stop=h == 1)
                    for h in range(2):
                        last = mm(pb[4 + w][0:S, 0:P], wqk[:, h, S:2 * S], xlT[:, w, h, :], start=h == 0, stop=h == 1)
                    last.then_inc(s_qk, 1)

            with pe.Fori(0, NCH // 2) as k:
                for b in range(2):
                    chunk_0(2 * k + b, b)
            chunk_0(NCH - 1, 0)

            def q_transposes(want):
                pe.wait_ge(s_qs, want)
                pe.sem_inc(tk_p, 1)
                for j in range(G):
                    last = nc.tensor.transpose(pb[0][0:S, j * P:(j + 1) * P], qs[:, j, :], ident[:, :])
                last.then_inc(s_qt, 1)

            def scores(want, first=False):
                pe.wait_ge(s_qTs, want)
                pe.wait_ge(s_kts, want)
                pe.wait_ge(s_mask, want)
                if not first:
                    pe.wait_ge(s_p, want - 1)
                pe.sem_inc(tk_p, 1)
                for j in range(G):
                    mm(pb[1][:, j * P:(j + 1) * P], mask[:, j, :], pen[:, :], start=j == 0, stop=False)
                mm(pb[1][:, :], kts[:, :], qT[:, :], start=False, stop=True).then_inc(s_sc, 1)

            def prob_transposes(want, first=False):
                pe.wait_ge(s_p, want)
                if not first:
                    pe.wait_ge(s_pts, want - 1)
                pe.sem_inc(tk_p, 1)
                for j in range(G):
                    last = nc.tensor.transpose(pb[2][:, j * P:(j + 1) * P], prob[:, j * P:(j + 1) * P], ident[:, :])
                last.then_inc(s_pt, 1)

            def sums(gr, want):
                pe.wait_ge(s_pts, want)
                pe.wait_ge(s_acc, want)
                pe.sem_inc(tk_p, 1)
                slot = pe.snap(gr % XSLOTS * G, min_val=0, max_val=(XSLOTS - 1) * G)
                for j in range(G):
                    last = mm(pb[3][:, 0:W1COLS], probT[:, j * P:(j + 1) * P],
                              xg[:, bass.ds(slot + j, 1), 0:W1COLS].rearrange("p o d -> p (o d)"),
                              start=j == 0, stop=j == G - 1)
                last.then_inc(s_pv, 1)

            pe.wait_ge(s_m0, 1)
            n_items = item_count(pe)
            q_transposes(1)
            scores(1, first=True)
            q_transposes(2)
            prob_transposes(1, first=True)
            _, g0 = load_code(pe, 0)
            scores(2)
            q_transposes(3)
            sums(g0, 1)
            prob_transposes(2)
            with pe.Fori(2, n_items) as i:
                _, gp = load_code(pe, i - 1)
                scores(i + 1)
                q_transposes(i + 2)
                sums(gp, i)
                prob_transposes(i + 1)
            _, gl = load_code(pe, last_item(pe))
            sums(gl, n_items)

            pe.wait_ge(s_acc, n_items + 1)
            pe.sem_inc(tk_p, 1)

            def chunk_a(c, b):
                for u in range(CH):
                    t = c * CH + u
                    w = (7 * b + u) % 2
                    pe.wait_ge(a_xn, 2 * CH * c + CH + u + 1)
                    pe.wait_ge(a_ev, 2 * t + 2)
                    pe.sem_inc(tk_p, 1)
                    for h in range(2):
                        nc.tensor.transpose(pb[4 + w][:, h * P:(h + 1) * P], rows[:, b, u, h * P:(h + 1) * P], ident[:, :])\
                            .then_inc(a_tp, 1)
                    pe.wait_ge(a_ev, 2 * t + 6)
                    pe.sem_inc(tk_p, 1)
                    for h in range(2):
                        last = mm(pb[6][:, u * NE:(u + 1) * NE], xnT[:, w, h, :], wr[:, h, :], start=h == 0, stop=h == 1,
                                  skip_group_check=True)
                    last.then_inc(a_lg, 1)
                pe.wait_ge(a_as, c + 1)
                pe.sem_inc(tk_p, 1)
                flat = asg[:, :, :].rearrange("p u e -> p (u e)")
                mm(pb[7][:, 0:CH * NE], tri[:, :], flat, start=True, stop=True, skip_group_check=True)
                mm(pb[7][:, 64:64 + CH * NE], ones[:, :], flat, start=True, stop=True, skip_group_check=True).then_inc(a_pos, 1)

            with pe.Fori(0, NCH // 2) as k:
                for b in range(2):
                    chunk_a(2 * k + b, b)
            chunk_a(NCH - 1, 0)

            pe.wait_ge(b_c, 1)

            def x_transposes(want):
                pe.wait_ge(b_rl, want * 16)
                pe.wait_ge(b_xe, want * 2)
                pe.sem_inc(tk_p, 1)
                for k in range(2):
                    for h in range(2):
                        last = nc.tensor.transpose(pb[0][:, h * ST + k * P:h * ST + (k + 1) * P],
                                                   xrows[:, k, h * P:(h + 1) * P], ident[:, :])
                last.then_inc(b_xt, 1)

            def expert(e, b, k):
                lo, hi = expert_ends(pe, e)
                pe.wait_ge(b_w[b], 32 * (k + 1))
                pe.sem_inc(tk_p, 1)
                with pe.Fori(lo, hi) as i:
                    pe.wait_ge(b_xe, i * 2 + 4)
                    for m in range(4):
                        pe.wait_ge(b_g, i * 4 + m + 2)
                        pe.sem_inc(tk_p, 1)
                        for c in range(2):
                            last = mm(pb[1 + m % 2][:, 0:ST], w1s[:, b, c, m * P:(m + 1) * P], xT[:, c, :],
                                      start=c == 0, stop=c == 1)
                        last.then_inc(b_h, 1)
                    x_transposes(i + 2)
                    pe.wait_ge(b_ys, i * 2 + 2)
                    for c in range(4):
                        pe.wait_ge(b_g, i * 4 + c + 4)
                        pe.sem_inc(tk_p, 1)
                        for k2 in range(2):
                            last = mm(pb[3 + k2][:, 0:D], hT[:, c, k2 * P:(k2 + 1) * P], w2s[:, b, c, :],
                                      start=c == 0, stop=c == 3)
                    last.then_inc(b_y, 1)

            pe.sem_inc(b_xt, 1)
            pe.sem_inc(b_xe, 2)
            x_transposes(1)
            with pe.Fori(0, NE // 2) as k:
                for b in range(2):
                    expert(2 * k + b, b, k)


_INS = ['x', 'src', 'dst', 'L0_gnn_Wq', 'L0_gnn_bq', 'L0_gnn_Wk', 'L0_gnn_bk', 'L0_ffn_gamma', 'L0_ffn_beta',
        'L0_ffn_Wr', 'L0_ffn_br', 'L0_ffn_W1', 'L0_ffn_b1', 'L0_ffn_W2', 'L0_ffn_b2']


def kernel(**inputs):
    import numpy as _np
    import concourse.bacc as _bacc
    from concourse import mybir as _mybir
    from concourse.bass_utils import run_bass_kernel_spmd as _run

    nc = _bacc.Bacc("TRN2", target_bir_lowering=False, num_devices=1)
    arrays, args = {}, []
    for name in _INS:
        a = _np.ascontiguousarray(inputs[name])
        arrays[f"in_{name}_dram"] = a
        args.append(nc.dram_tensor(f"in_{name}_dram", a.shape, _mybir.dt.from_np(a.dtype), kind="ExternalInput").ap())
    args.append(nc.dram_tensor("out_0_dram", (OUT_ROWS, D), _mybir.dt.float32, kind="ExternalOutput").ap())
    build(nc, *args)
    r = _run(nc, [arrays], core_ids=[0])
    return r.results[0]["out_0_dram"][0:N]
```

```python
import numpy as np
import concourse.bass as bass
from concourse import mybir
from contextlib import ExitStack

F32 = mybir.dt.float32
BF16 = mybir.dt.bfloat16
I32 = mybir.dt.int32
I16 = mybir.dt.int16
U32 = mybir.dt.uint32
ALU = mybir.AluOpType
ACT = mybir.ActivationFunctionType
X_AXIS = mybir.AxisListType.X
AT_LEAST = "sem-ge"

P = 128
N = 6250
D = 256
S = 25
E_IN = 106250
NE = 8
H = 512
EPS = 1e-5

NT = -(-N // P)
LAST = N - (NT - 1) * P
CH = 7
NCH = NT // CH
CHROWS = CH * P
NULL_T = NT
NTX = NT + 1
PAD_DST = NT * P - 1

G = 4
GE = G * P
NG = -(-E_IN // GE)
GP = NG // 2
FULLP = E_IN // (2 * GE)
RESTE = E_IN - FULLP * 2 * GE
ROW = D + 1 + S
W1COLS = D + 1
XSLOTS = 8
ISLOTS = 8
AHEAD = 8

ICOLS = 80
ITEMS = P * ICOLS
TBITS = 64
BIG = 1e30
DK = 5.0

CAP = 6528
ST = 256
MROW = D + 4
XE_ROWS = NE * CAP
OUT_ROWS = N + ST


def build(nc, x, src, dst, Wq, bq, Wk, bk, gamma, beta, Wr, br, W1, b1, W2, b2, out):
    ctx = ExitStack()
    with ctx:
        def sb(name, shape, dt=F32):
            return ctx.enter_context(nc.sbuf_tensor(name, shape, dt))

        def sem(name):
            return ctx.enter_context(nc.semaphore(name))

        ctx.enter_context(nc.allow_non_contiguous_dma(reason="small columns of weights"))

        rows_dram = nc.dram_tensor("rows_dram", (NT * P, ROW), F32, kind="Internal").ap()
        item_dram = nc.dram_tensor("item_dram", (ITEMS,), I16, kind="Internal").ap()
        xe_dram = nc.dram_tensor("xe_dram", (XE_ROWS, MROW), F32, kind="Internal").ap()

        acc = sb("acc", [P, NTX, W1COLS])
        m_all = sb("m_all", [P, NTX])
        item_row = sb("item_row", [1, ITEMS], I16)
        srccol = sb("srccol", [P, NG, G], I32)
        dstcol = sb("dstcol", [P, NG, G])
        ident = sb("ident", [P, P])
        pen = sb("pen", [P, P], BF16)
        tri = sb("tri", [P, P])
        ones = sb("ones", [P, P])
        iota8 = sb("iota8", [P, NE])
        ecap = sb("ecap", [P, NE])
        tok = sb("tok", [P, NT])
        itemidx = sb("itemidx", [P, ICOLS])
        vmask = sb("vmask", [P, 1])
        tail = sb("tail", [P, 2, MROW])
        wqk = sb("wqk", [P, 2, 2 * S])
        bqk = sb("bqk", [P, 2 * S])
        bkcol = sb("bkcol", [S, 1])
        wr = sb("wr", [P, 2, NE])
        brb = sb("brb", [P, NE])
        gcol = sb("gcol", [P, 2])
        bcol = sb("bcol", [P, 2])
        epsc = sb("epsc", [P, 2])

        arena_b = sb("arena_b", [P, 2 * NTX * P])
        kT = arena_b[:, 0:NTX * P]
        iota_n = arena_b[:, NTX * P:2 * NTX * P]
        w1s = arena_b[:, 0:2048].rearrange("p (e c h) -> p e c h", e=2, c=2)
        w2s = arena_b[:, 2048:4096].rearrange("p (e c d) -> p e c d", e=2, c=4)
        b2b = arena_b[:, 4096:6144].rearrange("p (e d) -> p e d", e=NE)
        b1c = arena_b[:, 6144:6144 + 4 * NE]
        xrows = arena_b[:, 6400:6400 + 2 * MROW].rearrange("p (k r) -> p k r", k=2)
        xT = arena_b[:, 7000:7512].rearrange("p (c n) -> p c n", c=2)
        hT = arena_b[:, 7600:8624].rearrange("p (m n) -> p m n", m=4)
        ybuf = arena_b[:, 8700:9212].rearrange("p (k d) -> p k d", k=2)
        ysum = arena_b[:, 9300:9812].rearrange("p (k d) -> p k d", k=2)

        arena_a = sb("arena_a", [P, 12750])
        xlr = arena_a[:, 0:2 * CH * W1COLS].rearrange("p (b u d) -> p b u d", b=2, u=CH)
        prod = arena_a[:, 3600:3600 + NT * S].rearrange("p (t s) -> p t s", t=NT)
        qk_all = arena_a[:, 4900:4900 + NT * 2 * S].rearrange("p (t s) -> p t s", t=NT)
        q_all = arena_a[:, 7400:7400 + NT * S].rearrange("p (t s) -> p t s", t=NT)
        rawf = arena_a[:, 8650:8650 + 2048].rearrange("p (k n) -> p k n", k=2)
        raw_i = arena_a[:, 10700:10700 + 2048].bitcast(I32).rearrange("p (k n) -> p k n", k=2)
        xg = arena_a[:, 0:XSLOTS * G * ROW].rearrange("p (n r) -> p n r", r=ROW)
        xr = arena_a[:, 0:2 * CH * D].rearrange("p (b u d) -> p b u d", b=2, u=CH)
        rows = arena_a[:, 3600:3600 + 2 * CH * MROW].rearrange("p (b u r) -> p b u r", b=2, u=CH)
        xnT = arena_a[:, 7300:7300 + 2 * D].rearrange("p (b c n) -> p b c n", b=2, c=2)

        xlT = sb("xlT", [P, 2, 2, P])
        st = sb("st", [P, 2, CH, 6])
        mv = sb("mv", [P, 2, CH, 2])
        lnv = sb("lnv", [P, 2, CH])
        rstd = sb("rstd", [P, 2, CH])
        gmax = sb("gmax", [P, 2])
        gmin = sb("gmin", [P, 2])
        ghl = sb("ghl", [P, 2, 2], I32)
        ghf = sb("ghf", [P, 2, 2])
        cntb = sb("cntb", [P, 2, NG])
        incl = sb("incl", [P, NG])
        basef = sb("basef", [P, NG])
        delta = sb("delta", [P, NG])
        stepw = sb("stepw", [P, NG])
        gsel = sb("gsel", [P, NG])
        diag = sb("diag", [P, 4, GP])
        icode = sb("icode", [P, ICOLS])
        ivalid = sb("ivalid", [P, ICOLS])
        ilist = sb("ilist", [ICOLS, P], I16)
        incl_i = sb("incl_i", [1, NG + 3], I32)
        idx = sb("idx", [P, ISLOTS, G], I32)
        kts = sb("kts", [S, P])
        qs = sb("qs", [P, G, S])
        qT = sb("qT", [S, GE])
        mask = sb("mask", [P, G, P], BF16)
        prob = sb("prob", [P, GE])
        probT = sb("probT", [P, GE])
        mx = sb("mx", [P, 1])
        mnew = sb("mnew", [P, 1])
        nbias = sb("nbias", [P, 1])
        mdiff = sb("mdiff", [P, 1])
        alpha = sb("alpha", [P, 1])
        rl = sb("rl", [P, CH])
        lg = sb("lg", [P, CH, NE])
        top = sb("top", [P, CH, NE])
        topi = sb("topi", [P, CH, NE], U32)
        idxf = sb("idxf", [P, CH, 2])
        oh = sb("oh", [P, 2, CH, NE])
        asg = sb("asg", [P, CH + 1, NE])
        tdiff = sb("tdiff", [P, CH])
        ex = sb("ex", [P, CH])
        den2 = sb("den2", [P, CH])
        w0 = sb("w0", [P, CH])
        ebase = sb("ebase", [P, NE])
        slotv = sb("slotv", [P, CH, NE])
        slotp = sb("slotp", [P, 2, CH, NE])
        slotf = sb("slotf", [P, 2, CH])
        slots = sb("slots", [P, 2, 2, CH], I32)
        cnt_i = sb("cnt_i", [1, NE], I32)
        nst_i = sb("nst_i", [1, NE], I32)
        nst_f = sb("nst_f", [1, NE])
        zero8 = sb("zero8", [1, NE])
        eend_f = sb("eend_f", [1, NE])
        eend = sb("eend", [1, NE + 1], I32)
        metaA = sb("metaA", [P, 2, 4])
        wsel = sb("wsel", [P, 2])
        weq = sb("weq", [P, 2])
        wtok = sb("wtok", [P, 2])
        tokB = sb("tokB", [P, 2], I32)
        b1e = sb("b1e", [P, 4])

        pb = [ctx.enter_context(nc.psum_tensor(f"pb{i}", [P, 512], F32)) for i in range(8)]

        hidden_bank = [pb[1], pb[2], pb[5], pb[6]]

        s_cst = sem("s_cst"); s_zero = sem("s_zero"); s_wl = sem("s_wl"); s_x = sem("s_x"); s_edge = sem("s_edge")
        s_id = sem("s_id"); s_iota = sem("s_iota"); s_grpd = sem("s_grpd"); s_gs = sem("s_gs"); s_ci = sem("s_ci"); s_rawf = sem("s_rawf"); s_et = sem("s_et"); s_ec = sem("s_ec"); s_eng0 = sem("s_eng0")
        s_v0 = sem("s_v0"); s_grp = sem("s_grp"); s_grpb = sem("s_grpb"); s_iw = sem("s_iw"); s_ir = sem("s_ir")
        s_st = sem("s_st"); s_mv = sem("s_mv"); s_ln = sem("s_ln"); s_rs = sem("s_rs"); s_xl = sem("s_xl")
        s_accw = sem("s_accw"); s_tp = sem("s_tp"); s_ev = sem("s_ev"); s_qk = sem("s_qk"); s_kt = sem("s_kt")
        s_qks = sem("s_qks"); s_q = sem("s_q"); s_m0 = sem("s_m0"); s_rw = sem("s_rw"); s_code = sem("s_code"); s_it = sem("s_it")
        s_idx = [sem(f"s_idx{i}") for i in range(ISLOTS)]
        s_g = [sem(f"s_g{i}") for i in range(XSLOTS)]
        xg_free = sem("xg_free"); xg_ready = sem("xg_ready")
        s_qs = sem("s_qs"); s_qt = sem("s_qt"); s_qTs = sem("s_qTs"); s_kts = sem("s_kts"); s_mask = sem("s_mask")
        s_sc = sem("s_sc"); s_mx = sem("s_mx"); s_mn = sem("s_mn"); s_nb = sem("s_nb"); s_md = sem("s_md")
        s_ms = sem("s_ms"); s_p = sem("s_p"); s_al = sem("s_al"); s_pt = sem("s_pt"); s_pts = sem("s_pts")
        s_pv = sem("s_pv"); s_acc = sem("s_acc")
        tk_v = sem("tk_v"); tk_a = sem("tk_a"); tk_p = sem("tk_p"); tk_g = sem("tk_g"); tk_s = sem("tk_s")
        a_x = [sem(f"a_x{i}") for i in range(2)]
        a_o = [sem(f"a_o{i}") for i in range(2)]
        a_v = sem("a_v"); a_x2 = sem("a_x2"); a_rl = sem("a_rl"); a_st = sem("a_st"); a_mv = sem("a_mv"); a_ln = sem("a_ln"); a_rs = sem("a_rs")
        a_xn = sem("a_xn"); a_tp = sem("a_tp"); a_ev = sem("a_ev"); a_lg = sem("a_lg"); a_df = sem("a_df")
        a_ex = sem("a_ex"); a_as = sem("a_as"); a_pos = sem("a_pos"); a_slot = sem("a_slot"); a_sc = sem("a_sc")
        a_free = sem("a_free"); a_cnt = sem("a_cnt"); a_tail = sem("a_tail")
        b_w = [sem(f"b_w{i}") for i in range(2)]
        b_c = sem("b_c"); b_v = sem("b_v"); b_rl = sem("b_rl"); b_eq = sem("b_eq"); b_ws = sem("b_ws"); b_tl = sem("b_tl"); b_tok = sem("b_tok"); b_b1 = sem("b_b1"); b_xt = sem("b_xt"); b_xe = sem("b_xe")
        b_h = sem("b_h"); b_g = sem("b_g"); b_y = sem("b_y"); b_meta = sem("b_meta"); b_lat = sem("b_lat")
        b_ys = sem("b_ys"); b_yb = sem("b_yb"); b_sc = sem("b_sc"); b_t = sem("b_t")

        block = ctx.enter_context(nc.Block())

        def col(ap, i, n=1):
            return ap[:, bass.ds(i, n)]

        item_words = item_row[:, :].bitcast(I32)

        def kept(eng, value, low, high):
            return eng.snap(eng.to_reg(value), donate=True, min_val=low, max_val=high)

        def item_reader(eng, k):
            words, known = {}, {}

            def field(j, shift, bits, high, scale=1):
                w = j // 2
                if w not in words:
                    words[w] = eng.value_load(item_words[0:1, bass.ds(k * 2 + w, 1)], min_val=0, max_val=2 ** 30 - 1)
                if (j, shift, bits) not in known:
                    value = (words[w] >> (16 * (j % 2) + shift)) & bits
                    known[j, shift, bits] = kept(eng, value * scale if scale > 1 else value, 0, high * scale)
                return known[j, shift, bits]

            return (lambda j: field(j, 0, TBITS - 1, NULL_T), lambda j: field(j, 6, 255, NG - 1),
                    lambda j: field(j, 6, XSLOTS - 1, XSLOTS - 1, scale=G))

        def quad_count(eng):
            return eng.value_load(incl_i[0:1, NG:NG + 1], min_val=NG // 4, max_val=NG * NT // 4)

        def last_quad(eng):
            return eng.value_load(incl_i[0:1, NG + 1:NG + 2], min_val=NG // 4 - 1, max_val=NG * NT // 4)

        def counts(eng, k):
            return [4 * k + j if isinstance(k, int) else eng.to_reg(k * 4 + j) for j in range(6)]

        def expert_ends(eng, e):
            lo = eng.value_load(eend[0:1, bass.ds(e, 1)], min_val=0, max_val=NE * 25)
            hi = eng.value_load(eend[0:1, bass.ds(e + 1, 1)], min_val=1, max_val=NE * 25)
            return lo, hi

        def x_tiles(ap, lo, n):
            return ap[bass.ds(lo, n * P), :].rearrange("(t p) d -> p t d", p=P)

        @block.sync
        def _(sp):
            for o, i in ((wqk[:, :, 0:S], Wq.rearrange("(c p) s -> p c s", p=P)),
                         (wqk[:, :, S:2 * S], Wk.rearrange("(c p) s -> p c s", p=P)),
                         (bqk[:, 0:S], bq.partition_broadcast(P)),
                         (bqk[:, S:2 * S], bk.partition_broadcast(P)),
                         (bkcol[:, :], bk.rearrange("(s o) -> s o", o=1)),
                         (wr[:, :, :], Wr.rearrange("(c p) e -> p c e", p=P)),
                         (brb[:, :], br.partition_broadcast(P)),
                         (gcol[:, :], gamma.rearrange("(c p) -> p c", p=P)),
                         (bcol[:, :], beta.rearrange("(c p) -> p c", p=P))):
                sp.dma_start(o, i).then_inc(s_wl, 16)
            sp.wait_ge(s_zero, 3)
            for k, e in enumerate((src, dst)):
                sp.dma_start(raw_i[0:FULLP, k, :],
                             e[0:FULLP * 2 * GE].rearrange("(p n) -> p n", p=FULLP)).then_inc(s_edge, 16)
                sp.dma_start(raw_i[FULLP:FULLP + 1, k, 0:RESTE],
                             e[FULLP * 2 * GE:E_IN].rearrange("(p n) -> p n", p=1)).then_inc(s_edge, 16)
            for c in range(NCH - 1):
                sp.dma_start(acc[:, c * CH:(c + 1) * CH, 0:D], x_tiles(x, c * CHROWS, CH)).then_inc(s_x, 16)
            sp.dma_start(acc[:, NT - CH:NT - 1, 0:D], x_tiles(x, (NT - CH) * P, CH - 1)).then_inc(s_x, 16)
            sp.dma_start(acc[0:LAST, NT - 1, 0:D], x[(NT - 1) * P:N, :]).then_inc(s_x, 16)
            sp.wait_ge(s_code, 1)
            sp.dma_start(item_dram.rearrange("(c p) -> c p", p=P), ilist[:, :]).then_inc(s_iw, 16)
            sp.wait_ge(s_iw, 16)
            sp.dma_start(item_row[:, :], item_dram.rearrange("(o n) -> o n", o=1)).then_inc(s_ir, 16)
            with sp.Fori(0, NCH - 1) as c:
                sp.wait_ge(s_accw, c + 3)
                sp.dma_start(rows_dram[bass.ds(c * CHROWS, CHROWS), 0:W1COLS].rearrange("(t p) d -> p t d", p=P),
                             acc[:, bass.ds(c * CH, CH), :]).then_inc(s_rw, 16)
            sp.wait_ge(s_accw, 2 + NCH)
            sp.dma_start(rows_dram[(NT - CH) * P:NT * P, 0:W1COLS].rearrange("(t p) d -> p t d", p=P),
                         acc[:, NT - CH:NT, :]).then_inc(s_rw, 16)
            sp.wait_ge(s_q, 1)
            sp.dma_start(rows_dram[:, W1COLS:ROW].rearrange("(t p) s -> p t s", p=P), q_all[:, :, :]).then_inc(s_rw, 16)

            sp.wait_ge(s_ec, 4)
            for v in range(AHEAD):
                sp.dma_start(idx[:, v, :], srccol[:, v, :]).then_inc(s_idx[v], 16)

            def give_back(g, v):
                done = sp.value_load(incl_i[0:1, bass.ds(g, 1)], min_val=1, max_val=NG * NT)
                sp.wait_ge(s_pv, done)
                sp.sem_inc(xg_free, 1)
                sp.dma_start(idx[:, (v + AHEAD) % ISLOTS, :], srccol[:, bass.ds(g + AHEAD, 1), :].rearrange("p o g -> p (o g)"))\
                    .then_inc(s_idx[(v + AHEAD) % ISLOTS], 16)

            sp.wait_ge(s_m0, 1)
            with sp.Fori(0, NG // ISLOTS - 1) as k:
                for v in range(ISLOTS):
                    give_back(k * ISLOTS + v, v)

            n_items = kept(sp, quad_count(sp) * 4, NG, ITEMS)
            sp.wait_ge(s_acc, n_items + 1)
            sp.sem_inc(tk_s, 1)
            sp.wait_ge(s_qs, n_items + 2)
            sp.sem_inc(tk_s, 1)

            def load_x(c, b, last=False):
                if not last:
                    sp.dma_start(xr[:, b, :, :], x_tiles(x, c * CHROWS, CH)).then_inc(a_x[b], 16)
                else:
                    sp.dma_start(xr[:, b, 0:CH - 1, :], x_tiles(x, c * CHROWS, CH - 1)).then_inc(a_x[b], 16)
                    sp.dma_start(xr[0:LAST, b, CH - 1, :], x[(NT - 1) * P:N, :]).then_inc(a_x[b], 16)

            def store_x2(c, b, k, last=False):
                sp.wait_ge(a_x2, CH * (c + 1))
                if not last:
                    sp.dma_start(x_tiles(out, c * CHROWS, CH), xr[:, b, :, :]).then_inc(a_o[b], 16)
                else:
                    sp.dma_start(x_tiles(out, c * CHROWS, CH - 1), xr[:, b, 0:CH - 1, :]).then_inc(a_o[b], 16)
                    sp.dma_start(out[(NT - 1) * P:N, :], xr[0:LAST, b, CH - 1, :]).then_inc(a_o[b], 16)

            for k in range(2):
                sp.dma_start(out[N + k * P:N + (k + 1) * P, :], tail[:, k, 0:D]).then_inc(a_tail, 16)
            sp.dma_start(b2b[:, :, :].rearrange("p e d -> p (e d)"),
                         b2.rearrange("e d -> (e d)").partition_broadcast(P)).then_inc(a_tail, 16)
            for e in range(NE):
                sp.dma_start(b1c[:, 4 * e:4 * e + 4], b1[e, :].rearrange("(m p) -> p m", p=P)).then_inc(a_tail, 16)
            load_x(0, 0)
            load_x(1, 1)
            with sp.Fori(0, 2) as k:
                for b in range(2):
                    store_x2(2 * k + b, b, k)
                    sp.wait_ge(a_o[b], 16 * (k + 1))
                    sp.sem_inc(tk_s, 1)
                    sp.wait_ge(a_xn, CH * (2 * k + b) + CH)
                    sp.sem_inc(tk_s, 1)
                    load_x(2 * k + b + 2, b)
            store_x2(4, 0, 2)
            sp.wait_ge(a_o[0], 16 * 3)
            sp.wait_ge(a_xn, CH * 5)
            load_x(6, 0, last=True)
            store_x2(5, 1, 2)
            store_x2(6, 0, 3, last=True)

            sp.wait_ge(a_cnt, 2)
            with sp.Fori(0, NE) as e:
                cnt = sp.value_load(cnt_i[0:1, bass.ds(e, 1)], min_val=0, max_val=N)
                for k in range(2):
                    sp.dma_start(xe_dram[bass.ds(e * CAP + cnt + k * P, P), :], tail[:, k, :]).then_inc(a_tail, 16)
            sp.wait_ge(a_tail, 16 * (3 + NE + 2 * NE))
            sp.wait_ge(a_free, 2 + NCH)
            sp.wait_ge(b_c, 1)
            with sp.Fori(0, NE) as e:
                lo, hi = expert_ends(sp, e)
                first = sp.snap(e * CAP - lo * ST)
                with sp.Fori(lo, hi) as i:
                    sp.wait_ge(b_xt, i)
                    sp.wait_ge(b_meta, i)
                    sp.sem_inc(tk_s, 1)
                    row = (first + i * ST).with_bounds(min_val=0, max_val=XE_ROWS - ST)
                    sp.dma_start(xrows[:, :, :], xe_dram[bass.ds(row, ST), :]
                                 .rearrange("(k p) r -> p k r", p=P)).then_inc(b_rl, 16)
            hi = sp.value_load(eend[0:1, NE:NE + 1], min_val=1, max_val=NE * 25)
            sp.wait_ge(b_xt, hi)
            sp.wait_ge(b_meta, hi)
            sp.sem_inc(tk_s, 1)
            sp.dma_start(xrows[:, :, :], xe_dram[0:ST, :].rearrange("(k p) r -> p k r", p=P)).then_inc(b_rl, 16)
            sp.wait_ge(b_rl, hi * 16 + 16)
            sp.sem_inc(tk_s, 1)
            sp.wait_ge(b_t, hi + 1)
            sp.sem_inc(tk_s, 1)

        @block.gpsimd
        def _(g):
            def cst(ins):
                ins.then_inc(s_cst, 1)

            cst(g.memset(ident[:, :], 0.0))
            cst(g.memset(pen[:, :], 0.0))
            cst(g.memset(ones[:, :], 1.0))
            cst(g.memset(tri[:, :], 1.0))
            cst(g.memset(vmask[:, :], 1.0))
            cst(g.memset(tail[:, :, :], 0.0))
            g.wait_ge(s_cst, 6)
            g.affine_select(out=ident[:, :], in_=ident[:, :], compare_op=ALU.not_equal, fill=1.0, base=0,
                            pattern=[[-1, P]], channel_multiplier=1).then_inc(s_id, 1)
            g.affine_select(out=pen[:, :], in_=pen[:, :], compare_op=ALU.not_equal, fill=-BIG, base=0,
                            pattern=[[-1, P]], channel_multiplier=1).then_inc(s_id, 1)
            g.affine_select(out=tri[:, :], in_=tri[:, :], compare_op=ALU.is_gt, fill=0.0, base=0,
                            pattern=[[1, P]], channel_multiplier=-1).then_inc(s_id, 1)
            g.affine_select(out=vmask[:, :], in_=vmask[:, :], compare_op=ALU.is_ge, fill=0.0, base=LAST - 1,
                            pattern=[[0, 1]], channel_multiplier=-1).then_inc(s_id, 1)
            g.iota(tail[:, :, D:D + 1], [[P, 2]], base=N, channel_multiplier=1,
                   allow_small_or_imprecise_dtypes=True).then_inc(s_id, 1)
            g.memset(tail[:, :, D + 3:D + 4], -1.0).then_inc(s_id, 1)
            g.iota(itemidx[:, :], [[P, ICOLS]], base=0, channel_multiplier=1,
                   allow_small_or_imprecise_dtypes=True).then_inc(s_id, 1)
            g.iota(iota8[:, :], [[1, NE]], base=0, channel_multiplier=0,
                   allow_small_or_imprecise_dtypes=True).then_inc(s_id, 1)
            g.iota(ecap[:, :], [[CAP, NE]], base=0, channel_multiplier=0,
                   allow_small_or_imprecise_dtypes=True).then_inc(s_id, 1)
            g.iota(tok[:, :], [[P, NT]], base=0, channel_multiplier=1,
                   allow_small_or_imprecise_dtypes=True).then_inc(s_id, 1)
            g.memset(kT[:, NT * P:NTX * P], 0.0).then_inc(s_id, 1)
            g.memset(acc[:, NULL_T, :], 0.0).then_inc(s_id, 1)
            g.memset(m_all[:, NULL_T:NTX], 0.0).then_inc(s_id, 1)
            g.iota(iota_n, [[1, NTX * P]], base=0, channel_multiplier=0,
                   allow_small_or_imprecise_dtypes=True).then_inc(s_iota, 1)
            g.sem_inc(s_accw, 2)

            def keep(c, b):
                g.wait_ge(s_xl, CH * (c + 1))
                g.sem_inc(tk_g, 1)
                g.tensor_copy(acc[:, bass.ds(c * CH, CH), :], xlr[:, b, :, :]).then_inc(s_accw, 1)

            with g.Fori(0, NCH // 2) as k:
                for b in range(2):
                    keep(2 * k + b, b)
            keep(NCH - 1, 0)

            g.wait_ge(s_rw, 16 * (NCH + 1))
            g.wait_ge(s_m0, 1)
            g.sem_inc(xg_free, XSLOTS)

            def gather(k, v, first=False):
                gr = k * ISLOTS + v
                slot = v % XSLOTS
                g.wait_ge(s_idx[v], 16 * (k + 1))
                g.wait_ge(xg_free, gr + 1)
                g.sem_inc(tk_g, 1)
                for j in range(G):
                    g.indirect_dma_start(
                        out=xg[:, slot * G + j, :], out_offset=None, in_=rows_dram[:, :],
                        in_offset=bass.IndirectOffsetOnAxis(ap=idx[:, v, j:j + 1], axis=0)).then_inc(s_g[slot], 16)
                if not first:
                    landed = ISLOTS // XSLOTS * k + (v - 1) // XSLOTS + 1
                    g.wait_ge(s_g[(v - 1) % XSLOTS], 16 * G * landed)
                    g.sem_inc(xg_ready, 1)

            for v in range(ISLOTS):
                gather(0, v, first=v == 0)
            with g.Fori(1, NG // ISLOTS) as k:
                for v in range(ISLOTS):
                    gather(k, v)
            g.wait_ge(s_g[XSLOTS - 1], 16 * G * (NG // XSLOTS))
            g.sem_inc(xg_ready, 1)

            def load_w(e, b):
                g.dma_start(w1s[:, b, :, :], W1[bass.ds(e, 1), :, :].rearrange("o (c p) h -> p (o c) h", p=P)).then_inc(b_w[b], 16)
                g.dma_start(w2s[:, b, :, :], W2[bass.ds(e, 1), :, :].rearrange("o (c p) d -> p (o c) d", p=P)).then_inc(b_w[b], 16)

            n_items = kept(g, quad_count(g) * 4, NG, ITEMS)
            g.wait_ge(s_acc, n_items + 1)
            g.sem_inc(tk_g, 1)
            load_w(0, 0)
            load_w(1, 1)

            def scatter(c, b, k, last=False):
                g.wait_ge(a_slot, c + 1)
                g.sem_inc(tk_g, 1)
                for u in range(CH):
                    n = LAST if last and u == CH - 1 else P
                    for r in range(2):
                        g.indirect_dma_start(
                            out=xe_dram[:, :], in_=rows[0:n, b, u, :], in_offset=None,
                            out_offset=bass.IndirectOffsetOnAxis(ap=slots[0:n, b, r, u:u + 1], axis=0))\
                            .then_inc(a_sc, 16)
                g.wait_ge(a_sc, 16 * 2 * CH * (c + 1))
                g.sem_inc(a_free, 1)

            with g.Fori(0, NCH // 2) as k:
                for b in range(2):
                    scatter(2 * k + b, b, k)
            scatter(NCH - 1, 0, NCH // 2, last=True)

            g.wait_ge(a_o[0], 16 * 5)
            g.wait_ge(a_o[1], 16 * 3)
            g.wait_ge(a_tail, 16 * (3 + NE + 2 * NE))
            g.wait_ge(b_c, 1)

            def add_rows(e):
                lo, hi = expert_ends(g, e)
                with g.Fori(lo, hi) as i:
                    for k in range(2):
                        g.wait_ge(b_yb, i * 2 + k + 1)
                        g.sem_inc(tk_g, 1)
                        g.indirect_dma_start(
                            out=out[:, :], in_=ybuf[:, k, :], in_offset=None,
                            out_offset=bass.IndirectOffsetOnAxis(ap=tokB[:, k:k + 1], axis=0),
                            compute_op=ALU.add).then_inc(b_sc, 16)
                        g.wait_ge(b_sc, i * 32 + 16 * (k + 1))
                        g.sem_inc(b_t if k else tk_g, 1)

            add_rows(0)
            with g.Fori(0, NE // 2 - 1) as k:
                for b in range(2):
                    load_w(2 * k + 2 + b, b)
                    add_rows(2 * k + 1 + b)
            add_rows(NE - 1)

        @block.vector
        def _(v):
            v.memset(acc[96:P, NT - 1, 0:D], 0.0).then_inc(s_zero, 1)
            v.memset(raw_i[96:P, 0, :], 0).then_inc(s_zero, 1)
            v.memset(raw_i[96:P, 1, :], PAD_DST).then_inc(s_zero, 1)
            v.memset(xlr[:, :, :, D:W1COLS], 1.0).then_inc(s_v0, 1)
            v.memset(epsc[:, 0:1], EPS).then_inc(s_v0, 1)
            v.memset(epsc[:, 1:2], EPS * EPS).then_inc(s_v0, 1)
            v.memset(zero8[:, :], 0.0).then_inc(s_v0, 1)
            v.memset(asg[:, :, :], 0.0).then_inc(s_v0, 1)
            v.memset(eend[:, :], 0).then_inc(s_v0, 1)
            v.sem_inc(s_qks, 2)
            v.sem_inc(s_acc, 1)
            v.memset(stepw[:, :], 0.0).then_inc(s_v0, 1)
            v.memset(icode[:, :], 0.0).then_inc(s_v0, 1)
            v.wait_ge(s_edge, 64)
            for k in range(2):
                v.tensor_copy(rawf[0:GP, k, :], raw_i[0:GP, k, :]).then_inc(s_rawf, 1)
            v.wait_ge(s_rawf, 2)
            dg = rawf[0:GP, 1, :].rearrange("p (h n) -> p h n", h=2)
            v.tensor_reduce(gmin[0:GP, :], dg, axis=X_AXIS, op=ALU.min).then_inc(s_eng0, 1)
            v.tensor_reduce(gmax[0:GP, :], dg, axis=X_AXIS, op=ALU.max).then_inc(s_eng0, 1)
            v.wait_ge(s_eng0, 2)
            v.tensor_copy(ghl[0:GP, 0, :], gmax[0:GP, :]).then_inc(s_eng0, 1)
            v.tensor_copy(ghl[0:GP, 1, :], gmin[0:GP, :]).then_inc(s_eng0, 1)
            v.wait_ge(s_eng0, 4)
            v.tensor_scalar(ghl[0:GP, :, :], ghl[0:GP, :, :], 7, None, ALU.arith_shift_right).then_inc(s_eng0, 1)
            v.wait_ge(s_eng0, 5)
            v.tensor_copy(ghf[0:GP, 1, :], ghl[0:GP, 1, :]).then_inc(s_eng0, 1)
            v.tensor_tensor(ghf[0:GP, 0, :], ghl[0:GP, 0, :], ghl[0:GP, 1, :], ALU.subtract).then_inc(s_eng0, 1)
            v.wait_ge(s_eng0, 7)
            v.tensor_scalar(ghf[0:GP, 0, :], ghf[0:GP, 0, :], 1.0, None, ALU.add).then_inc(s_grp, 1)
            v.wait_ge(s_grp, 1)
            v.wait_ge(s_id, 13)
            for k in range(2):
                for h in range(2):
                    v.tensor_scalar(diag[0:GP, 2 * k + h, :], ident[0:GP, 0:GP], ghf[0:GP, k, h:h + 1], None, ALU.mult)\
                        .then_inc(s_grpd, 1)
            for h in range(2):
                for k, o in ((0, srccol), (1, dstcol)):
                    v.wait_ge(s_et, 2 * h + k + 1)
                    v.tensor_copy(o[:, h:NG:2, :].rearrange("p q j -> p j q"),
                                  pb[6 + k][:, 0:G * GP].rearrange("p (j q) -> p j q", j=G)).then_inc(s_ec, 1)
            v.wait_ge(s_grpb, 1)
            v.wait_ge(s_v0, 8)
            for k in range(2):
                v.tensor_copy(cntb[:, k, :].rearrange("p (q h) -> p h q", h=2),
                              pb[0][:, k * 2 * GP:(k + 1) * 2 * GP].rearrange("p (h q) -> p h q", h=2)).then_inc(s_grpd, 1)
            v.wait_ge(s_grpd, 6)
            v.tensor_tensor_scan(incl[:, :], cntb[:, 0, :], stepw[:, :], 0.0, ALU.add, ALU.add).then_inc(s_eng0, 1)
            v.wait_ge(s_eng0, 8)
            v.tensor_tensor(basef[:, :], incl[:, :], cntb[:, 0, :], ALU.subtract).then_inc(s_eng0, 1)
            v.tensor_copy(incl_i[:, 0:NG], incl[0:1, :]).then_inc(s_eng0, 1)
            for o, more in ((NG, 3), (NG + 2, P + 4)):
                v.tensor_scalar(incl_i[:, o:o + 1], incl[0:1, NG - 1:NG], float(more), None, ALU.add).then_inc(s_ci, 1)
            v.wait_ge(s_ci, 2)
            for o, shift in ((NG, 2), (NG + 2, 7)):
                v.tensor_scalar(incl_i[:, o:o + 1], incl_i[:, o:o + 1], shift, None, ALU.arith_shift_right).then_inc(s_ci, 1)
            v.wait_ge(s_ci, 4)
            v.tensor_scalar(incl_i[:, NG + 1:NG + 2], incl_i[:, NG:NG + 1], -1.0, None, ALU.add).then_inc(s_ci, 1)
            v.wait_ge(s_eng0, 10)
            v.tensor_tensor(delta[:, :], cntb[:, 1, :], basef[:, :], ALU.subtract).then_inc(s_eng0, 1)
            v.wait_ge(s_eng0, 11)
            v.tensor_scalar(stepw[:, 0:1], delta[:, 0:1], 1.0, float(TBITS), ALU.mult, ALU.add).then_inc(s_eng0, 1)
            v.tensor_tensor(stepw[:, 1:NG], delta[:, 1:NG], delta[:, 0:NG - 1], ALU.subtract).then_inc(s_eng0, 1)
            v.wait_ge(s_eng0, 13)
            v.tensor_scalar(stepw[:, 1:NG], stepw[:, 1:NG], float(TBITS), None, ALU.add).then_inc(s_eng0, 1)
            v.wait_ge(s_eng0, 14)
            v.wait_ge(s_ci, 5)
            v.sem_inc(s_gs, 1)
            columns = v.value_load(incl_i[0:1, NG + 2:NG + 3], min_val=1, max_val=ICOLS)
            with v.Fori(0, columns) as c:
                free = v.to_reg(c + 1)
                v.scalar_tensor_tensor(out=gsel[:, :], in0=basef[:, :], scalar=col(itemidx, c), in1=stepw[:, :],
                                       op0=ALU.is_le, op1=ALU.mult, accum_out=col(icode, c))\
                    .wait_op(s_gs, free, AT_LEAST).then_inc(s_gs, 1)
            v.wait_ge(s_gs, columns + 1)
            v.sem_inc(tk_v, 1)
            v.tensor_tensor(icode[:, :], icode[:, :], itemidx[:, :], ALU.add).then_inc(s_eng0, 1)
            v.tensor_scalar(ivalid[:, :], itemidx[:, :], incl[:, NG - 1:NG], None, ALU.is_lt).then_inc(s_eng0, 1)
            null = float(NULL_T + TBITS * (NG - 1))
            v.wait_ge(s_eng0, 16)
            v.tensor_scalar(icode[:, :], icode[:, :], -float(TBITS) - null, None, ALU.add).then_inc(s_eng0, 1)
            v.wait_ge(s_eng0, 17)
            v.tensor_tensor(icode[:, :], icode[:, :], ivalid[:, :], ALU.mult).then_inc(s_eng0, 1)
            v.wait_ge(s_it, 1)
            v.tensor_scalar(ilist[:, :], pb[1][0:ICOLS, 0:P], null, None, ALU.add).then_inc(s_code, 1)

            v.wait_ge(s_x, 16 * (NCH + 1))
            v.wait_ge(s_wl, 16 * 9)
            v.wait_ge(s_zero, 3)

            def node_tile(t):
                return acc[:, bass.ds(t, 1), 0:D].rearrange("p o d -> p (o d)")

            def statistics_0(c, b):
                for u in range(CH):
                    v.bn_stats(st[:, b, u, :], node_tile(c * CH + u)).then_inc(s_st, 1)
                v.wait_ge(s_st, CH * (c + 1))
                v.sem_inc(tk_v, 1)
                for u in range(CH):
                    v.bn_aggr(mv[:, b, u, :], st[:, b, u, :]).then_inc(s_mv, 1)

            def normalise_0(c, b):
                v.wait_ge(s_tp, CH * (c + 1))
                v.sem_inc(tk_v, 1)
                v.wait_ge(s_accw, c + 1)
                v.sem_inc(tk_v, 1)
                v.wait_ge(s_rs, c + 1)
                v.sem_inc(tk_v, 1)
                for u in range(CH):
                    v.tensor_scalar(xlr[:, b, u, 0:D], node_tile(c * CH + u), mv[:, b, u, 0:1], rstd[:, b, u:u + 1],
                                    ALU.subtract, ALU.mult).then_inc(s_xl, 1)

            def add_biases(c, b):
                made = CH * c + CH if isinstance(c, int) else v.to_reg(c * CH + CH)
                v.tensor_tensor(qk_all[:, bass.ds(c * CH, CH), :],
                                pb[2 + b][:, 0:CH * 2 * S].rearrange("p (u s) -> p u s", u=CH),
                                bqk[:, :].unsqueeze(1).to_broadcast([P, CH, 2 * S]), ALU.add)\
                    .wait_op(s_qk, made, AT_LEAST).then_inc(s_qks, 1)

            statistics_0(0, 0)
            statistics_0(1, 1)
            normalise_0(0, 0)
            with v.Fori(0, NCH // 2 - 1) as k:
                for b in range(2):
                    c = 2 * k + b
                    statistics_0(c + 2, b)
                    normalise_0(c + 1, 1 - b)
                    add_biases(c, b)
            c = NCH - 3
            statistics_0(c + 2, 0)
            normalise_0(c + 1, 1)
            add_biases(c, 0)
            normalise_0(c + 2, 0)
            add_biases(c + 1, 1)
            add_biases(c + 2, 0)
            v.wait_ge(s_q, 1)
            v.wait_ge(s_qks, 2 + NCH)
            v.tensor_tensor(prod[:, :, :], q_all[:, :, :], qk_all[:, :, S:2 * S], ALU.mult).then_inc(s_eng0, 1)
            v.wait_ge(s_eng0, 19)
            v.wait_ge(s_accw, 2 + NCH)
            v.wait_ge(s_kt, 2 + 2 * NCH)
            v.wait_ge(s_ir, 16)
            v.wait_ge(s_iota, 1)
            v.wait_ge(s_id, 13)
            v.tensor_reduce(m_all[:, 0:NT], prod[:, :, :], axis=X_AXIS, op=ALU.add).then_inc(s_m0, 1)
            v.wait_ge(s_m0, 1)

            def edge_mask(t, gr):
                v.tensor_tensor(mask[:, :, :],
                                iota_n[:, bass.ds(t * P, P)].unsqueeze(1).to_broadcast([P, G, P]),
                                dstcol[:, bass.ds(gr, 1), :].rearrange("p o j -> p (o j)").unsqueeze(2).to_broadcast([P, G, P]),
                                ALU.not_equal).then_inc(s_mask, 1)

            def add_sums(t, done):
                a = acc[:, bass.ds(t, 1), :].rearrange("p o d -> p (o d)")
                v.scalar_tensor_tensor(out=a, in0=a, scalar=alpha[:, :], in1=pb[3][:, 0:W1COLS],
                                       op0=ALU.mult, op1=ALU.add).wait_op(s_pv, done, AT_LEAST).then_inc(s_acc, 1)

            def maximum(tile, i, done):
                v.wait_ge(s_sc, done)
                v.tensor_reduce(mx[:, :], pb[1][:, :], axis=X_AXIS, op=ALU.max).then_inc(s_mx, 1)
                v.tensor_tensor(mnew[:, :], m_all[:, bass.ds(tile(i), 1)], mx[:, :], ALU.max)\
                    .wait_op(s_mx, done, AT_LEAST).then_inc(s_mn, 1)
                v.wait_ge(s_mn, done)
                v.tensor_scalar(nbias[:, :], mnew[:, :], -1.0 / DK, None, ALU.mult).then_inc(s_nb, 1)

            def keep_maximum(t, before, done):
                m = m_all[:, bass.ds(t, 1)]
                ins = v.tensor_tensor(mdiff[:, :], m, mnew[:, :], ALU.subtract)
                if before is not None:
                    ins.wait_op(s_al, before, AT_LEAST)
                ins.then_inc(s_md, 1)
                v.tensor_tensor(m, m, mnew[:, :], ALU.max).wait_op(s_md, done, AT_LEAST).then_inc(s_ms, 1)

            def quad(k):
                cnt = counts(v, k)
                tile, group, _ = item_reader(v, k)
                for i in range(4):
                    first = isinstance(k, int) and i == 0
                    maximum(tile, i, cnt[i + 1])
                    edge_mask(tile(i + 1), group(i + 1))
                    if not first:
                        add_sums(tile(i - 1), cnt[i])
                    keep_maximum(tile(i), None if first else cnt[i], cnt[i + 1])

            n_quads = quad_count(v)
            tile, group, _ = item_reader(v, 0)
            edge_mask(tile(0), group(0))
            quad(0)
            with v.Fori(1, n_quads) as k:
                quad(k)
            n_items = kept(v, n_quads * 4, NG, ITEMS)
            add_sums(item_reader(v, last_quad(v))[0](3), v.to_reg(n_items))

            v.wait_ge(s_acc, n_items + 1)
            v.sem_inc(tk_v, 1)

            def statistics(c, b, loaded):
                t0 = c * CH
                v.reciprocal(rl[:, :], acc[:, bass.ds(t0, CH), D:W1COLS].rearrange("p u o -> p (u o)")).then_inc(a_rl, 1)
                v.wait_ge(a_x[b], loaded)
                v.wait_ge(a_rl, c + 1)
                v.sem_inc(tk_v, 1)
                for u in range(CH):
                    v.scalar_tensor_tensor(out=xr[:, b, u, :], in0=acc[:, bass.ds(t0 + u, 1), 0:D].rearrange("p o d -> p (o d)"),
                                           scalar=rl[:, u:u + 1], in1=xr[:, b, u, :],
                                           op0=ALU.mult, op1=ALU.add).then_inc(a_x2, 1)
                for u in range(CH):
                    v.wait_ge(a_x2, CH * c + u + 1)
                    v.bn_stats(st[:, 0, u, :], xr[:, b, u, :]).then_inc(a_st, 1)
                v.wait_ge(a_st, CH * (c + 1))
                v.sem_inc(tk_v, 1)
                for u in range(CH):
                    v.bn_aggr(mv[:, 0, u, :], st[:, 0, u, :]).then_inc(a_mv, 1)

            def normalise(c, b):
                v.wait_ge(a_free, c + 1)
                v.sem_inc(tk_v, 1)
                v.wait_ge(a_rs, c + 1)
                for u in range(CH):
                    v.tensor_scalar(rows[:, b, u, 0:D], xr[:, b, u, :], mv[:, 0, u, 0:1], rstd[:, 0, u:u + 1],
                                    ALU.subtract, ALU.mult).then_inc(a_xn, 1)

            STEPS = 17

            def route(c, b, last=False):
                n = [0]

                def step(ins):
                    ins.then_inc(a_v, 1)
                    n[0] += 1

                def steps():
                    return c * STEPS + n[0]

                v.wait_ge(a_lg, CH * (c + 1))
                step(v.tensor_tensor(lg[:, :, :], pb[6][:, 64 * b:64 * b + CH * NE].rearrange("p (u e) -> p u e", u=CH),
                                     brb[:, :].unsqueeze(1).to_broadcast([P, CH, NE]), ALU.add))
                v.wait_ge(a_v, steps())
                v.sem_inc(tk_v, 1)
                for u in range(CH):
                    ins = v.max(top[:, u, :], lg[:, u, :])
                step(ins)
                v.wait_ge(a_v, steps())
                v.tensor_tensor(tdiff[:, :], top[:, :, 1], top[:, :, 0], ALU.subtract).then_inc(a_df, 1)
                for u in range(CH):
                    ins = v.max_index(topi[:, u, :], top[:, u, :], lg[:, u, :])
                step(ins)
                v.wait_ge(a_v, steps())
                step(v.tensor_copy(idxf[:, :, :], topi[:, :, 0:2]))
                v.wait_ge(a_v, steps())
                for r in range(2):
                    step(v.tensor_tensor(oh[:, r, :, :], iota8[:, :].unsqueeze(1).to_broadcast([P, CH, NE]),
                                         idxf[:, :, r:r + 1].to_broadcast([P, CH, NE]), ALU.is_equal))
                v.wait_ge(a_v, steps())
                ins = v.tensor_tensor(asg[:, 0:CH, :], oh[:, 0, :, :], oh[:, 1, :, :], ALU.add)
                if last:
                    step(ins)
                    v.wait_ge(a_v, steps())
                    ins = v.tensor_scalar(asg[:, CH - 1, :], asg[:, CH - 1, :], vmask[:, :], None, ALU.mult)
                ins.then_inc(a_as, 1)
                step(v.tensor_copy(rows[:, b, :, D], tok[:, bass.ds(c * CH, CH)]))
                step(v.tensor_copy(rows[:, b, :, D + 3], idxf[:, :, 0]))
                v.wait_ge(a_ex, c + 1)
                step(v.tensor_scalar(den2[:, :], ex[:, :], 1.0, None, ALU.add))
                v.wait_ge(a_v, steps())
                step(v.reciprocal(w0[:, :], den2[:, :]))
                v.wait_ge(a_v, steps())
                step(v.tensor_tensor(rows[:, b, :, D + 1], ex[:, :], w0[:, :], ALU.mult))
                v.wait_ge(a_v, steps())
                step(v.tensor_tensor(rows[:, b, :, D + 2], w0[:, :], rows[:, b, :, D + 1], ALU.subtract))
                ahead = pb[7][:, 64 * b:64 * (b + 1)].rearrange("p (u e) -> p u e", u=CH + 1)
                v.wait_ge(a_pos, c + 1)
                step(v.tensor_tensor(slotv[:, :, :], ahead[:, 0:CH, :],
                                     ebase[:, :].unsqueeze(1).to_broadcast([P, CH, NE]), ALU.add))
                v.wait_ge(a_v, steps())
                step(v.tensor_tensor(ebase[:, :], ebase[:, :], ahead[:, CH, :], ALU.add))
                for r in range(2):
                    step(v.tensor_tensor(slotp[:, r, :, :], oh[:, r, :, :], slotv[:, :, :], ALU.mult))
                v.wait_ge(a_v, steps())
                step(v.tensor_reduce(slotf[:, :, :], slotp[:, :, :, :], axis=X_AXIS, op=ALU.add))
                v.wait_ge(a_v, steps())
                v.tensor_copy(slots[:, b, :, :], slotf[:, :, :]).then_inc(a_slot, 1)
                assert n[0] == STEPS + last, n[0]

            v.sem_inc(a_free, 2)
            v.wait_ge(s_id, 13)
            v.tensor_copy(ebase[:, :], ecap[:, :]).then_inc(a_cnt, 1)
            v.wait_ge(a_cnt, 1)
            statistics(0, 0, 16)
            normalise(0, 0)
            with v.Fori(0, NCH // 2 - 1) as k:
                for b in range(2):
                    statistics(2 * k + b + 1, 1 - b, 16 * (k + 1 + b))
                    route(2 * k + b, b)
                    normalise(2 * k + b + 1, 1 - b)
            for c in range(NCH - 3, NCH - 1):
                statistics(c + 1, 1 - c % 2, 16 * ((c + 1) // 2 + 1) + (16 if c + 1 == NCH - 1 else 0))
                route(c, c % 2)
                normalise(c + 1, 1 - c % 2)
            route(NCH - 1, 0, last=True)

            v.wait_ge(a_slot, NCH)
            v.tensor_tensor(nst_f[:, :], ebase[0:1, :], ecap[0:1, :], ALU.subtract).then_inc(b_v, 1)
            v.wait_ge(b_v, 1)
            v.tensor_copy(cnt_i[:, :], nst_f[:, :]).then_inc(a_cnt, 1)
            v.wait_ge(a_cnt, 2)
            v.tensor_scalar(nst_f[:, :], cnt_i[:, :], float(ST - 1), None, ALU.add).then_inc(b_v, 1)
            v.wait_ge(b_v, 2)
            v.tensor_copy(nst_i[:, :], nst_f[:, :]).then_inc(b_v, 1)
            v.wait_ge(b_v, 3)
            v.tensor_scalar(nst_i[:, :], nst_i[:, :], 8, None, ALU.arith_shift_right).then_inc(b_v, 1)
            v.wait_ge(b_v, 4)
            v.tensor_scalar(nst_f[:, :], nst_i[:, :], 1.0, None, ALU.max).then_inc(b_v, 1)
            v.wait_ge(b_v, 5)
            v.tensor_tensor_scan(eend_f[:, :], nst_f[:, :], zero8[:, :], 0.0, ALU.add, ALU.add).then_inc(b_v, 1)
            v.wait_ge(b_v, 6)
            v.tensor_copy(eend[:, 1:NE + 1], eend_f[:, :]).then_inc(b_c, 1)
            v.wait_ge(b_c, 1)

            def meta(ready):
                v.wait_ge(b_rl, ready)
                v.tensor_copy(metaA[:, :, :], xrows[:, :, D:MROW]).then_inc(b_meta, 1)

            def finish(e, i):
                one = v.to_reg(i + 1)
                halves = [v.to_reg(i * 2 + j) for j in (1, 2)]
                v.scalar_tensor_tensor(out=weq[:, :], in0=metaA[:, :, 3], scalar=iota8[:, bass.ds(e, 1)], in1=metaA[:, :, 2],
                                       op0=ALU.is_equal, op1=ALU.mult).wait_op(b_meta, one, AT_LEAST).then_inc(b_eq, 1)
                v.wait_ge(b_eq, one)
                v.tensor_tensor(wsel[:, :], weq[:, :], metaA[:, :, 1], ALU.add).then_inc(b_ws, 1)
                v.tensor_copy(wtok[:, :], metaA[:, :, 0]).then_inc(b_tl, 1)
                v.wait_ge(b_tl, one)
                v.sem_inc(tk_v, 1)
                meta(v.to_reg(i * 16 + 32))
                v.wait_ge(b_t, one)
                v.tensor_copy(tokB[:, :], wtok[:, :]).then_inc(b_tok, 1)
                for k in range(2):
                    ins = v.tensor_tensor(ysum[:, k, :], pb[3 + k][:, 0:D],
                                          b2b[:, bass.ds(e, 1), :].rearrange("p o d -> p (o d)"), ALU.add)
                    if k == 0:
                        ins.wait_op(b_y, one, AT_LEAST)
                    ins.then_inc(b_ys, 1)
                for k in range(2):
                    v.wait_ge(b_ys, halves[k])
                    v.tensor_scalar(ybuf[:, k, :], ysum[:, k, :], wsel[:, k:k + 1], None, ALU.mult).then_inc(b_yb, 1)

            v.wait_ge(a_tail, 16 * (3 + NE + 2 * NE))
            v.sem_inc(b_t, 1)
            meta(16)
            with v.Fori(0, NE) as e:
                lo, hi = expert_ends(v, e)
                with v.Fori(lo, hi) as i:
                    finish(e, i)

        @block.scalar
        def _(a):
            a.preload_act_table_set("natural_log_exp_and_others")
            a.sem_inc(s_kt, 2)
            a.wait_ge(s_wl, 16 * 9)
            a.wait_ge(s_v0, 8)

            def inverse_std(c, b):
                a.wait_ge(s_mv, CH * (c + 1))
                nc.scalar.activation(lnv[:, b, :], mv[:, b, :, 1], ACT.Ln, bias=epsc[:, 0:1]).then_inc(s_ln, 1)
                a.wait_ge(s_ln, c + 1)
                nc.scalar.activation(rstd[:, b, :], lnv[:, b, :], ACT.Exp, scale=-0.5).then_inc(s_rs, 1)

            def copy_keys(c, lo, n, bank):
                a.wait_ge(s_qk, CH * c + lo + n)
                a.sem_inc(tk_a, 1)
                nc.scalar.activation(kT[0:S, bass.ds((c * CH + lo) * P, n * P)], bank[0:S, 0:n * P], ACT.Identity,
                                     bias=bkcol[:, :]).then_inc(s_kt, 1)

            def chunk_0(c, b, last=False):
                if not last:
                    inverse_std(c + 1, 1 - b)
                for u in range(CH):
                    a.wait_ge(s_tp, 2 * CH + c * CH + u + 1)
                    nc.scalar.copy(xlT[:, (7 * b + u) % 2, :, :].rearrange("p c n -> p (c n)"),
                                   pb[(7 * b + u) % 2][:, 0:D]).then_inc(s_ev, 1)
                    if u == CH - 2:
                        copy_keys(c, 0, 4, pb[4])
                copy_keys(c, 4, CH - 4, pb[5])

            inverse_std(0, 0)
            with a.Fori(0, NCH // 2) as k:
                for b in range(2):
                    chunk_0(2 * k + b, b)
            chunk_0(NCH - 1, 0, last=True)
            a.wait_ge(s_qks, 2 + NCH)
            nc.scalar.activation(q_all[:, :, :], qk_all[:, :, 0:S], ACT.Tanh).then_inc(s_q, 1)

            a.wait_ge(s_m0, 1)
            a.wait_ge(s_kt, 2 + 2 * NCH)

            def copy_k(t):
                nc.scalar.copy(kts[:, :], kT[0:S, bass.ds(t * P, P)]).then_inc(s_kts, 1)

            def copy_q(ready, slot):
                a.wait_ge(xg_ready, ready)
                a.sem_inc(tk_a, 1)
                nc.scalar.copy(qs[:, :, :], xg[:, bass.ds(slot, G), W1COLS:ROW]).then_inc(s_qs, 1)

            def copy_qT(ahead):
                a.wait_ge(s_qt, ahead)
                nc.scalar.copy(qT[:, :], pb[0][0:S, :]).then_inc(s_qTs, 1)

            def exponentials(done):
                a.wait_ge(s_nb, done)
                nc.scalar.activation(prob[:, :], pb[1][:, :], ACT.Exp, bias=nbias[:, :], scale=1.0 / DK).then_inc(s_p, 1)

            def scale_and_copy(done):
                a.wait_ge(s_md, done)
                nc.scalar.activation(alpha[:, :], mdiff[:, :], ACT.Exp, scale=1.0 / DK).then_inc(s_al, 1)
                a.wait_ge(s_pt, done)
                nc.scalar.copy(probT[:, :], pb[2][:, :]).then_inc(s_pts, 1)

            def quad(k):
                cnt = counts(a, k)
                tile, group, slot = item_reader(a, k)
                for i in range(4):
                    ready, q_slot = a.to_reg(group(i + 2) + 1), slot(i + 2)
                    copy_qT(cnt[i + 2])
                    copy_k(tile(i + 1))
                    exponentials(cnt[i + 1])
                    scale_and_copy(cnt[i + 1])
                    copy_q(ready, q_slot)

            n_quads = quad_count(a)
            tile, group, slot = item_reader(a, 0)
            copy_q(a.to_reg(group(0) + 1), slot(0))
            copy_qT(1)
            copy_k(tile(0))
            copy_q(a.to_reg(group(1) + 1), slot(1))
            quad(0)
            with a.Fori(1, n_quads) as k:
                quad(k)
            n_items = kept(a, n_quads * 4, NG, ITEMS)

            a.preload_act_table_set("natural_log_exp_and_others")
            a.wait_ge(s_acc, n_items + 1)
            a.sem_inc(tk_a, 1)

            def both_stds(c):
                a.wait_ge(a_mv, CH * (c + 1))
                nc.scalar.activation(lnv[:, 0, :], mv[:, 0, :, 1], ACT.Ln, bias=epsc[:, 1:2], scale=1.0 + EPS).then_inc(a_ln, 1)
                a.wait_ge(a_ln, c + 1)
                nc.scalar.activation(rstd[:, 0, :], lnv[:, 0, :], ACT.Exp, scale=-0.5).then_inc(a_rs, 1)

            def chunk_a(c, b, last=False):
                for u in range(CH):
                    w = (7 * b + u) % 2
                    a.wait_ge(a_tp, c * CH + u + 1)
                    for h in range(2):
                        nc.scalar.activation(xnT[:, w, h, :], pb[4 + w][:, h * P:(h + 1) * P], ACT.Identity,
                                             bias=bcol[:, h:h + 1], scale=gcol[:, h:h + 1]).then_inc(a_ev, 1)
                if not last:
                    both_stds(c + 1)
                a.wait_ge(a_df, c + 1)
                nc.scalar.activation(ex[:, :], tdiff[:, :], ACT.Exp).then_inc(a_ex, 1)

            both_stds(0)
            with a.Fori(0, NCH // 2) as k:
                for b in range(2):
                    chunk_a(2 * k + b, b)
            chunk_a(NCH - 1, 0, last=True)

            a.preload_act_table_set("gelu_and_others")
            a.wait_ge(b_c, 1)
            a.wait_ge(a_tail, 16 * (3 + NE + 2 * NE))

            def xT_copy(ready):
                a.wait_ge(b_xt, ready)
                for h in range(2):
                    nc.scalar.activation(xT[:, h, :], pb[0][:, h * ST:(h + 1) * ST], ACT.Identity,
                                         bias=bcol[:, h:h + 1], scale=gcol[:, h:h + 1]).then_inc(b_xe, 1)

            xT_copy(1)
            with a.Fori(0, NE) as e:
                lo, hi = expert_ends(a, e)
                a.wait_ge(b_g, lo * 4)
                a.sem_inc(tk_a, 1)
                nc.scalar.copy(b1e[:, :], b1c[:, bass.ds(e * 4, 4)]).then_inc(b_b1, 1)
                a.wait_ge(b_b1, e + 1)
                a.sem_inc(tk_a, 1)
                with a.Fori(lo, hi) as i:
                    rows_ready = [a.to_reg(i * 4 + m + 1) for m in range(4)]
                    ready = a.to_reg(i + 2)
                    for m in range(4):
                        a.wait_ge(b_h, rows_ready[m])
                        nc.scalar.activation(hT[:, m, :], hidden_bank[m][:, 0:ST], ACT.Gelu,
                                             bias=b1e[:, m:m + 1]).then_inc(b_g, 1)
                    xT_copy(ready)

        @block.tensor
        def _(pe):
            mm = nc.tensor.matmul
            pe.wait_ge(s_id, 13)
            pe.wait_ge(s_rawf, 2)
            pe.sem_inc(s_tp, 2 * CH)
            for h in range(2):
                if h:
                    pe.wait_ge(s_ec, 2)
                for k in range(2):
                    for j in range(G):
                        last = nc.tensor.transpose(pb[6 + k][:, j * GP:(j + 1) * GP],
                                                   rawf[0:GP, k, (h * G + j) * P:(h * G + j + 1) * P], ident[0:GP, 0:GP])
                    last.then_inc(s_et, 1)
            pe.wait_ge(s_grpd, 4)
            for k in range(4):
                last = mm(pb[0][:, k * GP:(k + 1) * GP], ones[0:GP, :], diag[0:GP, k, :], start=True, stop=True,
                          skip_group_check=True)
            last.then_inc(s_grpb, 1)
            pe.wait_ge(s_eng0, 18)
            nc.tensor.transpose(pb[1][0:ICOLS, 0:P], icode[:, :], ident[:, :]).then_inc(s_it, 1)
            pe.wait_ge(s_wl, 16 * 9)
            pe.wait_ge(s_code, 1)

            def transposes_0(c, b, u):
                pe.wait_ge(s_xl, c * CH + u + 1)
                for h in range(2):
                    last = nc.tensor.transpose(pb[(7 * b + u) % 2][:, h * P:(h + 1) * P], xlr[:, b, u, h * P:(h + 1) * P],
                                               ident[:, :])
                last.then_inc(s_tp, 1)

            def products_0(c, b, u):
                w = (7 * b + u) % 2
                keys = pb[4][0:S, u * P:(u + 1) * P] if u < 4 else pb[5][0:S, (u - 4) * P:(u - 3) * P]
                pe.wait_ge(s_ev, c * CH + u + 1)
                for h in range(2):
                    mm(pb[2 + b][:, u * 2 * S:(u + 1) * 2 * S], xlT[:, w, h, :], wqk[:, h, :], start=h == 0, stop=h == 1,
                       skip_group_check=True)
                for h in range(2):
                    last = mm(keys, wqk[:, h, S:2 * S], xlT[:, w, h, :], start=h == 0, stop=h == 1, skip_group_check=True)
                last.then_inc(s_qk, 1)

            def chunk_0(c, b):
                transposes_0(c, b, 0)
                transposes_0(c, b, 1)
                pe.wait_ge(s_qks, c + 1)
                pe.sem_inc(tk_p, 1)
                pe.wait_ge(s_kt, c * 2 + 2)
                pe.sem_inc(tk_p, 1)
                for u in range(CH):
                    products_0(c, b, u)
                    if u + 2 < CH:
                        transposes_0(c, b, u + 2)

            with pe.Fori(0, NCH // 2) as k:
                for b in range(2):
                    chunk_0(2 * k + b, b)
            chunk_0(NCH - 1, 0)

            def q_transposes(ahead):
                pe.wait_ge(s_qs, ahead)
                for j in range(G):
                    last = nc.tensor.transpose(pb[0][0:S, j * P:(j + 1) * P], qs[:, j, :], ident[:, :])
                last.then_inc(s_qt, 1)

            def scores(done):
                pe.wait_ge(s_mask, done)
                for j in range(G):
                    mm(pb[1][:, j * P:(j + 1) * P], mask[:, j, :], pen[:, :], start=j == 0, stop=False)
                pe.wait_ge(s_kts, done)
                mm(pb[1][:, :], kts[:, :], qT[:, :], start=False, stop=True).then_inc(s_sc, 1)

            def prob_transposes(done):
                pe.wait_ge(s_p, done)
                for j in range(G):
                    last = nc.tensor.transpose(pb[2][:, j * P:(j + 1) * P], prob[:, j * P:(j + 1) * P], ident[:, :])
                last.then_inc(s_pt, 1)

            def sums(slot, done):
                for j in range(G):
                    last = mm(pb[3][:, 0:W1COLS], probT[:, j * P:(j + 1) * P],
                              xg[:, bass.ds(slot + j, 1), 0:W1COLS].rearrange("p o d -> p (o d)"),
                              start=j == 0, stop=j == G - 1)
                    if j == 0:
                        last.wait_op(s_pts, done, AT_LEAST)
                last.then_inc(s_pv, 1)

            def quad(k):
                cnt = counts(pe, k)
                _, _, slot = item_reader(pe, k)
                for i in range(4):
                    first = isinstance(k, int) and i == 0
                    scores(cnt[i + 1])
                    before = None if first else slot(i - 1)
                    q_transposes(cnt[i + 2])
                    if not first:
                        sums(before, cnt[i])
                    prob_transposes(cnt[i + 1])

            pe.wait_ge(s_m0, 1)
            n_quads = quad_count(pe)
            q_transposes(1)
            quad(0)
            with pe.Fori(1, n_quads) as k:
                quad(k)
            n_items = kept(pe, n_quads * 4, NG, ITEMS)
            sums(item_reader(pe, last_quad(pe))[2](3), pe.to_reg(n_items))

            pe.wait_ge(s_acc, n_items + 1)
            pe.sem_inc(tk_p, 1)

            def transposes_a(c, b, u):
                pe.wait_ge(a_xn, c * CH + u + 1)
                for h in range(2):
                    last = nc.tensor.transpose(pb[4 + (7 * b + u) % 2][:, h * P:(h + 1) * P],
                                               rows[:, b, u, h * P:(h + 1) * P], ident[:, :])
                last.then_inc(a_tp, 1)

            def logits(c, b, u):
                pe.wait_ge(a_ev, (c * CH + u + 1) * 2)
                for h in range(2):
                    last = mm(pb[6][:, 64 * b + u * NE:64 * b + (u + 1) * NE], xnT[:, (7 * b + u) % 2, h, :], wr[:, h, :],
                              start=h == 0, stop=h == 1, skip_group_check=True)
                last.then_inc(a_lg, 1)

            def chunk_a(c, b):
                transposes_a(c, b, 0)
                for u in range(1, CH):
                    transposes_a(c, b, u)
                    logits(c, b, u - 1)
                logits(c, b, CH - 1)
                flat = asg[:, :, :].rearrange("p u e -> p (u e)")
                width = (CH + 1) * NE
                pe.wait_ge(a_as, c + 1)
                mm(pb[7][:, 64 * b:64 * b + width], tri[:, :], flat, start=True, stop=False, skip_group_check=True)
                for d in range(1, CH + 1):
                    last = mm(pb[7][:, 64 * b + d * NE:64 * b + width], ones[:, :], flat[:, 0:width - d * NE],
                              start=False, stop=d == CH, skip_group_check=True)
                last.then_inc(a_pos, 1)

            with pe.Fori(0, NCH // 2) as k:
                for b in range(2):
                    chunk_a(2 * k + b, b)
            chunk_a(NCH - 1, 0)

            pe.wait_ge(b_c, 1)

            def x_transposes(loaded, taken=None):
                pe.wait_ge(b_rl, loaded)
                for k in range(2):
                    for h in range(2):
                        if k == 1 and h == 0 and taken is not None:
                            pe.wait_ge(b_ys, taken)
                        last = nc.tensor.transpose(pb[0][:, h * ST + k * P:h * ST + (k + 1) * P],
                                                   xrows[:, k, h * P:(h + 1) * P], ident[:, :])
                last.then_inc(b_xt, 1)

            def expert(e, b, k):
                lo, hi = expert_ends(pe, e)
                pe.wait_ge(b_w[b], 32 * (k + 1))
                pe.sem_inc(tk_p, 1)
                with pe.Fori(lo, hi) as i:
                    copied, taken = pe.to_reg(i * 2 + 2), pe.to_reg(i * 2)
                    loaded = pe.to_reg(i * 16 + 32)
                    hidden = [pe.to_reg(i * 4 + c + 1) for c in range(4)]
                    pe.wait_ge(b_xe, copied)
                    for m in range(4):
                        for c in range(2):
                            last = mm(hidden_bank[m][:, 0:ST],
                                      w1s[:, b, c, m * P:(m + 1) * P], xT[:, c, :], start=c == 0, stop=c == 1,
                                      skip_group_check=True)
                        last.then_inc(b_h, 1)
                    x_transposes(loaded, taken)
                    for c in range(4):
                        pe.wait_ge(b_g, hidden[c])
                        for k2 in range(2):
                            last = mm(pb[3 + k2][:, 0:D], hT[:, c, k2 * P:(k2 + 1) * P], w2s[:, b, c, :],
                                      start=c == 0, stop=c == 3)
                    last.then_inc(b_y, 1)

            x_transposes(16)
            with pe.Fori(0, NE // 2) as k:
                for b in range(2):
                    expert(2 * k + b, b, k)


_INS = ['x', 'src', 'dst', 'L0_gnn_Wq', 'L0_gnn_bq', 'L0_gnn_Wk', 'L0_gnn_bk', 'L0_ffn_gamma', 'L0_ffn_beta',
        'L0_ffn_Wr', 'L0_ffn_br', 'L0_ffn_W1', 'L0_ffn_b1', 'L0_ffn_W2', 'L0_ffn_b2']


def kernel(**inputs):
    import numpy as _np
    import concourse.bacc as _bacc
    from concourse import mybir as _mybir
    from concourse.bass_utils import run_bass_kernel_spmd as _run

    nc = _bacc.Bacc("TRN2", target_bir_lowering=False, num_devices=1)
    arrays, args = {}, []
    for name in _INS:
        a = _np.ascontiguousarray(inputs[name])
        arrays[f"in_{name}_dram"] = a
        args.append(nc.dram_tensor(f"in_{name}_dram", a.shape, _mybir.dt.from_np(a.dtype), kind="ExternalInput").ap())
    args.append(nc.dram_tensor("out_0_dram", (OUT_ROWS, D), _mybir.dt.float32, kind="ExternalOutput").ap())
    build(nc, *args)
    r = _run(nc, [arrays], core_ids=[0])
    return r.results[0]["out_0_dram"][0:N]
```

```python
import concourse.bass as bass
from concourse import mybir
from contextlib import ExitStack

F32 = mybir.dt.float32
BF16 = mybir.dt.bfloat16
I32 = mybir.dt.int32
I16 = mybir.dt.int16
U32 = mybir.dt.uint32
ALU = mybir.AluOpType
ACT = mybir.ActivationFunctionType
X_AXIS = mybir.AxisListType.X
AT_LEAST = "sem-ge"

P = 128
N = 6250
D = 256
S = 25
E_IN = 106250
NE = 8
H = 512
EPS = 1e-5

NT = -(-N // P)
LAST = N - (NT - 1) * P
CH = 7
NCH = NT // CH
CHROWS = CH * P
NULL_T = NT
NTX = NT + 1
PAD_DST = NT * P - 1

G = 4
GE = G * P
NG = -(-E_IN // GE)
GP = NG // 2
FULLP = E_IN // (2 * GE)
RESTE = E_IN - FULLP * 2 * GE
BAND = P // G
ROW = D + 1 + S
W1COLS = D + 1
XSLOTS = 8
ISLOTS = 8
AHEAD = 8

ICOLS = 80
ITEMS = P * ICOLS
TBITS = 64
BIG = 1e30
DK = 5.0

CAP = 6528
ST = 256
MROW = D + 4
XE_ROWS = NE * CAP
OUT_ROWS = N + ST


def build(nc, x, src, dst, Wq, bq, Wk, bk, gamma, beta, Wr, br, W1, b1, W2, b2, out):
    ctx = ExitStack()
    with ctx:
        def sb(name, shape, dt=F32):
            return ctx.enter_context(nc.sbuf_tensor(name, shape, dt))

        def sem(name):
            return ctx.enter_context(nc.semaphore(name))

        ctx.enter_context(nc.allow_non_contiguous_dma(reason="small columns of weights"))

        rows_dram = nc.dram_tensor("rows_dram", (NT * P, ROW), F32, kind="Internal").ap()
        item_dram = nc.dram_tensor("item_dram", (ITEMS,), I16, kind="Internal").ap()
        xe_dram = nc.dram_tensor("xe_dram", (XE_ROWS, MROW), F32, kind="Internal").ap()

        acc = sb("acc", [P, NTX, W1COLS])
        m_all = sb("m_all", [P, NTX])
        item_row = sb("item_row", [1, ITEMS], I16)
        srccol = sb("srccol", [P, NG, G], I32)
        dstcol = sb("dstcol", [P, NG, G])
        ident = sb("ident", [P, P])
        pen = sb("pen", [P, P], BF16)
        tri = sb("tri", [P, P], BF16)
        ones = sb("ones", [P, P])
        ones_b = sb("ones_b", [P, P], BF16)
        iota8 = sb("iota8", [P, NE])
        ecap = sb("ecap", [P, NE])
        tok = sb("tok", [P, NT])
        itemidx = sb("itemidx", [P, ICOLS])
        vmask = sb("vmask", [P, 1])
        tail = sb("tail", [P, 2, MROW])
        wqk = sb("wqk", [P, 2, 2 * S])
        bqk = sb("bqk", [P, 2 * S])
        bkcol = sb("bkcol", [S, 1])
        wr = sb("wr", [P, 2, NE])
        brb = sb("brb", [P, NE])
        wrg = sb("wrg", [P, 2, NE])
        lbias = sb("lbias", [P, NE])
        betas = sb("betas", [P, 2, P])
        gcol = sb("gcol", [P, 2])
        bcol = sb("bcol", [P, 2])
        epsc = sb("epsc", [P, 2])

        arena_b = sb("arena_b", [P, 2 * NTX * P])
        kT = arena_b[:, 0:NTX * P]
        iota_n = arena_b[:, NTX * P:2 * NTX * P]
        w1s = arena_b[:, 0:2048].rearrange("p (e c h) -> p e c h", e=2, c=2)
        w2s = arena_b[:, 2048:4096].rearrange("p (e c d) -> p e c d", e=2, c=4)
        b2b = arena_b[:, 4096:6144].rearrange("p (e d) -> p e d", e=NE)
        b1c = arena_b[:, 6144:6144 + 4 * NE]
        xrows = arena_b[:, 6400:6400 + 2 * MROW].rearrange("p (k r) -> p k r", k=2)
        xT = arena_b[:, 7000:7512].rearrange("p (c n) -> p c n", c=2)
        hT = arena_b[:, 7600:8624].rearrange("p (m n) -> p m n", m=4)
        ybuf = arena_b[:, 8700:9212].rearrange("p (k d) -> p k d", k=2)
        ysum = arena_b[:, 9300:9812].rearrange("p (k d) -> p k d", k=2)

        arena_a = sb("arena_a", [P, 12750])
        xlr = arena_a[:, 0:2 * CH * W1COLS].rearrange("p (b u d) -> p b u d", b=2, u=CH)
        prod = arena_a[:, 3600:3600 + NT * S].rearrange("p (t s) -> p t s", t=NT)
        qk_all = arena_a[:, 4900:4900 + NT * 2 * S].rearrange("p (t s) -> p t s", t=NT)
        q_all = arena_a[:, 7400:7400 + NT * S].rearrange("p (t s) -> p t s", t=NT)
        rawf = arena_a[:, 8650:8650 + 2048].rearrange("p (k n) -> p k n", k=2)
        raw_i = arena_a[:, 10700:10700 + 2048].bitcast(I32).rearrange("p (k n) -> p k n", k=2)
        xg = arena_a[:, 0:XSLOTS * G * ROW].rearrange("p (n r) -> p n r", r=ROW)
        xr = arena_a[:, 9100:9100 + 2 * CH * D].rearrange("p (b u d) -> p b u d", b=2, u=CH)
        rows = arena_a[:, 3600:3600 + 2 * CH * MROW].rearrange("p (b u r) -> p b u r", b=2, u=CH)
        xnT = arena_a[:, 7300:7300 + 2 * D].rearrange("p (b c n) -> p b c n", b=2, c=2)

        xlT = sb("xlT", [P, 2, 2, P])
        st = sb("st", [P, 2, CH, 6])
        mv = sb("mv", [P, 2, CH, 2])
        lnv = sb("lnv", [P, 2, CH])
        rstd = sb("rstd", [P, 2, CH])
        gmax = sb("gmax", [P, 2])
        gmin = sb("gmin", [P, 2])
        ghl = sb("ghl", [P, 2, 2], I32)
        ghf = sb("ghf", [P, 2, 2])
        cntb = sb("cntb", [P, 2, NG])
        incl = sb("incl", [P, NG])
        basef = sb("basef", [P, NG])
        delta = sb("delta", [P, NG])
        stepw = sb("stepw", [P, NG])
        gsel = sb("gsel", [P, NG])
        diag = sb("diag", [P, 4, GP])
        icode = sb("icode", [P, ICOLS])
        ivalid = sb("ivalid", [P, ICOLS])
        ilist = sb("ilist", [ICOLS, P], I16)
        incl_i = sb("incl_i", [1, NG + 3], I32)
        idx = sb("idx", [P, ISLOTS, G], I32)
        kts = sb("kts", [S, P])
        qs = sb("qs", [P, G, BAND])
        qT = sb("qT", [BAND, G, P])
        mask = sb("mask", [P, 2, G, P], BF16)
        prob = sb("prob", [P, GE])
        probT = sb("probT", [P, GE])
        mx = sb("mx", [P, 1])
        mnew = sb("mnew", [P, 1])
        nbias = sb("nbias", [P, 2])
        mdiff = sb("mdiff", [P, 2])
        alpha = sb("alpha", [P, 2])
        rl = sb("rl", [P, CH])
        lg = sb("lg", [P, CH, NE])
        top = sb("top", [P, CH, NE])
        topi = sb("topi", [P, CH, NE], U32)
        idxf = sb("idxf", [P, CH, 2])
        oh = sb("oh", [P, 2, CH, NE])
        asg = sb("asg", [P, CH + 1, NE], BF16)
        tdiff = sb("tdiff", [P, CH])
        ex = sb("ex", [P, CH])
        den2 = sb("den2", [P, CH])
        w0 = sb("w0", [P, CH])
        ebase = sb("ebase", [P, NE])
        slotv = sb("slotv", [P, CH, NE])
        slotp = sb("slotp", [P, 2, CH, NE])
        slotf = sb("slotf", [P, 2, CH])
        slots = sb("slots", [P, 2, 2, CH], I32)
        cnt_i = sb("cnt_i", [1, NE], I32)
        nst_i = sb("nst_i", [1, NE], I32)
        nst_f = sb("nst_f", [1, NE])
        zero8 = sb("zero8", [1, NE])
        eend_f = sb("eend_f", [1, NE])
        eend = sb("eend", [1, NE + 1], I32)
        metaA = sb("metaA", [P, 2, 4])
        wsel = sb("wsel", [P, 2])
        weq = sb("weq", [P, 2])
        wtok = sb("wtok", [P, 2])
        tokB = sb("tokB", [P, 2], I32)
        b1e = sb("b1e", [P, 4])

        pb = [ctx.enter_context(nc.psum_tensor(f"pb{i}", [P, 512], F32)) for i in range(8)]
        score_bank = [pb[1], pb[4]]
        sums_bank = [pb[3], pb[5]]
        hidden_bank = [pb[1], pb[2], pb[5], pb[6]]

        s_cst = sem("s_cst"); s_zero = sem("s_zero"); s_wl = sem("s_wl"); s_x = sem("s_x")
        s_xf = [sem(f"s_xf{i}") for i in range(2)]; s_edge = sem("s_edge")
        s_id = sem("s_id"); s_iota = sem("s_iota"); s_grpd = sem("s_grpd"); s_gs = sem("s_gs")
        s_ci = sem("s_ci"); s_rawf = sem("s_rawf"); s_et = sem("s_et"); s_ec = sem("s_ec")
        s_eng0 = sem("s_eng0")
        s_v0 = sem("s_v0"); s_grp = sem("s_grp"); s_grpb = sem("s_grpb"); s_iw = sem("s_iw"); s_ir = sem("s_ir")
        s_st = sem("s_st"); s_mv = sem("s_mv"); s_ln = sem("s_ln"); s_rs = sem("s_rs"); s_xl = sem("s_xl")
        s_accw = sem("s_accw"); s_tp = sem("s_tp"); s_ev = sem("s_ev"); s_qk = sem("s_qk"); s_kt = sem("s_kt")
        s_qks = sem("s_qks"); s_q = sem("s_q"); s_m0 = sem("s_m0"); s_rw = sem("s_rw"); s_code = sem("s_code")
        s_it = sem("s_it")
        s_idx = [sem(f"s_idx{i}") for i in range(ISLOTS)]
        s_g = [sem(f"s_g{i}") for i in range(XSLOTS)]
        xg_free = sem("xg_free"); xg_ready = sem("xg_ready")
        s_qs = sem("s_qs"); s_qt = sem("s_qt"); s_qTs = sem("s_qTs"); s_kts = sem("s_kts"); s_mask = sem("s_mask")
        s_sc = sem("s_sc"); s_mx = sem("s_mx"); s_mn = sem("s_mn"); s_nb = sem("s_nb"); s_md = sem("s_md")
        s_ms = sem("s_ms"); s_p = sem("s_p"); s_al = sem("s_al"); s_pt = sem("s_pt"); s_pts = sem("s_pts")
        s_pv = sem("s_pv"); s_acc = sem("s_acc")
        tk_v = sem("tk_v"); tk_a = sem("tk_a"); tk_p = sem("tk_p"); tk_g = sem("tk_g"); tk_s = sem("tk_s")
        a_x = [sem(f"a_x{i}") for i in range(2)]
        a_o = [sem(f"a_o{i}") for i in range(2)]
        a_v = sem("a_v"); a_wr = sem("a_wr"); a_lb = sem("a_lb"); a_x2 = sem("a_x2"); a_rl = sem("a_rl")
        a_st = sem("a_st"); a_mv = sem("a_mv"); a_ln = sem("a_ln"); a_rs = sem("a_rs")
        a_xn = sem("a_xn"); a_tp = sem("a_tp"); a_ev = sem("a_ev"); a_lg = sem("a_lg"); a_df = sem("a_df")
        a_ex = sem("a_ex"); a_as = sem("a_as"); a_pos = sem("a_pos"); a_slot = sem("a_slot")
        a_sc = [sem(f"a_sc{i}") for i in range(2)]
        a_cnt = sem("a_cnt"); a_tail = sem("a_tail")
        b_w = [sem(f"b_w{i}") for i in range(2)]
        b_c = sem("b_c"); b_v = sem("b_v"); b_rl = sem("b_rl"); b_eq = sem("b_eq"); b_ws = sem("b_ws")
        b_tl = sem("b_tl"); b_tok = sem("b_tok"); b_b1 = sem("b_b1"); b_xt = sem("b_xt"); b_xe = sem("b_xe")
        b_h = sem("b_h"); b_g = sem("b_g"); b_y = sem("b_y"); b_meta = sem("b_meta")
        b_ys = sem("b_ys"); b_yb = sem("b_yb"); b_sc = sem("b_sc"); b_t = sem("b_t")

        block = ctx.enter_context(nc.Block())

        def col(ap, i, n=1):
            return ap[:, bass.ds(i, n)]

        item_words = item_row[:, :].bitcast(I32)

        def kept(eng, value, low, high):
            return eng.snap(eng.to_reg(value), donate=True, min_val=low, max_val=high)

        def item_reader(eng, k):
            words, known = {}, {}

            def field(j, shift, bits, high, scale=1):
                w = j // 2
                if w not in words:
                    words[w] = eng.value_load(item_words[0:1, bass.ds(k * 2 + w, 1)], min_val=0, max_val=2 ** 30 - 1)
                if (j, shift, bits) not in known:
                    value = (words[w] >> (16 * (j % 2) + shift)) & bits
                    known[j, shift, bits] = kept(eng, value * scale if scale > 1 else value, 0, high * scale)
                return known[j, shift, bits]

            return (lambda j: field(j, 0, TBITS - 1, NULL_T), lambda j: field(j, 6, 255, NG - 1),
                    lambda j: field(j, 6, XSLOTS - 1, XSLOTS - 1, scale=G))

        def quad_count(eng):
            return eng.value_load(incl_i[0:1, NG:NG + 1], min_val=NG // 4, max_val=NG * NT // 4)

        def last_quad(eng):
            return eng.value_load(incl_i[0:1, NG + 1:NG + 2], min_val=NG // 4 - 1, max_val=NG * NT // 4)

        def counter(eng, k):
            known = {}

            def number(j):
                if j not in known:
                    known[j] = 4 * k + j if isinstance(k, int) else eng.to_reg(k * 4 + j)
                return known[j]
            return number

        def expert_ends(eng, e):
            lo = eng.value_load(eend[0:1, bass.ds(e, 1)], min_val=0, max_val=NE * 25)
            hi = eng.value_load(eend[0:1, bass.ds(e + 1, 1)], min_val=1, max_val=NE * 25)
            return lo, hi

        def x_tiles(ap, lo, n):
            return ap[bass.ds(lo, n * P), :].rearrange("(t p) d -> p t d", p=P)

        @block.sync
        def _(sp):
            sp.wait_ge(s_zero, 3)
            for k, e in enumerate((src, dst)):
                sp.dma_start(raw_i[0:FULLP, k, :],
                             e[0:FULLP * 2 * GE].rearrange("(p n) -> p n", p=FULLP)).then_inc(s_edge, 16)
                sp.dma_start(raw_i[FULLP:FULLP + 1, k, 0:RESTE],
                             e[FULLP * 2 * GE:E_IN].rearrange("(p n) -> p n", p=1)).then_inc(s_edge, 16)
            for c in range(NCH - 1):
                sp.dma_start(acc[:, c * CH:(c + 1) * CH, 0:D], x_tiles(x, c * CHROWS, CH)).then_inc(s_xf[c] if c < 2 else s_x, 16)
            sp.dma_start(acc[:, NT - CH:NT - 1, 0:D], x_tiles(x, (NT - CH) * P, CH - 1)).then_inc(s_x, 16)
            sp.dma_start(acc[0:LAST, NT - 1, 0:D], x[(NT - 1) * P:N, :]).then_inc(s_x, 16)
            sp.wait_ge(s_ec, 4)
            for v in range(AHEAD):
                sp.dma_start(idx[:, v, :], srccol[:, v, :]).then_inc(s_idx[v], 16)
            with sp.Fori(0, NCH - 1) as c:
                sp.wait_ge(s_accw, c + 3)
                sp.dma_start(rows_dram[bass.ds(c * CHROWS, CHROWS), 0:W1COLS].rearrange("(t p) d -> p t d", p=P),
                             acc[:, bass.ds(c * CH, CH), :]).then_inc(s_rw, 16)
            sp.wait_ge(s_code, 1)
            sp.dma_start(item_dram.rearrange("(c p) -> c p", p=P), ilist[:, :]).then_inc(s_iw, 16)
            sp.wait_ge(s_iw, 16)
            sp.dma_start(item_row[:, :], item_dram.rearrange("(o n) -> o n", o=1)).then_inc(s_ir, 16)
            sp.wait_ge(s_accw, 2 + NCH)
            sp.dma_start(rows_dram[(NT - CH) * P:NT * P, 0:W1COLS].rearrange("(t p) d -> p t d", p=P),
                         acc[:, NT - CH:NT, :]).then_inc(s_rw, 16)
            sp.wait_ge(s_q, 1)
            sp.dma_start(rows_dram[:, W1COLS:ROW].rearrange("(t p) s -> p t s", p=P), q_all[:, :, :]).then_inc(s_rw, 16)


            def give_back(g, v):
                done = sp.value_load(incl_i[0:1, bass.ds(g, 1)], min_val=1, max_val=NG * NT)
                sp.wait_ge(s_pv, done)
                sp.sem_inc(xg_free, 1)
                sp.dma_start(idx[:, (v + AHEAD) % ISLOTS, :], srccol[:, bass.ds(g + AHEAD, 1), :].rearrange("p o g -> p (o g)"))\
                    .then_inc(s_idx[(v + AHEAD) % ISLOTS], 16)

            def load_x(c, b, last=False):
                if not last:
                    sp.dma_start(xr[:, b, :, :], x_tiles(x, c * CHROWS, CH)).then_inc(a_x[b], 16)
                else:
                    sp.dma_start(xr[:, b, 0:CH - 1, :], x_tiles(x, c * CHROWS, CH - 1)).then_inc(a_x[b], 16)
                    sp.dma_start(xr[0:LAST, b, CH - 1, :], x[(NT - 1) * P:N, :]).then_inc(a_x[b], 16)

            sp.wait_ge(s_m0, 1)
            load_x(0, 0)
            load_x(1, 1)
            with sp.Fori(0, NG // ISLOTS - 1) as k:
                for v in range(ISLOTS):
                    give_back(k * ISLOTS + v, v)

            n_items = kept(sp, quad_count(sp) * 4, NG, ITEMS)
            sp.wait_ge(s_acc, n_items + 1)
            sp.sem_inc(tk_s, 1)
            sp.wait_ge(s_qs, n_items + 3)
            sp.sem_inc(tk_s, 1)

            def store_x2(c, b, k, last=False):
                sp.wait_ge(a_x2, CH * (c + 1))
                if not last:
                    sp.dma_start(x_tiles(out, c * CHROWS, CH), xr[:, b, :, :]).then_inc(a_o[b], 16)
                else:
                    sp.dma_start(x_tiles(out, c * CHROWS, CH - 1), xr[:, b, 0:CH - 1, :]).then_inc(a_o[b], 16)
                    sp.dma_start(out[(NT - 1) * P:N, :], xr[0:LAST, b, CH - 1, :]).then_inc(a_o[b], 16)

            for k in range(2):
                sp.dma_start(out[N + k * P:N + (k + 1) * P, :], tail[:, k, 0:D]).then_inc(a_tail, 16)
            sp.dma_start(b2b[:, :, :].rearrange("p e d -> p (e d)"),
                         b2.rearrange("e d -> (e d)").partition_broadcast(P)).then_inc(a_tail, 16)
            for e in range(NE):
                sp.dma_start(b1c[:, 4 * e:4 * e + 4], b1[e, :].rearrange("(m p) -> p m", p=P)).then_inc(a_tail, 16)
            with sp.Fori(0, 2) as k:
                for b in range(2):
                    store_x2(2 * k + b, b, k)
                    sp.wait_ge(a_o[b], 16 * (k + 1))
                    sp.sem_inc(tk_s, 1)
                    sp.wait_ge(a_xn, CH * (2 * k + b) + CH)
                    sp.sem_inc(tk_s, 1)
                    load_x(2 * k + b + 2, b)
            store_x2(4, 0, 2)
            sp.wait_ge(a_o[0], 16 * 3)
            sp.wait_ge(a_xn, CH * 5)
            load_x(6, 0, last=True)
            store_x2(5, 1, 2)
            store_x2(6, 0, 3, last=True)

            sp.wait_ge(a_cnt, 2)
            with sp.Fori(0, NE) as e:
                cnt = sp.value_load(cnt_i[0:1, bass.ds(e, 1)], min_val=0, max_val=N)
                for k in range(2):
                    sp.dma_start(xe_dram[bass.ds(e * CAP + cnt + k * P, P), :], tail[:, k, :]).then_inc(a_tail, 16)
            sp.wait_ge(a_tail, 16 * (3 + NE + 2 * NE))
            for b in range(2):
                sp.wait_ge(a_sc[b], 16 * 2 * CH * ((NCH + 1 - b) // 2))
            sp.wait_ge(b_c, 1)
            with sp.Fori(0, NE) as e:
                lo, hi = expert_ends(sp, e)
                first = sp.snap(e * CAP - lo * ST)
                with sp.Fori(lo, hi) as i:
                    sp.wait_ge(b_xt, i)
                    sp.wait_ge(b_meta, i)
                    sp.sem_inc(tk_s, 1)
                    row = (first + i * ST).with_bounds(min_val=0, max_val=XE_ROWS - ST)
                    sp.dma_start(xrows[:, :, :], xe_dram[bass.ds(row, ST), :]
                                 .rearrange("(k p) r -> p k r", p=P)).then_inc(b_rl, 16)
            hi = sp.value_load(eend[0:1, NE:NE + 1], min_val=1, max_val=NE * 25)
            sp.wait_ge(b_xt, hi)
            sp.wait_ge(b_meta, hi)
            sp.sem_inc(tk_s, 1)
            sp.dma_start(xrows[:, :, :], xe_dram[0:ST, :].rearrange("(k p) r -> p k r", p=P)).then_inc(b_rl, 16)
            sp.wait_ge(b_rl, hi * 16 + 16)
            sp.sem_inc(tk_s, 1)
            sp.wait_ge(b_t, hi + 1)
            sp.sem_inc(tk_s, 1)

        @block.gpsimd
        def _(g):
            def cst(ins):
                ins.then_inc(s_cst, 1)

            cst(g.memset(ident[:, :], 0.0))
            cst(g.memset(pen[:, :], 0.0))
            cst(g.memset(ones[:, :], 1.0))
            cst(g.memset(ones_b[:, :], 1.0))
            cst(g.memset(tri[:, :], 1.0))
            cst(g.memset(vmask[:, :], 1.0))
            cst(g.memset(tail[:, :, :], 0.0))
            g.wait_ge(s_cst, 7)
            g.affine_select(out=ident[:, :], in_=ident[:, :], compare_op=ALU.not_equal, fill=1.0, base=0,
                            pattern=[[-1, P]], channel_multiplier=1).then_inc(s_id, 1)
            g.affine_select(out=pen[:, :], in_=pen[:, :], compare_op=ALU.not_equal, fill=-BIG, base=0,
                            pattern=[[-1, P]], channel_multiplier=1).then_inc(s_id, 1)
            g.affine_select(out=tri[:, :], in_=tri[:, :], compare_op=ALU.is_gt, fill=0.0, base=0,
                            pattern=[[1, P]], channel_multiplier=-1).then_inc(s_id, 1)
            g.affine_select(out=vmask[:, :], in_=vmask[:, :], compare_op=ALU.is_ge, fill=0.0, base=LAST - 1,
                            pattern=[[0, 1]], channel_multiplier=-1).then_inc(s_id, 1)
            g.iota(tail[:, :, D:D + 1], [[P, 2]], base=N, channel_multiplier=1,
                   allow_small_or_imprecise_dtypes=True).then_inc(s_id, 1)
            g.memset(tail[:, :, D + 3:D + 4], -1.0).then_inc(s_id, 1)
            g.iota(itemidx[:, :], [[P, ICOLS]], base=0, channel_multiplier=1,
                   allow_small_or_imprecise_dtypes=True).then_inc(s_id, 1)
            g.iota(iota8[:, :], [[1, NE]], base=0, channel_multiplier=0,
                   allow_small_or_imprecise_dtypes=True).then_inc(s_id, 1)
            g.iota(ecap[:, :], [[CAP, NE]], base=0, channel_multiplier=0,
                   allow_small_or_imprecise_dtypes=True).then_inc(s_id, 1)
            g.iota(tok[:, :], [[P, NT]], base=0, channel_multiplier=1,
                   allow_small_or_imprecise_dtypes=True).then_inc(s_id, 1)
            g.memset(kT[:, NT * P:NTX * P], 0.0).then_inc(s_id, 1)
            g.memset(acc[:, NULL_T, :], 0.0).then_inc(s_id, 1)
            g.memset(m_all[:, NULL_T:NTX], 0.0).then_inc(s_id, 1)
            g.iota(iota_n, [[1, NTX * P]], base=0, channel_multiplier=0,
                   allow_small_or_imprecise_dtypes=True).then_inc(s_iota, 1)
            g.sem_inc(s_accw, 2)

            def keep(c, b):
                g.wait_ge(s_xl, CH * (c + 1))
                g.sem_inc(tk_g, 1)
                g.tensor_copy(acc[:, bass.ds(c * CH, CH), :], xlr[:, b, :, :]).then_inc(s_accw, 1)

            with g.Fori(0, NCH // 2) as k:
                for b in range(2):
                    keep(2 * k + b, b)
            keep(NCH - 1, 0)

            g.wait_ge(s_rw, 16 * (NCH + 1))
            g.wait_ge(s_m0, 1)
            g.sem_inc(xg_free, XSLOTS)

            def gather(k, v, first=False):
                gr = k * ISLOTS + v
                slot = v % XSLOTS
                g.wait_ge(s_idx[v], 16 * (k + 1))
                g.wait_ge(xg_free, gr + 1)
                g.sem_inc(tk_g, 1)
                for j in range(G):
                    g.indirect_dma_start(
                        out=xg[:, slot * G + j, :], out_offset=None, in_=rows_dram[:, :],
                        in_offset=bass.IndirectOffsetOnAxis(ap=idx[:, v, j:j + 1], axis=0)).then_inc(s_g[slot], 16)
                if not first:
                    landed = ISLOTS // XSLOTS * k + (v - 1) // XSLOTS + 1
                    g.wait_ge(s_g[(v - 1) % XSLOTS], 16 * G * landed)
                    g.sem_inc(xg_ready, 1)

            for v in range(ISLOTS):
                gather(0, v, first=v == 0)
            with g.Fori(1, NG // ISLOTS) as k:
                for v in range(ISLOTS):
                    gather(k, v)
            g.wait_ge(s_g[XSLOTS - 1], 16 * G * (NG // XSLOTS))
            g.sem_inc(xg_ready, 1)

            def load_w(e, b):
                g.dma_start(w1s[:, b, :, :], W1[bass.ds(e, 1), :, :].rearrange("o (c p) h -> p (o c) h", p=P)).then_inc(b_w[b], 16)
                g.dma_start(w2s[:, b, :, :], W2[bass.ds(e, 1), :, :].rearrange("o (c p) d -> p (o c) d", p=P)).then_inc(b_w[b], 16)

            n_items = kept(g, quad_count(g) * 4, NG, ITEMS)
            g.wait_ge(s_acc, n_items + 1)
            g.sem_inc(tk_g, 1)
            load_w(0, 0)
            load_w(1, 1)

            def scatter(c, b, k, last=False):
                g.wait_ge(a_slot, c + 1)
                g.sem_inc(tk_g, 1)
                for u in range(CH):
                    n = LAST if last and u == CH - 1 else P
                    for r in range(2):
                        g.indirect_dma_start(
                            out=xe_dram[:, :], in_=rows[0:n, b, u, :], in_offset=None,
                            out_offset=bass.IndirectOffsetOnAxis(ap=slots[0:n, b, r, u:u + 1], axis=0))\
                            .then_inc(a_sc[b], 16)

            with g.Fori(0, NCH // 2) as k:
                for b in range(2):
                    scatter(2 * k + b, b, k)
            scatter(NCH - 1, 0, NCH // 2, last=True)

            g.wait_ge(a_o[0], 16 * 5)
            g.wait_ge(a_o[1], 16 * 3)
            g.wait_ge(a_tail, 16 * (3 + NE + 2 * NE))
            g.wait_ge(b_c, 1)

            def add_rows(e):
                lo, hi = expert_ends(g, e)
                with g.Fori(lo, hi) as i:
                    for k in range(2):
                        g.wait_ge(b_yb, i * 2 + k + 1)
                        g.sem_inc(tk_g, 1)
                        g.indirect_dma_start(
                            out=out[:, :], in_=ybuf[:, k, :], in_offset=None,
                            out_offset=bass.IndirectOffsetOnAxis(ap=tokB[:, k:k + 1], axis=0),
                            compute_op=ALU.add).then_inc(b_sc, 16)
                        g.wait_ge(b_sc, i * 32 + 16 * (k + 1))
                        g.sem_inc(b_t if k else tk_g, 1)

            add_rows(0)
            with g.Fori(0, NE // 2 - 1) as k:
                for b in range(2):
                    load_w(2 * k + 2 + b, b)
                    add_rows(2 * k + 1 + b)
            add_rows(NE - 1)

        @block.vector
        def _(v):
            v.memset(acc[96:P, NT - 1, 0:D], 0.0).then_inc(s_zero, 1)
            v.memset(raw_i[96:P, 0, :], 0).then_inc(s_zero, 1)
            v.memset(raw_i[96:P, 1, :], PAD_DST).then_inc(s_zero, 1)
            v.memset(qs[:, :, :], 0.0).then_inc(s_v0, 1)
            v.memset(xlr[:, :, :, D:W1COLS], 1.0).then_inc(s_v0, 1)
            v.memset(epsc[:, 0:1], EPS).then_inc(s_v0, 1)
            v.memset(epsc[:, 1:2], EPS * EPS).then_inc(s_v0, 1)
            v.memset(zero8[:, :], 0.0).then_inc(s_v0, 1)
            v.memset(asg[:, :, :], 0.0).then_inc(s_v0, 1)
            v.memset(eend[:, :], 0).then_inc(s_v0, 1)
            v.sem_inc(s_qks, 2)
            v.sem_inc(s_acc, 1)
            v.memset(stepw[:, :], 0.0).then_inc(s_v0, 1)
            v.memset(icode[:, :], 0.0).then_inc(s_v0, 1)
            v.wait_ge(s_edge, 64)
            for k in range(2):
                v.tensor_copy(rawf[0:GP, k, :], raw_i[0:GP, k, :]).then_inc(s_rawf, 1)
            v.wait_ge(s_rawf, 2)
            dg = rawf[0:GP, 1, :].rearrange("p (h n) -> p h n", h=2)
            v.tensor_reduce(gmin[0:GP, :], dg, axis=X_AXIS, op=ALU.min).then_inc(s_eng0, 1)
            v.tensor_reduce(gmax[0:GP, :], dg, axis=X_AXIS, op=ALU.max).then_inc(s_eng0, 1)
            v.wait_ge(s_eng0, 2)
            v.tensor_copy(ghl[0:GP, 0, :], gmax[0:GP, :]).then_inc(s_eng0, 1)
            v.tensor_copy(ghl[0:GP, 1, :], gmin[0:GP, :]).then_inc(s_eng0, 1)
            v.wait_ge(s_eng0, 4)
            v.tensor_scalar(ghl[0:GP, :, :], ghl[0:GP, :, :], 7, None, ALU.arith_shift_right).then_inc(s_eng0, 1)
            v.wait_ge(s_eng0, 5)
            v.tensor_copy(ghf[0:GP, 1, :], ghl[0:GP, 1, :]).then_inc(s_eng0, 1)
            v.tensor_tensor(ghf[0:GP, 0, :], ghl[0:GP, 0, :], ghl[0:GP, 1, :], ALU.subtract).then_inc(s_eng0, 1)
            v.wait_ge(s_eng0, 7)
            v.tensor_scalar(ghf[0:GP, 0, :], ghf[0:GP, 0, :], 1.0, None, ALU.add).then_inc(s_grp, 1)
            v.wait_ge(s_grp, 1)
            v.wait_ge(s_id, 13)
            for k in range(2):
                for h in range(2):
                    v.tensor_scalar(diag[0:GP, 2 * k + h, :], ident[0:GP, 0:GP], ghf[0:GP, k, h:h + 1], None, ALU.mult)\
                        .then_inc(s_grpd, 1)
            v.wait_ge(s_zero, 3)

            def node_tile(t):
                return acc[:, bass.ds(t, 1), 0:D].rearrange("p o d -> p (o d)")

            def statistics_0(c, b):
                for u in range(CH):
                    v.bn_stats(st[:, b, u, :], node_tile(c * CH + u)).then_inc(s_st, 1)
                v.wait_ge(s_st, CH * (c + 1))
                v.sem_inc(tk_v, 1)
                for u in range(CH):
                    v.bn_aggr(mv[:, b, u, :], st[:, b, u, :]).then_inc(s_mv, 1)

            def normalise_0(c, b):
                v.wait_ge(s_tp, CH * (c + 1))
                v.sem_inc(tk_v, 1)
                v.wait_ge(s_accw, c + 1)
                v.sem_inc(tk_v, 1)
                v.wait_ge(s_rs, c + 1)
                v.sem_inc(tk_v, 1)
                for u in range(CH):
                    v.tensor_scalar(xlr[:, b, u, 0:D], node_tile(c * CH + u), mv[:, b, u, 0:1], rstd[:, b, u:u + 1],
                                    ALU.subtract, ALU.mult).then_inc(s_xl, 1)

            def add_biases(c, b):
                made = CH * c + CH if isinstance(c, int) else v.to_reg(c * CH + CH)
                v.tensor_tensor(qk_all[:, bass.ds(c * CH, CH), :],
                                pb[2 + b][:, 0:CH * 2 * S].rearrange("p (u s) -> p u s", u=CH),
                                bqk[:, :].unsqueeze(1).to_broadcast([P, CH, 2 * S]), ALU.add)\
                    .wait_op(s_qk, made, AT_LEAST).then_inc(s_qks, 1)

            v.wait_ge(s_xf[0], 16)
            statistics_0(0, 0)
            v.wait_ge(s_xf[1], 16)
            statistics_0(1, 1)
            normalise_0(0, 0)
            v.wait_ge(s_grpb, 1)
            v.wait_ge(s_v0, 9)
            for k in range(2):
                v.tensor_copy(cntb[:, k, :].rearrange("p (q h) -> p h q", h=2),
                              pb[3][:, k * 2 * GP:(k + 1) * 2 * GP].rearrange("p (h q) -> p h q", h=2)).then_inc(s_grpd, 1)
            v.wait_ge(s_wl, 16 * 9)
            with v.Fori(0, NCH // 2 - 1) as k:
                for b in range(2):
                    c = 2 * k + b
                    normalise_0(c + 1, 1 - b)
                    v.wait_ge(s_x, 16 * (NCH - 1))
                    v.sem_inc(tk_v, 1)
                    statistics_0(c + 2, b)
                    add_biases(c, b)
            normalise_0(NCH - 2, 1)
            statistics_0(NCH - 1, 0)
            add_biases(NCH - 3, 0)
            v.wait_ge(s_grpd, 6)
            v.tensor_tensor_scan(incl[:, :], cntb[:, 0, :], stepw[:, :], 0.0, ALU.add, ALU.add).then_inc(s_eng0, 1)
            v.wait_ge(s_eng0, 8)
            v.tensor_tensor(basef[:, :], incl[:, :], cntb[:, 0, :], ALU.subtract).then_inc(s_eng0, 1)
            v.tensor_copy(incl_i[:, 0:NG], incl[0:1, :]).then_inc(s_eng0, 1)
            for o, more in ((NG, 3), (NG + 2, P + 5)):
                v.tensor_scalar(incl_i[:, o:o + 1], incl[0:1, NG - 1:NG], float(more), None, ALU.add).then_inc(s_ci, 1)
            v.wait_ge(s_ci, 2)
            for o, shift in ((NG, 2), (NG + 2, 7)):
                v.tensor_scalar(incl_i[:, o:o + 1], incl_i[:, o:o + 1], shift, None, ALU.arith_shift_right).then_inc(s_ci, 1)
            v.wait_ge(s_ci, 4)
            v.tensor_scalar(incl_i[:, NG + 1:NG + 2], incl_i[:, NG:NG + 1], -1.0, None, ALU.add).then_inc(s_ci, 1)
            v.wait_ge(s_eng0, 10)
            v.tensor_tensor(delta[:, :], cntb[:, 1, :], basef[:, :], ALU.subtract).then_inc(s_eng0, 1)
            v.wait_ge(s_eng0, 11)
            v.tensor_scalar(stepw[:, 0:1], delta[:, 0:1], 1.0, float(TBITS), ALU.mult, ALU.add).then_inc(s_eng0, 1)
            v.tensor_tensor(stepw[:, 1:NG], delta[:, 1:NG], delta[:, 0:NG - 1], ALU.subtract).then_inc(s_eng0, 1)
            v.wait_ge(s_eng0, 13)
            v.tensor_scalar(stepw[:, 1:NG], stepw[:, 1:NG], float(TBITS), None, ALU.add).then_inc(s_eng0, 1)
            v.wait_ge(s_eng0, 14)
            v.wait_ge(s_ci, 5)
            v.sem_inc(s_gs, 1)
            columns = v.value_load(incl_i[0:1, NG + 2:NG + 3], min_val=1, max_val=ICOLS)
            with v.Fori(0, columns) as c:
                free = v.to_reg(c + 1)
                v.scalar_tensor_tensor(out=gsel[:, :], in0=basef[:, :], scalar=col(itemidx, c), in1=stepw[:, :],
                                       op0=ALU.is_le, op1=ALU.mult, accum_out=col(icode, c))\
                    .wait_op(s_gs, free, AT_LEAST).then_inc(s_gs, 1)
            v.wait_ge(s_gs, columns + 1)
            v.sem_inc(tk_v, 1)
            v.tensor_tensor(icode[:, :], icode[:, :], itemidx[:, :], ALU.add).then_inc(s_eng0, 1)
            v.tensor_scalar(ivalid[:, :], itemidx[:, :], incl[:, NG - 1:NG], None, ALU.is_lt).then_inc(s_eng0, 1)
            null = float(NULL_T + TBITS * (NG - 1))
            v.wait_ge(s_eng0, 16)
            v.tensor_scalar(icode[:, :], icode[:, :], -float(TBITS) - null, None, ALU.add).then_inc(s_eng0, 1)
            v.wait_ge(s_eng0, 17)
            v.tensor_tensor(icode[:, :], icode[:, :], ivalid[:, :], ALU.mult).then_inc(s_eng0, 1)
            normalise_0(NCH - 1, 0)
            add_biases(NCH - 2, 1)
            v.wait_ge(s_it, 1)
            v.tensor_scalar(ilist[:, :], pb[6][0:ICOLS, 0:P], null, None, ALU.add).then_inc(s_code, 1)
            add_biases(NCH - 1, 0)
            v.wait_ge(s_q, 1)
            v.wait_ge(s_qks, 2 + NCH)
            v.tensor_tensor(prod[:, :, :], q_all[:, :, :], qk_all[:, :, S:2 * S], ALU.mult).then_inc(s_eng0, 1)
            v.wait_ge(s_eng0, 19)
            v.wait_ge(s_accw, 2 + NCH)
            v.wait_ge(s_kt, 2 + 2 * NCH)
            v.wait_ge(s_ir, 16)
            v.wait_ge(s_iota, 1)
            v.wait_ge(s_id, 13)
            v.tensor_reduce(m_all[:, 0:NT], prod[:, :, :], axis=X_AXIS, op=ALU.add).then_inc(s_m0, 1)
            v.wait_ge(s_m0, 1)

            def edge_mask(i, t, gr):
                v.tensor_tensor(mask[:, i % 2, :, :],
                                iota_n[:, bass.ds(t * P, P)].unsqueeze(1).to_broadcast([P, G, P]),
                                dstcol[:, bass.ds(gr, 1), :].rearrange("p o j -> p (o j)").unsqueeze(2).to_broadcast([P, G, P]),
                                ALU.not_equal).then_inc(s_mask, 1)

            def add_sums(i, t, done):
                a = acc[:, bass.ds(t, 1), :].rearrange("p o d -> p (o d)")
                v.scalar_tensor_tensor(out=a, in0=a, scalar=alpha[:, i % 2:i % 2 + 1], in1=sums_bank[i % 2][:, 0:W1COLS],
                                       op0=ALU.mult, op1=ALU.add).wait_op(s_pv, done, AT_LEAST).then_inc(s_acc, 1)

            def maximum(i, tile, done):
                v.wait_ge(s_sc, done)
                v.tensor_reduce(mx[:, :], score_bank[i % 2][:, :], axis=X_AXIS, op=ALU.max).then_inc(s_mx, 1)
                v.tensor_tensor(mnew[:, :], m_all[:, bass.ds(tile(i), 1)], mx[:, :], ALU.max)\
                    .wait_op(s_mx, done, AT_LEAST).then_inc(s_mn, 1)
                v.wait_ge(s_mn, done)
                v.tensor_scalar(nbias[:, i % 2:i % 2 + 1], mnew[:, :], -1.0 / DK, None, ALU.mult).then_inc(s_nb, 1)

            def keep_maximum(i, t, before, done):
                m = m_all[:, bass.ds(t, 1)]
                ins = v.tensor_tensor(mdiff[:, i % 2:i % 2 + 1], m, mnew[:, :], ALU.subtract)
                if before is not None:
                    ins.wait_op(s_al, before, AT_LEAST)
                ins.then_inc(s_md, 1)
                v.tensor_tensor(m, m, mnew[:, :], ALU.max).wait_op(s_md, done, AT_LEAST).then_inc(s_ms, 1)

            def quad(k):
                cnt = counter(v, k)
                tile, group, _ = item_reader(v, k)
                for i in range(4):
                    first = isinstance(k, int) and i == 0
                    edge_mask(i + 2, tile(i + 2), group(i + 2))
                    maximum(i + 1, tile, cnt(i + 2))
                    if not first:
                        add_sums(i - 1, tile(i - 1), cnt(i))
                    keep_maximum(i + 1, tile(i + 1), None if first else cnt(i), cnt(i + 2))

            n_quads = quad_count(v)
            tile, group, _ = item_reader(v, 0)
            edge_mask(0, tile(0), group(0))
            edge_mask(1, tile(1), group(1))
            maximum(0, tile, 1)
            keep_maximum(0, tile(0), None, 1)
            quad(0)
            with v.Fori(1, n_quads) as k:
                quad(k)
            n_items = kept(v, n_quads * 4, NG, ITEMS)
            last_tile, all_sums = item_reader(v, last_quad(v))[0](3), v.to_reg(n_items)
            add_sums(3, last_tile, all_sums)

            v.wait_ge(s_acc, n_items + 1)
            v.sem_inc(tk_v, 1)

            def statistics(c, b, loaded):
                t0 = c * CH
                v.reciprocal(rl[:, :], acc[:, bass.ds(t0, CH), D:W1COLS].rearrange("p u o -> p (u o)")).then_inc(a_rl, 1)
                v.wait_ge(a_x[b], loaded)
                v.wait_ge(a_rl, c + 1)
                v.sem_inc(tk_v, 1)
                for u in range(CH):
                    v.scalar_tensor_tensor(out=xr[:, b, u, :], in0=acc[:, bass.ds(t0 + u, 1), 0:D].rearrange("p o d -> p (o d)"),
                                           scalar=rl[:, u:u + 1], in1=xr[:, b, u, :],
                                           op0=ALU.mult, op1=ALU.add).then_inc(a_x2, 1)
                for u in range(CH):
                    v.wait_ge(a_x2, CH * c + u + 1)
                    v.bn_stats(st[:, 0, u, :], xr[:, b, u, :]).then_inc(a_st, 1)
                v.wait_ge(a_st, CH * (c + 1))
                v.sem_inc(tk_v, 1)
                for u in range(CH):
                    v.bn_aggr(mv[:, 0, u, :], st[:, 0, u, :]).then_inc(a_mv, 1)

            def normalise(c, b, scattered):
                v.wait_ge(a_sc[b], scattered * 16 * 2 * CH)
                v.sem_inc(tk_v, 1)
                v.wait_ge(a_rs, c + 1)
                for u in range(CH):
                    v.tensor_scalar(rows[:, b, u, 0:D], xr[:, b, u, :], mv[:, 0, u, 0:1], rstd[:, 0, u:u + 1],
                                    ALU.subtract, ALU.mult).then_inc(a_xn, 1)

            STEPS = 17

            def route(c, b, last=False):
                n = [0]

                def step(ins):
                    ins.then_inc(a_v, 1)
                    n[0] += 1

                def steps():
                    return c * STEPS + n[0]

                v.wait_ge(a_lg, CH * (c + 1))
                step(v.tensor_tensor(lg[:, :, :], pb[6][:, 64 * b:64 * b + CH * NE].rearrange("p (u e) -> p u e", u=CH),
                                     lbias[:, :].unsqueeze(1).to_broadcast([P, CH, NE]), ALU.add))
                v.wait_ge(a_v, steps())
                v.sem_inc(tk_v, 1)
                for u in range(CH):
                    ins = v.max(top[:, u, :], lg[:, u, :])
                step(ins)
                v.wait_ge(a_v, steps())
                v.tensor_tensor(tdiff[:, :], top[:, :, 1], top[:, :, 0], ALU.subtract).then_inc(a_df, 1)
                for u in range(CH):
                    ins = v.max_index(topi[:, u, :], top[:, u, :], lg[:, u, :])
                step(ins)
                v.wait_ge(a_v, steps())
                step(v.tensor_copy(idxf[:, :, :], topi[:, :, 0:2]))
                v.wait_ge(a_v, steps())
                for r in range(2):
                    step(v.tensor_tensor(oh[:, r, :, :], iota8[:, :].unsqueeze(1).to_broadcast([P, CH, NE]),
                                         idxf[:, :, r:r + 1].to_broadcast([P, CH, NE]), ALU.is_equal))
                v.wait_ge(a_v, steps())
                ins = v.tensor_tensor(asg[:, 0:CH, :], oh[:, 0, :, :], oh[:, 1, :, :], ALU.add)
                if last:
                    step(ins)
                    v.wait_ge(a_v, steps())
                    ins = v.tensor_scalar(asg[:, CH - 1, :], asg[:, CH - 1, :], vmask[:, :], None, ALU.mult)
                ins.then_inc(a_as, 1)
                step(v.tensor_copy(rows[:, b, :, D], tok[:, bass.ds(c * CH, CH)]))
                step(v.tensor_copy(rows[:, b, :, D + 3], idxf[:, :, 0]))
                v.wait_ge(a_ex, c + 1)
                step(v.tensor_scalar(den2[:, :], ex[:, :], 1.0, None, ALU.add))
                v.wait_ge(a_v, steps())
                step(v.reciprocal(w0[:, :], den2[:, :]))
                v.wait_ge(a_v, steps())
                step(v.tensor_tensor(rows[:, b, :, D + 1], ex[:, :], w0[:, :], ALU.mult))
                v.wait_ge(a_v, steps())
                step(v.tensor_tensor(rows[:, b, :, D + 2], w0[:, :], rows[:, b, :, D + 1], ALU.subtract))
                ahead = pb[7][:, 64 * b:64 * (b + 1)].rearrange("p (u e) -> p u e", u=CH + 1)
                v.wait_ge(a_pos, c + 1)
                step(v.tensor_tensor(slotv[:, :, :], ahead[:, 0:CH, :],
                                     ebase[:, :].unsqueeze(1).to_broadcast([P, CH, NE]), ALU.add))
                v.wait_ge(a_v, steps())
                step(v.tensor_tensor(ebase[:, :], ebase[:, :], ahead[:, CH, :], ALU.add))
                for r in range(2):
                    step(v.tensor_tensor(slotp[:, r, :, :], oh[:, r, :, :], slotv[:, :, :], ALU.mult))
                v.wait_ge(a_v, steps())
                step(v.tensor_reduce(slotf[:, :, :], slotp[:, :, :, :], axis=X_AXIS, op=ALU.add))
                v.wait_ge(a_v, steps())
                v.tensor_copy(slots[:, b, :, :], slotf[:, :, :]).then_inc(a_slot, 1)
                assert n[0] == STEPS + last, n[0]

            v.wait_ge(s_id, 13)
            v.tensor_copy(ebase[:, :], ecap[:, :]).then_inc(a_cnt, 1)
            v.wait_ge(a_cnt, 1)
            for h in range(2):
                v.tensor_scalar(wrg[:, h, :], wr[:, h, :], gcol[:, h:h + 1], None, ALU.mult).then_inc(a_wr, 1)
                v.tensor_copy(betas[:, h, :], bcol[:, h:h + 1].to_broadcast([P, P])).then_inc(a_wr, 1)
            statistics(0, 0, 16)
            normalise(0, 0, 0)
            v.wait_ge(a_lb, 1)
            v.tensor_tensor(lbias[:, :], pb[3][:, 0:NE], brb[:, :], ALU.add).then_inc(a_wr, 1)
            v.wait_ge(a_wr, 5)
            with v.Fori(0, NCH // 2 - 1) as k:
                for b in range(2):
                    statistics(2 * k + b + 1, 1 - b, 16 * (k + 1 + b))
                    route(2 * k + b, b)
                    normalise(2 * k + b + 1, 1 - b, k + b)
            for c in range(NCH - 3, NCH - 1):
                statistics(c + 1, 1 - c % 2, 16 * ((c + 1) // 2 + 1) + (16 if c + 1 == NCH - 1 else 0))
                route(c, c % 2)
                normalise(c + 1, 1 - c % 2, (c + 1) // 2)
            route(NCH - 1, 0, last=True)

            v.wait_ge(a_slot, NCH)
            v.tensor_tensor(nst_f[:, :], ebase[0:1, :], ecap[0:1, :], ALU.subtract).then_inc(b_v, 1)
            v.wait_ge(b_v, 1)
            v.tensor_copy(cnt_i[:, :], nst_f[:, :]).then_inc(a_cnt, 1)
            v.wait_ge(a_cnt, 2)
            v.tensor_scalar(nst_f[:, :], cnt_i[:, :], float(ST - 1), None, ALU.add).then_inc(b_v, 1)
            v.wait_ge(b_v, 2)
            v.tensor_copy(nst_i[:, :], nst_f[:, :]).then_inc(b_v, 1)
            v.wait_ge(b_v, 3)
            v.tensor_scalar(nst_i[:, :], nst_i[:, :], 8, None, ALU.arith_shift_right).then_inc(b_v, 1)
            v.wait_ge(b_v, 4)
            v.tensor_scalar(nst_f[:, :], nst_i[:, :], 1.0, None, ALU.max).then_inc(b_v, 1)
            v.wait_ge(b_v, 5)
            v.tensor_tensor_scan(eend_f[:, :], nst_f[:, :], zero8[:, :], 0.0, ALU.add, ALU.add).then_inc(b_v, 1)
            v.wait_ge(b_v, 6)
            v.tensor_copy(eend[:, 1:NE + 1], eend_f[:, :]).then_inc(b_c, 1)
            v.wait_ge(b_c, 1)

            def meta(ready):
                v.wait_ge(b_rl, ready)
                v.tensor_copy(metaA[:, :, :], xrows[:, :, D:MROW]).then_inc(b_meta, 1)

            def finish(e, i):
                one = v.to_reg(i + 1)
                halves = [v.to_reg(i * 2 + j) for j in (1, 2)]
                v.scalar_tensor_tensor(out=weq[:, :], in0=metaA[:, :, 3], scalar=iota8[:, bass.ds(e, 1)], in1=metaA[:, :, 2],
                                       op0=ALU.is_equal, op1=ALU.mult).wait_op(b_meta, one, AT_LEAST).then_inc(b_eq, 1)
                v.wait_ge(b_eq, one)
                v.tensor_tensor(wsel[:, :], weq[:, :], metaA[:, :, 1], ALU.add).then_inc(b_ws, 1)
                v.tensor_copy(wtok[:, :], metaA[:, :, 0]).then_inc(b_tl, 1)
                v.wait_ge(b_tl, one)
                v.sem_inc(tk_v, 1)
                meta(v.to_reg(i * 16 + 32))
                v.wait_ge(b_t, one)
                v.tensor_copy(tokB[:, :], wtok[:, :]).then_inc(b_tok, 1)
                for k in range(2):
                    ins = v.tensor_tensor(ysum[:, k, :], pb[3 + k][:, 0:D],
                                          b2b[:, bass.ds(e, 1), :].rearrange("p o d -> p (o d)"), ALU.add)
                    if k == 0:
                        ins.wait_op(b_y, one, AT_LEAST)
                    ins.then_inc(b_ys, 1)
                for k in range(2):
                    v.wait_ge(b_ys, halves[k])
                    v.tensor_scalar(ybuf[:, k, :], ysum[:, k, :], wsel[:, k:k + 1], None, ALU.mult).then_inc(b_yb, 1)

            v.wait_ge(a_tail, 16 * (3 + NE + 2 * NE))
            v.sem_inc(b_t, 1)
            meta(16)
            with v.Fori(0, NE) as e:
                lo, hi = expert_ends(v, e)
                with v.Fori(lo, hi) as i:
                    finish(e, i)

        @block.scalar
        def _(a):
            a.preload_act_table_set("natural_log_exp_and_others")
            a.sem_inc(s_kt, 2)
            for o, i in ((wqk[:, :, 0:S], Wq.rearrange("(c p) s -> p c s", p=P)),
                         (wqk[:, :, S:2 * S], Wk.rearrange("(c p) s -> p c s", p=P)),
                         (bqk[:, 0:S], bq.partition_broadcast(P)),
                         (bqk[:, S:2 * S], bk.partition_broadcast(P)),
                         (wr[:, :, :], Wr.rearrange("(c p) e -> p c e", p=P)),
                         (brb[:, :], br.partition_broadcast(P)),
                         (gcol[:, :], gamma.rearrange("(c p) -> p c", p=P)),
                         (bcol[:, :], beta.rearrange("(c p) -> p c", p=P))):
                a.dma_start(o, i).then_inc(s_wl, 16)
            a.dma_start(bkcol[:, :], bk.rearrange("(s o) -> s o", o=1)).then_inc(s_wl, 16)
            a.wait_ge(s_wl, 16 * 9)
            a.wait_ge(s_v0, 9)

            def inverse_std(c, b):
                a.wait_ge(s_mv, CH * (c + 1))
                nc.scalar.activation(lnv[:, b, :], mv[:, b, :, 1], ACT.Ln, bias=epsc[:, 0:1]).then_inc(s_ln, 1)
                a.wait_ge(s_ln, c + 1)
                nc.scalar.activation(rstd[:, b, :], lnv[:, b, :], ACT.Exp, scale=-0.5).then_inc(s_rs, 1)

            def copy_keys(c, lo, n, bank):
                a.wait_ge(s_qk, CH * c + lo + n)
                a.sem_inc(tk_a, 1)
                nc.scalar.activation(kT[0:S, bass.ds((c * CH + lo) * P, n * P)], bank[0:S, 0:n * P], ACT.Identity,
                                     bias=bkcol[:, :]).then_inc(s_kt, 1)

            def chunk_0(c, b, first=False, last=False):
                for u in range(CH):
                    a.wait_ge(s_tp, 2 * CH + c * CH + u + 1)
                    nc.scalar.copy(xlT[:, (7 * b + u) % 2, :, :].rearrange("p c n -> p (c n)"),
                                   pb[(7 * b + u) % 2][:, 0:D]).then_inc(s_ev, 1)
                    if u == 1 and not first:
                        copy_keys(c - 1, 4, CH - 4, pb[5])
                    if u == 1 and not last:
                        inverse_std(c + 1, 1 - b)
                    if u == CH - 2:
                        copy_keys(c, 0, 4, pb[4])

            for h in range(2):
                for k, o in ((0, srccol), (1, dstcol)):
                    a.wait_ge(s_et, 2 * h + k + 1)
                    nc.scalar.copy(o[:, h:NG:2, :].rearrange("p q j -> p j q"),
                                   pb[6 + k][:, 0:G * GP].rearrange("p (j q) -> p j q", j=G)).then_inc(s_ec, 1)
            inverse_std(0, 0)
            chunk_0(0, 0, first=True)
            with a.Fori(0, NCH // 2 - 1) as k:
                for b in (1, 0):
                    chunk_0(2 * k + 2 - b, b)
            chunk_0(NCH - 2, 1)
            chunk_0(NCH - 1, 0, last=True)
            copy_keys(NCH - 1, 4, CH - 4, pb[5])
            a.wait_ge(s_qks, 2 + NCH)
            nc.scalar.activation(q_all[:, :, :], qk_all[:, :, 0:S], ACT.Tanh).then_inc(s_q, 1)

            a.wait_ge(s_m0, 1)
            a.wait_ge(s_kt, 2 + 2 * NCH)

            def copy_k(t):
                nc.scalar.copy(kts[:, :], kT[0:S, bass.ds(t * P, P)]).then_inc(s_kts, 1)

            def copy_q(ready, slot):
                a.wait_ge(xg_ready, ready)
                a.sem_inc(tk_a, 1)
                nc.scalar.copy(qs[:, :, 0:S], xg[:, bass.ds(slot, G), W1COLS:ROW]).then_inc(s_qs, 1)

            def copy_qT(ahead):
                a.wait_ge(s_qt, ahead)
                for j in range(G):
                    nc.scalar.copy(qT[:, j, :], pb[0][j * BAND:(j + 1) * BAND, 0:P]).then_inc(s_qTs, 1)

            def exponentials(i, done):
                a.wait_ge(s_nb, done)
                nc.scalar.activation(prob[:, :], score_bank[i % 2][:, :], ACT.Exp, bias=nbias[:, i % 2:i % 2 + 1],
                                     scale=1.0 / DK).then_inc(s_p, 1)

            def scale_and_copy(i, done):
                a.wait_ge(s_md, done)
                nc.scalar.activation(alpha[:, i % 2:i % 2 + 1], mdiff[:, i % 2:i % 2 + 1], ACT.Exp, scale=1.0 / DK)\
                    .then_inc(s_al, 1)
                a.wait_ge(s_pt, done)
                nc.scalar.copy(probT[:, :], pb[2][:, :]).then_inc(s_pts, 1)

            def quad(k):
                cnt = counter(a, k)
                tile, group, slot = item_reader(a, k)
                for i in range(4):
                    ready, q_slot = a.to_reg(group(i + 3) + 1), slot(i + 3)
                    exponentials(i, cnt(i + 1))
                    copy_qT(cnt(i + 3))
                    copy_q(ready, q_slot)
                    copy_k(tile(i + 2))
                    scale_and_copy(i, cnt(i + 1))

            n_quads = quad_count(a)
            tile, group, slot = item_reader(a, 0)
            copy_q(a.to_reg(group(0) + 1), slot(0))
            for i in range(2):
                copy_qT(i + 1)
                copy_k(tile(i))
                copy_q(a.to_reg(group(i + 1) + 1), slot(i + 1))
            quad(0)
            with a.Fori(1, n_quads) as k:
                quad(k)
            n_items = kept(a, n_quads * 4, NG, ITEMS)

            a.preload_act_table_set("natural_log_exp_and_others")
            a.wait_ge(s_acc, n_items + 1)
            a.sem_inc(tk_a, 1)

            def both_stds(c):
                a.wait_ge(a_mv, CH * (c + 1))
                nc.scalar.activation(lnv[:, 0, :], mv[:, 0, :, 1], ACT.Ln, bias=epsc[:, 1:2], scale=1.0 + EPS).then_inc(a_ln, 1)
                a.wait_ge(a_ln, c + 1)
                nc.scalar.activation(rstd[:, 0, :], lnv[:, 0, :], ACT.Exp, scale=-0.5).then_inc(a_rs, 1)

            def chunk_a(c, b, last=False):
                for u in range(CH):
                    w = (7 * b + u) % 2
                    a.wait_ge(a_tp, c * CH + u + 1)
                    nc.scalar.copy(xnT[:, w, :, :].rearrange("p c n -> p (c n)"), pb[4 + w][:, 0:D]).then_inc(a_ev, 1)
                if not last:
                    both_stds(c + 1)
                a.wait_ge(a_df, c + 1)
                nc.scalar.activation(ex[:, :], tdiff[:, :], ACT.Exp).then_inc(a_ex, 1)

            both_stds(0)
            with a.Fori(0, NCH // 2) as k:
                for b in range(2):
                    chunk_a(2 * k + b, b)
            chunk_a(NCH - 1, 0, last=True)

            a.preload_act_table_set("gelu_and_others")
            a.wait_ge(b_c, 1)
            a.wait_ge(a_tail, 16 * (3 + NE + 2 * NE))

            def xT_copy(ready):
                a.wait_ge(b_xt, ready)
                for h in range(2):
                    nc.scalar.activation(xT[:, h, :], pb[0][:, h * ST:(h + 1) * ST], ACT.Identity,
                                         bias=bcol[:, h:h + 1], scale=gcol[:, h:h + 1]).then_inc(b_xe, 1)

            xT_copy(1)
            with a.Fori(0, NE) as e:
                lo, hi = expert_ends(a, e)
                a.wait_ge(b_g, lo * 4)
                a.sem_inc(tk_a, 1)
                nc.scalar.copy(b1e[:, :], b1c[:, bass.ds(e * 4, 4)]).then_inc(b_b1, 1)
                a.wait_ge(b_b1, e + 1)
                a.sem_inc(tk_a, 1)
                with a.Fori(lo, hi) as i:
                    rows_ready = [a.to_reg(i * 4 + m + 1) for m in range(4)]
                    ready = a.to_reg(i + 2)
                    for m in range(4):
                        a.wait_ge(b_h, rows_ready[m])
                        nc.scalar.activation(hT[:, m, :], hidden_bank[m][:, 0:ST], ACT.Gelu,
                                             bias=b1e[:, m:m + 1]).then_inc(b_g, 1)
                    xT_copy(ready)

        @block.tensor
        def _(pe):
            mm = nc.tensor.matmul
            pe.wait_ge(s_id, 13)
            pe.wait_ge(s_rawf, 2)
            pe.sem_inc(s_tp, 2 * CH)
            for h in range(2):
                if h:
                    pe.wait_ge(s_ec, 2)
                for k in range(2):
                    for j in range(G):
                        last = nc.tensor.transpose(pb[6 + k][:, j * GP:(j + 1) * GP],
                                                   rawf[0:GP, k, (h * G + j) * P:(h * G + j + 1) * P], ident[0:GP, 0:GP])
                    last.then_inc(s_et, 1)
            pe.wait_ge(s_grpd, 4)
            for k in range(4):
                last = mm(pb[3][:, k * GP:(k + 1) * GP], ones[0:GP, :], diag[0:GP, k, :], start=True, stop=True,
                          skip_group_check=True)
            last.then_inc(s_grpb, 1)
            pe.wait_ge(s_wl, 16 * 9)

            def transposes_0(c, b, u):
                pe.wait_ge(s_xl, c * CH + u + 1)
                for h in range(2):
                    last = nc.tensor.transpose(pb[(7 * b + u) % 2][:, h * P:(h + 1) * P], xlr[:, b, u, h * P:(h + 1) * P],
                                               ident[:, :])
                last.then_inc(s_tp, 1)

            def products_0(c, b, u):
                w = (7 * b + u) % 2
                keys = pb[4][0:S, u * P:(u + 1) * P] if u < 4 else pb[5][0:S, (u - 4) * P:(u - 3) * P]
                pe.wait_ge(s_ev, c * CH + u + 1)
                for h in range(2):
                    mm(pb[2 + b][:, u * 2 * S:(u + 1) * 2 * S], xlT[:, w, h, :], wqk[:, h, :], start=h == 0, stop=h == 1,
                       skip_group_check=True)
                for h in range(2):
                    last = mm(keys, wqk[:, h, S:2 * S], xlT[:, w, h, :], start=h == 0, stop=h == 1, skip_group_check=True)
                last.then_inc(s_qk, 1)

            def chunk_0(c, b):
                transposes_0(c, b, 0)
                transposes_0(c, b, 1)
                pe.wait_ge(s_qks, c + 1)
                pe.sem_inc(tk_p, 1)
                pe.wait_ge(s_kt, c * 2 + 1)
                pe.sem_inc(tk_p, 1)
                for u in range(CH):
                    if u == 4:
                        pe.wait_ge(s_kt, c * 2 + 2)
                        pe.sem_inc(tk_p, 1)
                    products_0(c, b, u)
                    if u + 2 < CH:
                        transposes_0(c, b, u + 2)

            with pe.Fori(0, NCH // 2) as k:
                for b in range(2):
                    chunk_0(2 * k + b, b)
            pe.wait_ge(s_eng0, 18)
            pe.wait_ge(s_ec, 4)
            nc.tensor.transpose(pb[6][0:ICOLS, 0:P], icode[:, :], ident[:, :]).then_inc(s_it, 1)
            chunk_0(NCH - 1, 0)

            def q_transposes(ahead):
                pe.wait_ge(s_qs, ahead)
                nc.tensor.transpose(pb[0][:, 0:P], qs[:, :, :].rearrange("p j s -> p (j s)"), ident[:, :]).then_inc(s_qt, 1)

            def scores(i, done):
                pe.wait_ge(s_mask, done)
                for j in range(G):
                    mm(score_bank[i % 2][:, j * P:(j + 1) * P], mask[:, i % 2, j, :], pen[:, :], start=j == 0, stop=False)
                pe.wait_ge(s_kts, done)
                mm(score_bank[i % 2][:, :], kts[:, :], qT[0:S, :, :].rearrange("s j n -> s (j n)"), start=False, stop=True)\
                    .then_inc(s_sc, 1)

            def prob_transposes(done):
                pe.wait_ge(s_p, done)
                for j in range(G):
                    last = nc.tensor.transpose(pb[2][:, j * P:(j + 1) * P], prob[:, j * P:(j + 1) * P], ident[:, :])
                last.then_inc(s_pt, 1)

            def sums(i, slot, done):
                for j in range(G):
                    last = mm(sums_bank[i % 2][:, 0:W1COLS], probT[:, j * P:(j + 1) * P],
                              xg[:, bass.ds(slot + j, 1), 0:W1COLS].rearrange("p o d -> p (o d)"),
                              start=j == 0, stop=j == G - 1)
                    if j == 0:
                        last.wait_op(s_pts, done, AT_LEAST)
                last.then_inc(s_pv, 1)

            def quad(k):
                cnt = counter(pe, k)
                _, _, slot = item_reader(pe, k)
                for i in range(4):
                    first = isinstance(k, int) and i == 0
                    scores(i + 1, cnt(i + 2))
                    if not first:
                        before, made = slot(i - 1), cnt(i)
                    q_transposes(cnt(i + 3))
                    if not first:
                        sums(i - 1, before, made)
                    prob_transposes(cnt(i + 1))

            pe.wait_ge(s_m0, 1)
            n_quads = quad_count(pe)
            q_transposes(1)
            scores(0, 1)
            q_transposes(2)
            quad(0)
            with pe.Fori(1, n_quads) as k:
                quad(k)
            n_items = kept(pe, n_quads * 4, NG, ITEMS)
            last_slot, all_made = item_reader(pe, last_quad(pe))[2](3), pe.to_reg(n_items)
            sums(3, last_slot, all_made)

            pe.wait_ge(s_acc, n_items + 1)
            pe.sem_inc(tk_p, 1)

            pe.wait_ge(a_wr, 4)
            for h in range(2):
                last = mm(pb[3][:, 0:NE], betas[:, h, :], wr[:, h, :], start=h == 0, stop=h == 1)
            last.then_inc(a_lb, 1)

            def transposes_a(c, b, u):
                pe.wait_ge(a_xn, c * CH + u + 1)
                for h in range(2):
                    last = nc.tensor.transpose(pb[4 + (7 * b + u) % 2][:, h * P:(h + 1) * P],
                                               rows[:, b, u, h * P:(h + 1) * P], ident[:, :])
                last.then_inc(a_tp, 1)

            def logits(c, b, u):
                pe.wait_ge(a_ev, c * CH + u + 1)
                for h in range(2):
                    last = mm(pb[6][:, 64 * b + u * NE:64 * b + (u + 1) * NE], xnT[:, (7 * b + u) % 2, h, :], wrg[:, h, :],
                              start=h == 0, stop=h == 1, skip_group_check=True)
                last.then_inc(a_lg, 1)

            def chunk_a(c, b):
                transposes_a(c, b, 0)
                for u in range(1, CH):
                    transposes_a(c, b, u)
                    logits(c, b, u - 1)
                logits(c, b, CH - 1)
                flat = asg[:, :, :].rearrange("p u e -> p (u e)")
                width = (CH + 1) * NE
                pe.wait_ge(a_as, c + 1)
                mm(pb[7][:, 64 * b:64 * b + width], tri[:, :], flat, start=True, stop=False, skip_group_check=True)
                for d in range(1, CH + 1):
                    last = mm(pb[7][:, 64 * b + d * NE:64 * b + width], ones_b[:, :], flat[:, 0:width - d * NE],
                              start=False, stop=d == CH, skip_group_check=True)
                last.then_inc(a_pos, 1)

            with pe.Fori(0, NCH // 2) as k:
                for b in range(2):
                    chunk_a(2 * k + b, b)
            chunk_a(NCH - 1, 0)

            pe.wait_ge(b_c, 1)

            def x_transposes(loaded, taken=None):
                pe.wait_ge(b_rl, loaded)
                for k in range(2):
                    for h in range(2):
                        if k == 1 and h == 0 and taken is not None:
                            pe.wait_ge(b_ys, taken)
                        last = nc.tensor.transpose(pb[0][:, h * ST + k * P:h * ST + (k + 1) * P],
                                                   xrows[:, k, h * P:(h + 1) * P], ident[:, :])
                last.then_inc(b_xt, 1)

            def expert(e, b, k):
                lo, hi = expert_ends(pe, e)
                pe.wait_ge(b_w[b], 32 * (k + 1))
                pe.sem_inc(tk_p, 1)
                with pe.Fori(lo, hi) as i:
                    copied, taken = pe.to_reg(i * 2 + 2), pe.to_reg(i * 2)
                    loaded = pe.to_reg(i * 16 + 32)
                    hidden = [pe.to_reg(i * 4 + c + 1) for c in range(4)]
                    pe.wait_ge(b_xe, copied)
                    for m in range(4):
                        for c in range(2):
                            last = mm(hidden_bank[m][:, 0:ST],
                                      w1s[:, b, c, m * P:(m + 1) * P], xT[:, c, :], start=c == 0, stop=c == 1,
                                      skip_group_check=True)
                        last.then_inc(b_h, 1)
                    x_transposes(loaded, taken)
                    for c in range(4):
                        pe.wait_ge(b_g, hidden[c])
                        for k2 in range(2):
                            last = mm(pb[3 + k2][:, 0:D], hT[:, c, k2 * P:(k2 + 1) * P], w2s[:, b, c, :],
                                      start=c == 0, stop=c == 3)
                    last.then_inc(b_y, 1)

            x_transposes(16)
            with pe.Fori(0, NE // 2) as k:
                for b in range(2):
                    expert(2 * k + b, b, k)


_INS = ['x', 'src', 'dst', 'L0_gnn_Wq', 'L0_gnn_bq', 'L0_gnn_Wk', 'L0_gnn_bk', 'L0_ffn_gamma', 'L0_ffn_beta',
        'L0_ffn_Wr', 'L0_ffn_br', 'L0_ffn_W1', 'L0_ffn_b1', 'L0_ffn_W2', 'L0_ffn_b2']


def kernel(**inputs):
    import numpy as _np
    import concourse.bacc as _bacc
    from concourse import mybir as _mybir
    from concourse.bass_utils import run_bass_kernel_spmd as _run

    nc = _bacc.Bacc("TRN2", target_bir_lowering=False, num_devices=1)
    arrays, args = {}, []
    for name in _INS:
        a = _np.ascontiguousarray(inputs[name])
        arrays[f"in_{name}_dram"] = a
        args.append(nc.dram_tensor(f"in_{name}_dram", a.shape, _mybir.dt.from_np(a.dtype), kind="ExternalInput").ap())
    args.append(nc.dram_tensor("out_0_dram", (OUT_ROWS, D), _mybir.dt.float32, kind="ExternalOutput").ap())
    build(nc, *args)
    r = _run(nc, [arrays], core_ids=[0])
    return r.results[0]["out_0_dram"][0:N]
```
